# Optimizing a Trainium2 kernel written in Bass

```python
import numpy as np
import jax
import jax.numpy as jnp

def _softmax(x, axis=-1):
    return jax.nn.softmax(x, axis=axis)

def _gelu(x):
    return jax.nn.gelu(x, approximate=True)

def _silu(x):
    return jax.nn.silu(x)

def _sigmoid(x):
    return jax.nn.sigmoid(x)

def _layernorm(x, axis=-1, eps=1e-05):
    m = jnp.mean(x, axis=axis, keepdims=True)
    v = jnp.var(x, axis=axis, keepdims=True)
    return (x - m) / jnp.sqrt(v + eps)

def _scatter_add(tgt, idx, src, axis=0):
    return tgt.at[idx].add(src)

def _segment_sum(src, seg, n):
    return jax.ops.segment_sum(src, seg, n)
kernel_name = 'mk_seq_postln_d1_jaxref_r8_ae1b4d'

def setup_inputs(seed: int=0):
    np.random.seed(seed)
    _w = jnp.asarray

    def _L0_attn_setup():
        import jax, jax.numpy as jnp
        import numpy as np
        D_MODEL = 256
        H = 16
        D_K = D_MODEL // H
        key = jax.random.key(seed)
        ks = jax.random.split(key, 9)
        b, n, d = (2, 256, D_MODEL)
        s = 1.0 / np.sqrt(d)
        return {'x': jax.random.normal(ks[0], (b, n, d), jnp.float32), 'Wq': jax.random.normal(ks[1], (d, d), jnp.float32) * s, 'bq': jax.random.normal(ks[2], (d,), jnp.float32) * 0.01, 'Wk': jax.random.normal(ks[3], (d, d), jnp.float32) * s, 'bk': jax.random.normal(ks[4], (d,), jnp.float32) * 0.01, 'Wv': jax.random.normal(ks[5], (d, d), jnp.float32) * s, 'bv': jax.random.normal(ks[6], (d,), jnp.float32) * 0.01, 'Wo': jax.random.normal(ks[7], (d, d), jnp.float32) * s, 'bo': jax.random.normal(ks[8], (d,), jnp.float32) * 0.01}
    _L0_attn_in = _L0_attn_setup()

    def _L0_ffn_setup():
        import jax, jax.numpy as jnp
        import numpy as np
        B, S, H = (1, 128, 256)
        F = 128
        E = 16
        K = 2
        NS = 1
        ROUTE_SCALE = 1.0
        key = jax.random.key(seed)
        ks = jax.random.split(key, 8)

        def w(k, shape, fan_in):
            return jax.random.normal(k, shape, jnp.float32) * fan_in ** (-0.5)
        return {'hidden_states': jax.random.normal(ks[0], (B, S, H), jnp.float32), 'gate_w': w(ks[1], (H, E), H), 'expert_bias': jnp.zeros((E,), jnp.float32), 'shared_gate_w': w(ks[2], (H, F * NS), H), 'shared_up_w': w(ks[3], (H, F * NS), H), 'shared_down_w': w(ks[4], (F * NS, H), F * NS), 'experts_gate_up': w(ks[5], (E, H, 2 * F), H), 'experts_down': w(ks[6], (E, F, H), F)}
    _L0_ffn_in = _L0_ffn_setup()
    _d = {'L0_attn_x': _L0_attn_in['x'], 'L0_attn_Wq': _L0_attn_in['Wq'], 'L0_attn_bq': _L0_attn_in['bq'], 'L0_attn_Wk': _L0_attn_in['Wk'], 'L0_attn_bk': _L0_attn_in['bk'], 'L0_attn_Wv': _L0_attn_in['Wv'], 'L0_attn_bv': _L0_attn_in['bv'], 'L0_attn_Wo': _L0_attn_in['Wo'], 'L0_attn_bo': _L0_attn_in['bo'], 'L0_ffn_gate_w': _L0_ffn_in['gate_w'], 'L0_ffn_expert_bias': _L0_ffn_in['expert_bias'], 'L0_ffn_shared_gate_w': _L0_ffn_in['shared_gate_w'], 'L0_ffn_shared_up_w': _L0_ffn_in['shared_up_w'], 'L0_ffn_shared_down_w': _L0_ffn_in['shared_down_w'], 'L0_ffn_experts_gate_up': _L0_ffn_in['experts_gate_up'], 'L0_ffn_experts_down': _L0_ffn_in['experts_down']}
    _x0 = _d['L0_attn_x']
    _d['L0_attn_x'] = jax.random.normal(jax.random.fold_in(jax.random.key(seed), 1), (4, 1024, 256), dtype=_x0.dtype)
    del _x0
    return _d

def reference(L0_attn_x, L0_attn_Wq, L0_attn_bq, L0_attn_Wk, L0_attn_bk, L0_attn_Wv, L0_attn_bv, L0_attn_Wo, L0_attn_bo, L0_ffn_gate_w, L0_ffn_expert_bias, L0_ffn_shared_gate_w, L0_ffn_shared_up_w, L0_ffn_shared_down_w, L0_ffn_experts_gate_up, L0_ffn_experts_down):

    def _L0_attn_ref(x, Wq, bq, Wk, bk, Wv, bv, Wo, bo):
        import jax, jax.numpy as jnp
        import numpy as np
        D_MODEL = 256
        H = 16
        D_K = D_MODEL // H
        b, n, d = x.shape
        h, dk = (H, D_K)

        def split_heads(t):
            return t.reshape(b, n, h, dk).transpose(0, 2, 1, 3)
        q = split_heads(x @ Wq + bq)
        k = split_heads(x @ Wk + bk)
        v = split_heads(x @ Wv + bv)
        scores = jnp.einsum('bhqd,bhkd->bhqk', q, k) / jnp.sqrt(jnp.float32(dk))
        causal = jnp.tril(jnp.ones((n, n), dtype=bool))
        scores = jnp.where(causal[None, None], scores, -jnp.inf)
        attn = jax.nn.softmax(scores, axis=-1)
        out = jnp.einsum('bhqk,bhkd->bhqd', attn, v)
        out = out.transpose(0, 2, 1, 3).reshape(b, n, d)
        return out @ Wo + bo

    def _L0_ffn_ref(hidden_states, gate_w, expert_bias, shared_gate_w, shared_up_w, shared_down_w, experts_gate_up, experts_down):
        import jax, jax.numpy as jnp
        import numpy as np
        B, S, H = (1, 128, 256)
        F = 128
        E = 16
        K = 2
        NS = 1
        ROUTE_SCALE = 1.0
        b, s, h = hidden_states.shape
        x = hidden_states.reshape(-1, h)
        T = x.shape[0]
        router_logits = (x @ gate_w).astype(jnp.float32)
        scores = jax.nn.sigmoid(router_logits)
        _, selected = jax.lax.top_k(scores + expert_bias[None, :], K)
        top_scores = jnp.take_along_axis(scores, selected, axis=1)
        top_scores = top_scores / (top_scores.sum(-1, keepdims=True) + 1e-20)
        top_scores = top_scores * ROUTE_SCALE
        shared = jax.nn.silu(x @ shared_gate_w) * (x @ shared_up_w) @ shared_down_w
        comb = jnp.zeros((T, E), jnp.float32).at[jnp.arange(T)[:, None], selected].add(top_scores)
        routed = jnp.zeros_like(x)
        for e in range(E):
            gu = x @ experts_gate_up[e]
            g, u = jnp.split(gu, 2, axis=-1)
            routed = routed + comb[:, e:e + 1] * (jax.nn.silu(g) * u @ experts_down[e])
        return (shared + routed).reshape(b, s, h)
    x = L0_attn_x
    x = _layernorm(x + _L0_attn_ref(x, L0_attn_Wq, L0_attn_bq, L0_attn_Wk, L0_attn_bk, L0_attn_Wv, L0_attn_bv, L0_attn_Wo, L0_attn_bo), axis=-1)
    x = _layernorm(x + _L0_ffn_ref(x, L0_ffn_gate_w, L0_ffn_expert_bias, L0_ffn_shared_gate_w, L0_ffn_shared_up_w, L0_ffn_shared_down_w, L0_ffn_experts_gate_up, L0_ffn_experts_down), axis=-1)
    return x

_drawn_inputs = setup_inputs


def setup_inputs(seed=0):
    import zlib

    import numpy as np

    out = dict(_drawn_inputs(seed))
    spreads = {'L0_ffn_expert_bias': (0.0, 0.1)}
    factors = {'L0_attn_bq': 8.0, 'L0_attn_bk': 8.0}
    for name, (base, spread) in spreads.items():
        noise = np.random.default_rng([zlib.crc32(name.encode()), seed]).standard_normal(out[name].shape)
        drawn = base * np.exp(spread * noise) if base else spread * noise
        out[name] = jnp.asarray(drawn.astype(out[name].dtype))
    for name, factor in factors.items():
        out[name] = (out[name] * factor).astype(out[name].dtype)
    return out
```

```python
from contextlib import ExitStack

import numpy as np
import concourse.bass as bass
from concourse import mybir

F32 = mybir.dt.float32
BF16 = mybir.dt.bfloat16
I32 = mybir.dt.int32
U32 = mybir.dt.uint32
ALU = mybir.AluOpType
ACT = mybir.ActivationFunctionType
AX = mybir.AxisListType

P = 128
B, N, D = 4, 1024, 256
H, DK = 16, 16
DC = D // P
GH = 4
GROUPS = H // GH
GW = GH * DK
STEPS = B * GROUPS
CH = 512
HALVES = N // CH
CT = CH // P
NT = N // P
TILES = B * NT
E, F, TOPK = 16, 128, 2
EPS = 1e-5
NEG = -1e30

PRODUCTS = [(0, 0), (0, 1), (1, 0), (0, 2), (2, 0), (1, 1)]
KS = len(PRODUCTS) * DK
KM = KS + 3

UNITS = [(qc, kt) for qc in range(HALVES) for kt in range(CT * (qc + 1))]
NU = len(UNITS)
DIAG = [u for u, (qc, kt) in enumerate(UNITS) if kt >= CT * qc]
PSLOTS = 3
MAXES = [(qt, h, half) for qt in range(NT) for h in range(GH) for half in range(qt // CT + 1)]
NM = len(MAXES)
MAX_AT = {u: (6 * (u - 1), min(6 * u, NM)) for u in range(1, 9)}

SLOT_BLOCKS = TILES * TOPK + E
PAIRS = SLOT_BLOCKS // 2
ROWS = SLOT_BLOCKS * P


def wait_count(eng, sem, value):
    if isinstance(value, int) and value <= 0:
        return
    eng.wait_ge(sem, value)


def wait_apart(eng, sem, value, waited):
    eng.wait_ge(sem, value)
    eng.sem_inc(waited, 1)


def build(nc, x, xT, Wq, bq, Wk, bk, Wv, bv, Wo, bo, gate_w, expert_bias, sg_w, su_w, sd_w, gu_w, down_w, out):
    with ExitStack() as ctx:
        def sb(name, shape, dt):
            return ctx.enter_context(nc.sbuf_tensor(name, shape, dt))

        def sem(name):
            return ctx.enter_context(nc.semaphore(name))

        def dram(name, shape, dt):
            return nc.dram_tensor(name, shape, dt, kind="Internal").ap()

        qk_parts = dram("qk_parts", (2, 3, B * D, N), BF16)
        y_sorted = dram("y_sorted", (ROWS, D), F32)
        z_sorted = dram("z_sorted", (ROWS, D), F32)

        ps = ctx.enter_context(nc.psum_tensor("ps", [P, 8, CH], F32))

        wqk = sb("wqk", [P, 2, DC, D], F32)
        wv = sb("wv", [P, DC, D], F32)
        wo = sb("wo", [P, DC, D], F32)
        bqk = sb("bqk", [P, 2, DC], F32)
        bv_all = sb("bv_all", [P, D], F32)
        bo_all = sb("bo_all", [P, D], F32)
        gate = sb("gate", [P, DC, E], F32)
        ebias = sb("ebias", [P, E], F32)
        wsg = sb("wsg", [P, DC, F], F32)
        wsu = sb("wsu", [P, DC, F], F32)
        wsd = sb("wsd", [P, D], F32)
        wgu = sb("wgu", [P, E, DC, 2 * F], F32)
        wdn = sb("wdn", [P, E, D], F32)
        ident = sb("ident", [P, P], F32)
        ident_b = sb("ident_b", [P, P], BF16)
        mask_b = sb("mask_b", [P, P], BF16)
        before_b = sb("before_b", [P, P], BF16)
        ones_b = sb("ones_b", [P, P], BF16)
        iota_e = sb("iota_e", [P, E], F32)
        minus_half = sb("minus_half", [P, CT], F32)
        v_all = sb("v_all", [P, STEPS, NT, GW], F32)
        y_all = v_all[:, :, :, :].rearrange("p a b c -> p (a b c)").rearrange("p (t d) -> p t d", d=D)
        a_all = sb("a_all", [P, STEPS, NT, GW], F32)
        sh_all = a_all[:, :, :, :].rearrange("p a b c -> p (a b c)").rearrange("p (t d) -> p t d", d=D)
        stacks = sb("stacks", [P, 2, 2, GH, N], BF16)
        yT_all = stacks[:, :, :, :, :].rearrange("p a b c d -> p (a b c d)").bitcast(F32) \
            .rearrange("p (c t) -> p c t", c=DC)
        work = sb("work", [P, 8192], F32)

        def piece(at, *dims):
            n = int(np.prod(dims))
            v = work[:, at:at + n]
            if len(dims) == 2:
                v = v.rearrange("p (a b) -> p a b", b=dims[1])
            if len(dims) == 3:
                v = v.rearrange("p (a b c) -> p a b c", b=dims[1], c=dims[2])
            return v

        w_loaded = sem("w_loaded")
        const_ready = sem("const_ready")
        const_zeroed = sem("const_zeroed")
        dve_waited = sem("dve_waited")
        pool_waited = sem("pool_waited")

        with ExitStack() as c1:
            xt = [piece(1024 * i, DC, CH) for i in range(2)]
            rest = [piece(2048 + 512 * t, CH) for t in range(4)]
            parts = [piece(4096 + 768 * t, 768).bitcast(BF16).rearrange("p (r t) -> p r t", r=3) for t in range(4)]
            xt_loaded = [sem(f"xt_loaded{i}") for i in range(2)]
            proj_ready = [sem(f"proj_ready{t}") for t in range(4)]
            hi_ready = sem("hi_ready")
            rest_ready = [sem(f"rest_ready{t}") for t in range(4)]
            mid_ready = sem("mid_ready")
            lo_ready = sem("lo_ready")
            stored = [sem(f"stored{t}") for t in range(4)]
            v_ready = [sem(f"v_ready{i}") for i in range(2)]
            v_copied = [sem(f"v_copied{i}") for i in range(2)]
            big_loaded = sem("big_loaded")
            xT_v = xT.rearrange("(c p) t -> p c t", p=P)
            blk = c1.enter_context(nc.Block())

            @blk.sync
            def _(sp):
                def load(b, half):
                    sp.dma_start(xt[half], xT_v[:, :, bass.ds(b * N + half * CH, CH)]).then_inc(xt_loaded[half], 16)

                def store(b, half):
                    for t in range(4):
                        sp.wait_ge(lo_ready, (2 * b + half) * 4 + t + 1)
                        sp.dma_start(
                            qk_parts[t // 2, :, bass.ds(b * D + (t % 2) * P, P), half * CH:(half + 1) * CH]
                            .rearrange("r p t -> p r t"), parts[t]).then_inc(stored[t], 16)

                load(0, 0)
                with sp.Fori(0, B - 1) as b:
                    sp.wait_ge(v_ready[1], 2 * b)
                    load(b, 1)
                    store(b, 0)
                    sp.wait_ge(v_ready[1], 2 * b + 1)
                    load(b + 1, 0)
                    store(b, 1)
                sp.wait_ge(v_ready[1], 2 * (B - 1))
                load(B - 1, 1)
                store(B - 1, 0)
                store(B - 1, 1)
                for t in range(4):
                    sp.wait_ge(stored[t], 16 * 2 * B)

            @blk.gpsimd
            def _(pool):
                pool.memset(ident[:, :], 0.0).then_inc(const_zeroed, 1)
                pool.memset(ident_b[:, :], 0.0).then_inc(const_zeroed, 1)
                pool.memset(mask_b[:, :], 0.0).then_inc(const_zeroed, 1)
                pool.memset(before_b[:, :], 0.0).then_inc(const_zeroed, 1)
                pool.memset(ones_b[:, :], 1.0).then_inc(const_zeroed, 1)
                pool.memset(minus_half[:, :], -0.5).then_inc(const_zeroed, 1)
                pool.wait_ge(const_zeroed, 6)
                pool.affine_select(out=ident[:, :], in_=ident[:, :], compare_op=ALU.not_equal, fill=1.0, base=0,
                                   pattern=[[-1, P]], channel_multiplier=1).then_inc(const_ready, 1)
                pool.affine_select(out=ident_b[:, :], in_=ident_b[:, :], compare_op=ALU.not_equal, fill=1.0, base=0,
                                   pattern=[[-1, P]], channel_multiplier=1).then_inc(const_ready, 1)
                pool.affine_select(out=mask_b[:, :], in_=mask_b[:, :], compare_op=ALU.is_ge, fill=NEG, base=0,
                                   pattern=[[-1, P]], channel_multiplier=1).then_inc(const_ready, 1)
                pool.affine_select(out=before_b[:, :], in_=before_b[:, :], compare_op=ALU.is_ge, fill=1.0, base=0,
                                   pattern=[[-1, P]], channel_multiplier=1).then_inc(const_ready, 1)
                pool.iota(iota_e[:, :], [[1, E]], base=0, channel_multiplier=0,
                          allow_small_or_imprecise_dtypes=True).then_inc(const_ready, 1)
                with pool.Fori(0, B) as b:
                    for half in range(2):
                        for t in range(4):
                            pool.wait_ge(mid_ready, (2 * b + half) * 4 + t + 1)
                            pool.tensor_tensor(parts[t][:, 2, :], rest[t], parts[t][:, 1, :],
                                               ALU.subtract).then_inc(lo_ready, 1)

            @blk.scalar
            def _(act):
                for i, w in enumerate((Wq, Wk)):
                    act.dma_start(wqk[:, i], w.rearrange("(c p) n -> p c n", p=P)).then_inc(w_loaded, 16)
                act.dma_start(wv[:, :, :], Wv.rearrange("(c p) n -> p c n", p=P)).then_inc(w_loaded, 16)
                for i, w in enumerate((bq, bk)):
                    act.dma_start(bqk[:, i], w).then_inc(w_loaded, 16)
                act.dma_start(bv_all[:, :], bv.partition_broadcast(P)).then_inc(w_loaded, 16)
                act.dma_start(bo_all[:, :], bo.partition_broadcast(P)).then_inc(big_loaded, 16)
                act.dma_start(ebias[:, :], expert_bias.partition_broadcast(P)).then_inc(big_loaded, 16)
                act.dma_start(wo[:, :, :], Wo.rearrange("(c p) n -> p c n", p=P)).then_inc(big_loaded, 16)
                act.dma_start(gate[:, :, :], gate_w.rearrange("(c p) n -> p c n", p=P)).then_inc(big_loaded, 16)
                act.dma_start(wsg[:, :, :], sg_w.rearrange("(c p) n -> p c n", p=P)).then_inc(big_loaded, 16)
                act.dma_start(wsu[:, :, :], su_w.rearrange("(c p) n -> p c n", p=P)).then_inc(big_loaded, 16)
                act.dma_start(wsd[:, :], sd_w).then_inc(big_loaded, 16)
                act.dma_start(wgu[:, :, :, :].rearrange("p e c n -> p (e c) n"),
                              gu_w.rearrange("e (c p) n -> p (e c) n", p=P)).then_inc(big_loaded, 16)
                act.dma_start(wdn[:, :, :], down_w.rearrange("e p n -> p e n")).then_inc(big_loaded, 16)
                act.wait_ge(w_loaded, 16 * 6)

                def high(b, half, t):
                    act.wait_ge(proj_ready[t], 2 * b + half + 1)
                    act.wait_ge(stored[t], 16 * (2 * b + half))
                    act.activation(parts[t][:, 0, :], ps[:, t, :], ACT.Identity,
                                   bias=bqk[:, t // 2, t % 2:t % 2 + 1]).then_inc(hi_ready, 1)

                def middle(b, half, t):
                    act.wait_ge(rest_ready[t], 2 * b + half + 1)
                    act.activation(parts[t][:, 1, :], rest[t], ACT.Copy).then_inc(mid_ready, 1)

                with act.Fori(0, B) as b:
                    for half in range(2):
                        high(b, half, 0)
                        for t in range(1, 4):
                            high(b, half, t)
                            middle(b, half, t - 1)
                        middle(b, half, 3)
                act.wait_ge(big_loaded, 16 * 9)

            @blk.vector
            def _(dve):
                dve.wait_ge(w_loaded, 16 * 6)
                with dve.Fori(0, B) as b:
                    for half in range(2):
                        for t in range(4):
                            dve.wait_ge(hi_ready, (2 * b + half) * 4 + t + 1)
                            dve.scalar_tensor_tensor(rest[t], ps[:, t, :], bqk[:, t // 2, t % 2:t % 2 + 1],
                                                     parts[t][:, 0, :], ALU.add,
                                                     ALU.subtract).then_inc(rest_ready[t], 1)
                        for i in range(2):
                            dve.wait_ge(v_ready[i], 2 * b + half + 1)
                            for j in range(2):
                                tile = half * CT + 2 * i + j
                                ins = dve.tensor_tensor(
                                    v_all[:, bass.ds(b * GROUPS, GROUPS), tile, :],
                                    ps[:, 4 + i, j * D:(j + 1) * D].rearrange("p (g e) -> p g e", g=GROUPS),
                                    bv_all[:, :].rearrange("p (g e) -> p g e", g=GROUPS), ALU.add)
                            ins.then_inc(v_copied[i], 1)

            @blk.tensor
            def _(pe):
                pe.wait_ge(w_loaded, 16 * 6)
                with pe.Fori(0, B) as b:
                    for half in range(2):
                        pe.wait_ge(xt_loaded[half], 16 * b + 16)
                        for t in range(4):
                            pe.wait_ge(rest_ready[t], 2 * b + half)
                            for c in range(DC):
                                mm = pe.matmul(ps[:, t, :], wqk[:, t // 2, c, (t % 2) * P:(t % 2 + 1) * P],
                                               xt[half][:, c, :], start=(c == 0), stop=(c == DC - 1))
                            mm.then_inc(proj_ready[t], 1)
                        for i in range(2):
                            pe.wait_ge(v_copied[i], 2 * b + half)
                            for j in range(2):
                                tt = 2 * i + j
                                for c in range(DC):
                                    mm = pe.matmul(ps[:, 4 + i, j * D:(j + 1) * D],
                                                   xt[half][:, c, tt * P:(tt + 1) * P], wv[:, c, :],
                                                   start=(c == 0), stop=(c == DC - 1))
                            mm.then_inc(v_ready[i], 1)

        with ExitStack() as c2:
            probs = piece(0, PSLOTS * GH, CH)
            vg = [c2.enter_context(nc.sbuf_tensor(f"vg{r}", [P, NT, GH, 32], F32)) for r in range(2)]
            oT = [c2.enter_context(nc.sbuf_tensor(f"oT{r}", [P, CH], F32)) for r in range(2)]
            mT = [c2.enter_context(nc.sbuf_tensor(f"mT{r}", [3 * GH, N], BF16)) for r in range(2)]
            recip = c2.enter_context(nc.sbuf_tensor("recip", [P, CT, GH], F32))
            m_lo_half = c2.enter_context(nc.sbuf_tensor("m_lo_half", [P, NT, GH], F32))
            m_hi_half = c2.enter_context(nc.sbuf_tensor("m_hi_half", [P, CT, GH], F32))
            m_neg = c2.enter_context(nc.sbuf_tensor("m_neg", [P, NT, GH], F32))
            m_rest = c2.enter_context(nc.sbuf_tensor("m_rest", [P, 2, NT, GH], F32))
            m_parts = c2.enter_context(nc.sbuf_tensor("m_parts", [P, NT, 3, GH], BF16))
            zero = piece(PSLOTS * GH * CH, 1024)
            qs = [stacks[:, r, 0] for r in range(2)]
            ks = [stacks[:, r, 1] for r in range(2)]
            SCORE_BANK, MAX_BANK, OUT_BANK, MISC_BANK = 0, 4, 6, 7
            misc_b = ps[:, MISC_BANK, :].bitcast(BF16)

            ones_ready = sem("ones_ready")
            zero_ready = sem("zero_ready")
            zero_stored = sem("zero_stored")
            stack_loaded = [sem(f"stack_loaded{r}") for r in range(2)]
            m_loaded = [sem(f"m_loaded{r}") for r in range(2)]
            score_max_ready = sem("score_max_ready")
            reduced = sem("reduced")
            m_step = sem("m_step")
            m_ready = sem("m_ready")
            mT_ready = sem("mT_ready")
            mT_copied = sem("mT_copied")
            score_ready = sem("score_ready")
            exp_done = sem("exp_done")
            masked = sem("masked")
            pv_done = sem("pv_done")
            o_copied = sem("o_copied")
            oT_ready = sem("oT_ready")
            recip_ready = sem("recip_ready")
            a_written = sem("a_written")
            vg_ready = sem("vg_ready")
            blk = c2.enter_context(nc.Block())

            @blk.sync
            def _(sp):
                def load_stacks(i, r):
                    for n, (qp, kp) in enumerate(PRODUCTS):
                        for s, (dst, part) in enumerate(((qs, qp), (ks, kp))):
                            sp.dma_start(dst[r][n * DK:(n + 1) * DK],
                                         qk_parts[s, part, bass.ds(i * GW, GW), :]
                                         .rearrange("(h d) t -> d h t", d=DK)).then_inc(stack_loaded[r], 16)

                def load_max(i, r):
                    sp.wait_ge(mT_copied, i + 1)
                    for part in range(3):
                        sp.dma_start(qs[r][KS + part:KS + part + 1], mT[r][part * GH:(part + 1) * GH, :])\
                            .then_inc(m_loaded[r], 16)

                load_stacks(0, 0)
                load_stacks(1, 1)
                sp.wait_ge(zero_ready, 1)
                for n in range(ROWS * D // (P * 4096)):
                    sp.dma_start(y_sorted[n * 16 * P:(n + 1) * 16 * P, :].rearrange("(p a) d -> p (a d)", p=P)
                                 .rearrange("p (a d) -> p a d", a=4),
                                 zero.unsqueeze(1).broadcast_to((P, 4, 1024))).then_inc(zero_stored, 16)
                load_max(0, 0)
                with sp.Fori(0, (STEPS - 2) // 2) as j:
                    for r in range(2):
                        load_max(2 * j + r + 1, 1 - r)
                        sp.wait_ge(pv_done, NU * (2 * j + r + 1))
                        load_stacks(2 * j + r + 2, r)
                load_max(STEPS - 1, 1)
                sp.wait_ge(zero_stored, 16 * (ROWS * D // (P * 4096)))

            @blk.gpsimd
            def _(pool):
                for r in range(2):
                    pool.memset(vg[r][:, :, :, DK:32], 1.0).then_inc(ones_ready, 1)
                pool.memset(zero, 0.0).then_inc(zero_ready, 1)
                pool.wait_ge(ones_ready, 4)

                def values(i, r):
                    pool.tensor_copy(vg[r][:, :, :, 0:DK],
                                     v_all[:, bass.ds(i, 1)].rearrange("p a t (h e) -> p (a t) h e", e=DK))\
                        .then_inc(vg_ready, 1)

                def mask(i, u):
                    off = P * (UNITS[u][1] - CT * UNITS[u][0])
                    s = (u % PSLOTS) * GH
                    wait_apart(pool, exp_done, 2 * (NU * i + u) + 2, pool_waited)
                    blk_ = probs[:, s:s + GH, off:off + P]
                    pool.affine_select(out=blk_, in_=blk_, compare_op=ALU.is_ge, fill=0.0, base=0,
                                       pattern=[[0, GH], [1, P]], channel_multiplier=-1).then_inc(masked, 1)

                def step(i, r, more=True):
                    for u in DIAG[:CT]:
                        mask(i, u)
                    if more:
                        wait_count(pool, pv_done, NU * i)
                        values(i + 1, 1 - r)
                    for u in DIAG[CT:]:
                        mask(i, u)

                values(0, 0)
                step(0, 0)
                with pool.Fori(0, (STEPS - 2) // 2) as j:
                    step(2 * j + 1, 1)
                    step(2 * j + 2, 0)
                step(STEPS - 1, 1, more=False)

            @blk.scalar
            def _(act):
                def exp(i, u):
                    qc, kt = UNITS[u]
                    off = max(0, P * (kt - CT * qc))
                    s = (u % PSLOTS) * GH
                    wait_count(act, pv_done, NU * i + u - PSLOTS + 1)
                    for pair in range(2):
                        act.wait_ge(score_ready, 2 * (NU * i + u) + pair + 1)
                        act.activation(probs[:, s + 2 * pair:s + 2 * pair + 2, off:CH],
                                       ps[:, SCORE_BANK + 2 * pair:SCORE_BANK + 2 * pair + 2, off:CH],
                                       ACT.Exp, scale=float(DK) ** -0.5).then_inc(exp_done, 1)

                def copy_out(i, qc):
                    act.wait_ge(pv_done, NU * i + (CT if qc == 0 else NU))
                    wait_count(act, oT_ready, 2 * i + qc - 1)
                    act.activation(oT[qc][:, :], ps[:, OUT_BANK, :], ACT.Copy).then_inc(o_copied, 1)

                def copy_max(i, k2, r):
                    act.wait_ge(mT_ready, i + 1)
                    wait_count(act, m_loaded[r], 48 * k2)
                    act.activation(mT[r][:, :], misc_b[0:3 * GH, :], ACT.Copy).then_inc(mT_copied, 1)

                def step(i, k2, r, prev=True, more=True):
                    for u in range(NU):
                        exp(i, u)
                        if u == 0 and prev:
                            copy_out(i - 1, 1)
                        if u == CT:
                            copy_out(i, 0)
                        if u == NU - 2 and more:
                            copy_max(i + 1, k2 + r, 1 - r)

                copy_max(0, 0, 0)
                step(0, 0, 0, prev=False)
                with act.Fori(0, (STEPS - 2) // 2) as j:
                    step(2 * j + 1, j, 1)
                    step(2 * j + 2, j + 1, 0)
                step(STEPS - 1, STEPS // 2 - 1, 1, more=False)
                copy_out(STEPS - 1, 1)

            @blk.vector
            def _(dve):
                def maxima(i, lo, hi):
                    for n in range(lo, hi):
                        qt, h, half = MAXES[n]
                        w = min(CH, (qt + 1) * P - half * CH)
                        dst = m_lo_half[:, qt, h:h + 1] if half == 0 else m_hi_half[:, qt - CT, h:h + 1]
                        dve.wait_ge(score_max_ready, NM * i + n + 1)
                        dve.tensor_reduce(dst, ps[:, MAX_BANK + n % 2, 0:w], AX.X, ALU.max).then_inc(reduced, 1)

                def max_parts(i):
                    dve.wait_ge(reduced, NM * (i + 1))
                    dve.tensor_tensor(m_lo_half[:, CT:NT, :], m_lo_half[:, CT:NT, :], m_hi_half[:, :, :],
                                      ALU.max).then_inc(m_step, 1)
                    dve.wait_ge(m_step, 6 * i + 1)
                    dve.tensor_scalar(m_neg[:, :, :], m_lo_half[:, :, :], -1.0, None, ALU.mult).then_inc(m_step, 1)
                    dve.wait_ge(m_step, 6 * i + 2)
                    wait_count(dve, mT_ready, i)
                    dve.tensor_copy(m_parts[:, :, 0, :], m_neg[:, :, :]).then_inc(m_step, 1)
                    dve.wait_ge(m_step, 6 * i + 3)
                    dve.tensor_tensor(m_rest[:, 0], m_neg[:, :, :], m_parts[:, :, 0, :], ALU.subtract)\
                        .then_inc(m_step, 1)
                    dve.wait_ge(m_step, 6 * i + 4)
                    dve.tensor_copy(m_parts[:, :, 1, :], m_rest[:, 0]).then_inc(m_step, 1)
                    dve.wait_ge(m_step, 6 * i + 5)
                    dve.tensor_tensor(m_rest[:, 1], m_rest[:, 0], m_parts[:, :, 1, :], ALU.subtract)\
                        .then_inc(m_step, 1)
                    dve.wait_ge(m_step, 6 * i + 6)
                    dve.tensor_copy(m_parts[:, :, 2, :], m_rest[:, 1]).then_inc(m_ready, 1)

                def normalise(i, qc):
                    o = ps[:, MISC_BANK, :].rearrange("p (t h e) -> p t h e", t=CT, e=32)
                    dve.wait_ge(oT_ready, 2 * i + qc + 1)
                    wait_count(dve, a_written, 2 * i + qc)
                    dve.reciprocal(recip[:, :, :], o[:, :, :, DK]).then_inc(recip_ready, 1)
                    dve.wait_ge(recip_ready, 2 * i + qc + 1)
                    dve.tensor_tensor(a_all[:, bass.ds(i, 1), qc * CT:(qc + 1) * CT, :]
                                      .rearrange("p a t (h e) -> p (a t) h e", e=DK), o[:, :, :, 0:DK],
                                      recip[:, :, :].unsqueeze(3).broadcast_to((P, CT, GH, DK)), ALU.mult)\
                        .then_inc(a_written, 1)

                def step(i, prev=True, more=True):
                    for u in range(NU):
                        if more and u in MAX_AT:
                            maxima(i + 1, *MAX_AT[u])
                        if u == 1 and prev:
                            normalise(i - 1, 1)
                        if u == 5:
                            normalise(i, 0)
                        if u == 9 and more:
                            max_parts(i + 1)

                for r in range(2):
                    dve.memset(stacks[KS:KM, r, 1], 1.0).then_inc(ones_ready, 1)
                maxima(0, 0, NM)
                max_parts(0)
                step(0, prev=False)
                with dve.Fori(0, (STEPS - 2) // 2) as j:
                    step(2 * j + 1)
                    step(2 * j + 2)
                step(STEPS - 1, more=False)
                normalise(STEPS - 1, 1)

            @blk.tensor
            def _(pe):
                pe.wait_ge(ones_ready, 4)

                def scores(i, r, u):
                    qc, kt = UNITS[u]
                    off = max(0, P * (kt - CT * qc))
                    for pair in range(2):
                        wait_count(pe, exp_done, 2 * (NU * i + u) + pair - 1)
                        for h in (2 * pair, 2 * pair + 1):
                            mm = pe.matmul(ps[:, SCORE_BANK + h, off:CH], ks[r][0:KM, h, kt * P:(kt + 1) * P],
                                           qs[r][0:KM, h, qc * CH + off:(qc + 1) * CH], start=True, stop=True)
                        mm.then_inc(score_ready, 1)

                def weigh(i, r, u):
                    qc, kt = UNITS[u]
                    off = max(0, P * (kt - CT * qc))
                    s = (u % PSLOTS) * GH
                    if u in DIAG:
                        pe.wait_ge(masked, len(DIAG) * i + DIAG.index(u) + 1)
                    else:
                        pe.wait_ge(exp_done, 2 * (NU * i + u) + 2)
                    if kt == 0:
                        wait_count(pe, o_copied, 2 * i + qc)
                    for h in range(GH):
                        mm = pe.matmul(ps[32 * h:32 * h + 32, OUT_BANK, off:CH], vg[r][:, kt, h, :],
                                       probs[:, s + h, off:CH], start=(kt == 0), stop=(kt == CT * (qc + 1) - 1))
                    mm.then_inc(pv_done, 1)

                def maxima(i, r, lo, hi):
                    for n in range(lo, hi):
                        qt, h, half = MAXES[n]
                        w = min(CH, (qt + 1) * P - half * CH)
                        dst = ps[:, MAX_BANK + n % 2, 0:w]
                        wait_count(pe, reduced, NM * i + n - 1)
                        diag = half == qt // CT
                        mm = pe.matmul(dst, qs[r][0:KS, h, qt * P:(qt + 1) * P],
                                       ks[r][0:KS, h, half * CH:half * CH + w], start=True, stop=not diag)
                        if diag:
                            mm = pe.matmul(dst[:, w - P:w], ident_b[:, :], mask_b[:, :], start=False, stop=True)
                        mm.then_inc(score_max_ready, 1)

                def turn_max(i):
                    pe.wait_ge(m_ready, i + 1)
                    wait_count(pe, a_written, 2 * i - 1)
                    for qt in range(NT):
                        mm = pe.transpose(misc_b[0:3 * GH, qt * P:(qt + 1) * P],
                                          m_parts[:, qt].rearrange("p r h -> p (r h)"), ident_b[:, :])
                    mm.then_inc(mT_ready, 1)

                def turn_out(i, qc):
                    pe.wait_ge(o_copied, 2 * i + qc + 1)
                    if qc == 1:
                        pe.wait_ge(mT_copied, i + 2 if not isinstance(i, int) else min(i + 2, STEPS))
                    wait_count(pe, a_written, 2 * i + qc)
                    for t in range(CT):
                        mm = pe.transpose(ps[:, MISC_BANK, t * P:(t + 1) * P], oT[qc][:, t * P:(t + 1) * P],
                                          ident[:, :])
                    mm.then_inc(oT_ready, 1)

                def step(i, k2, r, prev=True, more=True):
                    pe.wait_ge(m_loaded[r], 48 * k2 + 48)
                    pe.wait_ge(vg_ready, i + 1)
                    scores(i, r, 0)
                    if prev:
                        weigh(i - 1, 1 - r, NU - 1)
                    for u in range(NU):
                        if u + 1 < NU:
                            scores(i, r, u + 1)
                        if more and u in MAX_AT:
                            if MAX_AT[u][0] == 0:
                                pe.wait_ge(stack_loaded[1 - r], 192 * (k2 + r) + 192)
                            maxima(i + 1, 1 - r, *MAX_AT[u])
                        if u + 1 < NU:
                            weigh(i, r, u)
                        if u == 1 and prev:
                            turn_out(i - 1, 1)
                        if u == 5:
                            turn_out(i, 0)
                        if u == 9 and more:
                            turn_max(i + 1)

                pe.wait_ge(stack_loaded[0], 192)
                maxima(0, 0, 0, NM)
                turn_max(0)
                step(0, 0, 0, prev=False)
                with pe.Fori(0, (STEPS - 2) // 2) as j:
                    step(2 * j + 1, j, 1)
                    step(2 * j + 2, j + 1, 0)
                step(STEPS - 1, STEPS // 2 - 1, 1, more=False)
                weigh(STEPS - 1, 1, NU - 1)
                turn_out(STEPS - 1, 1)

        scores_all = sb("scores_all", [P, TILES, E], F32)
        chosen = sb("chosen", [P, TOPK, TILES], F32)
        weight = sb("weight", [P, TOPK, TILES], F32)
        row_of = sb("row_of", [P, TOPK, TILES], U32)
        block_expert = sb("block_expert", [P, SLOT_BLOCKS], U32)

        with ExitStack() as c3:
            attn = [piece(1024 * r, CT, D) for r in range(2)]
            attnT = [piece(2048 + 1024 * r, DC, CH) for r in range(2)]
            xr = [piece(4096 + 1024 * r, CT, D) for r in range(2)]
            res = [piece(6144 + 1024 * r, CT, D) for r in range(2)]
            yT = [c3.enter_context(nc.sbuf_tensor(f"yT{r}", [P, DC, CH], F32)) for r in range(2)]
            stats = c3.enter_context(nc.sbuf_tensor("stats", [P, CT, 6], F32))
            moments = c3.enter_context(nc.sbuf_tensor("moments", [P, CT, 2], F32))
            rstd = c3.enter_context(nc.sbuf_tensor("rstd", [P, CT], F32))
            enl = c3.enter_context(nc.sbuf_tensor("enl", [P, CT, E], F32))
            biased = c3.enter_context(nc.sbuf_tensor("biased", [P, CT, E], F32))
            top = c3.enter_context(nc.sbuf_tensor("top", [P, CT, 8], F32))
            top_at = c3.enter_context(nc.sbuf_tensor("top_at", [P, CT, 8], U32))
            x_loaded = [sem(f"x_loaded{r}") for r in range(2)]
            xb_ready = sem("xb_ready")
            attn_ready = sem("attn_ready")
            aT_ready = sem("aT_ready")
            aT_copied = sem("aT_copied")
            wo_ready = sem("wo_ready")
            res_ready = sem("res_ready")
            stats_ready = sem("stats_ready")
            moments_ready = sem("moments_ready")
            rstd_step = sem("rstd_step")
            rstd_ready = sem("rstd_ready")
            y_ready = sem("y_ready")
            y_saved = sem("y_saved")
            yT_saved = sem("yT_saved")
            yT_ready = sem("yT_ready")
            yT_copied = sem("yT_copied")
            logit_ready = sem("logit_ready")
            enl_ready = sem("enl_ready")
            route_step = sem("route_step")
            x_v = x.rearrange("b (t p) d -> p (b t) d", p=P)
            RS = 4 + 2 * CT
            blk = c3.enter_context(nc.Block())

            def two_stages(eng, front, back):
                front(0, 0, 0)
                with eng.Fori(0, B - 1) as b:
                    front(2 * b + 1, b, 1)
                    back(2 * b, b, 0)
                    front(2 * b + 2, b + 1, 0)
                    back(2 * b + 1, b, 1)
                front(2 * B - 1, B - 1, 1)
                back(2 * B - 2, B - 1, 0)
                back(2 * B - 1, B - 1, 1)

            @blk.sync
            def _(sp):
                with sp.Fori(0, B) as b:
                    for r in range(2):
                        sp.wait_ge(res_ready, 2 * b)
                        sp.dma_start(xr[r], x_v[:, bass.ds(b * NT + r * CT, CT), :]).then_inc(x_loaded[r], 16)

            @blk.gpsimd
            def _(pool):
                def front(c, b, r):
                    pool.wait_ge(aT_ready, 2 * b)
                    pool.tensor_copy(attn[r].rearrange("p t (g e) -> p t g e", g=GROUPS),
                                     a_all[:, bass.ds(b * GROUPS, GROUPS), r * CT:(r + 1) * CT, :]
                                     .rearrange("p g t e -> p t g e")).then_inc(attn_ready, 1)
                    pool.wait_ge(x_loaded[r], 16 * b + 16)
                    pool.tensor_tensor(xr[r], xr[r], bo_all[:, :].unsqueeze(1).broadcast_to((P, CT, D)),
                                       ALU.add).then_inc(xb_ready, 1)
                    wait_apart(pool, moments_ready, CT * c + CT, pool_waited)
                    pool.tensor_scalar(rstd[:, :], moments[:, :, 1], EPS, None, ALU.add).then_inc(rstd_step, 1)
                    pool.wait_ge(rstd_step, c + 1)
                    pool.tensor_tensor(rstd[:, :], rstd[:, :], minus_half[:, :], ALU.pow).then_inc(rstd_ready, 1)

                def back(c, b, r):
                    pool.wait_ge(y_ready, c + 1)
                    pool.tensor_copy(y_all[:, bass.ds(c * CT, CT), :], res[r]).then_inc(y_saved, 1)
                    pool.wait_ge(yT_copied, c + 1)
                    pool.tensor_copy(yT_all[:, :, bass.ds(c * CH, CH)], yT[r][:, :, :]).then_inc(yT_saved, 1)

                two_stages(pool, front, back)

            @blk.scalar
            def _(act):
                def front(c, b, r):
                    act.wait_ge(aT_ready, c + 1)
                    wait_count(act, wo_ready, 2 * c - 2)
                    act.activation(attnT[r], ps[:, 0:2, :], ACT.Copy).then_inc(aT_copied, 1)

                def back(c, b, r):
                    act.wait_ge(yT_ready, c + 1)
                    act.wait_ge(yT_saved, c)
                    act.activation(yT[r][:, :, :], ps[:, 4:6, :], ACT.Copy).then_inc(yT_copied, 1)
                    act.wait_ge(logit_ready, c + 1)
                    act.wait_ge(route_step, RS * c)
                    act.activation(enl[:, :, :], ps[:, 6, 0:CT * E].rearrange("p (t e) -> p t e", e=E), ACT.Exp,
                                   scale=-1.0).then_inc(enl_ready, 1)

                two_stages(act, front, back)

            @blk.vector
            def _(dve):
                def norm(c, b, r):
                    wait_count(dve, yT_ready, c - 1)
                    wait_count(dve, y_saved, c - 1)
                    dve.wait_ge(xb_ready, c + 1)
                    for i in range(2):
                        dve.wait_ge(wo_ready, 2 * c + i + 1)
                        ins = dve.tensor_tensor(res[r][:, 2 * i:2 * i + 2, :],
                                                ps[:, 2 + i, :].rearrange("p (t d) -> p t d", d=D),
                                                xr[r][:, 2 * i:2 * i + 2, :], ALU.add)
                    ins.then_inc(res_ready, 1)
                    dve.wait_ge(res_ready, c + 1)
                    for t in range(CT):
                        dve.bn_stats(stats[:, t, :], res[r][:, t, :]).then_inc(stats_ready, 1)
                    wait_apart(dve, stats_ready, CT * c + CT, dve_waited)
                    for t in range(CT):
                        dve.bn_aggr(moments[:, t, :], stats[:, t, :]).then_inc(moments_ready, 1)
                    dve.wait_ge(rstd_ready, c + 1)
                    for t in range(CT):
                        ins = dve.tensor_scalar(res[r][:, t, :], res[r][:, t, :],
                                                moments[:, t, 0:1], rstd[:, t:t + 1], ALU.subtract, ALU.mult)
                    ins.then_inc(y_ready, 1)

                def route(c, b, r):
                    tiles = bass.ds(c * CT, CT)
                    dve.wait_ge(enl_ready, c + 1)
                    dve.tensor_scalar(biased[:, :, :], enl[:, :, :], 1.0, None, ALU.add).then_inc(route_step, 1)
                    dve.wait_ge(route_step, RS * c + 1)
                    dve.reciprocal(scores_all[:, tiles, :], biased[:, :, :]).then_inc(route_step, 1)
                    dve.wait_ge(route_step, RS * c + 2)
                    dve.tensor_tensor(biased[:, :, :], scores_all[:, tiles, :],
                                      ebias[:, :].unsqueeze(1).broadcast_to((P, CT, E)), ALU.add)\
                        .then_inc(route_step, 1)
                    wait_apart(dve, route_step, RS * c + 3, dve_waited)
                    for t in range(CT):
                        dve.max(top[:, t, :], biased[:, t, :]).then_inc(route_step, 1)
                    wait_apart(dve, route_step, RS * c + 3 + CT, dve_waited)
                    for t in range(CT):
                        dve.max_index(top_at[:, t, :], top[:, t, :], biased[:, t, :]).then_inc(route_step, 1)
                    dve.wait_ge(route_step, RS * c + 3 + 2 * CT)
                    dve.tensor_copy(chosen[:, :, tiles].rearrange("p j t -> p t j"), top_at[:, :, 0:TOPK])\
                        .then_inc(route_step, 1)

                two_stages(dve, norm, route)

            @blk.tensor
            def _(pe):
                def project(c, b, r):
                    pe.wait_ge(attn_ready, c + 1)
                    pe.wait_ge(aT_copied, c)
                    for h in range(DC):
                        for t in range(CT):
                            mm = pe.transpose(ps[:, h, t * P:(t + 1) * P], attn[r][:, t, h * P:(h + 1) * P],
                                              ident[:, :])
                    mm.then_inc(aT_ready, 1)
                    pe.wait_ge(aT_copied, c + 1)
                    pe.wait_ge(res_ready, c)
                    for i in range(2):
                        for t in (2 * i, 2 * i + 1):
                            for h in range(DC):
                                mm = pe.matmul(ps[:, 2 + i, (t % 2) * D:(t % 2 + 1) * D],
                                               attnT[r][:, h, t * P:(t + 1) * P], wo[:, h, :],
                                               start=(h == 0), stop=(h == DC - 1))
                        mm.then_inc(wo_ready, 1)

                def back(c, b, r):
                    pe.wait_ge(y_ready, c + 1)
                    pe.wait_ge(yT_copied, c)
                    for h in range(DC):
                        for t in range(CT):
                            mm = pe.transpose(ps[:, 4 + h, t * P:(t + 1) * P], res[r][:, t, h * P:(h + 1) * P],
                                              ident[:, :])
                    mm.then_inc(yT_ready, 1)
                    pe.wait_ge(yT_copied, c + 1)
                    pe.wait_ge(enl_ready, c)
                    for t in range(CT):
                        for h in range(DC):
                            mm = pe.matmul(ps[:, 6, t * E:(t + 1) * E], yT[r][:, h, t * P:(t + 1) * P], gate[:, h, :],
                                           start=(h == 0), stop=(h == DC - 1))
                    mm.then_inc(logit_ready, 1)

                two_stages(pe, project, back)

        with ExitStack() as c4:
            gact = [piece(512 * r, CH) for r in range(2)]
            hid = [piece(1024 + 512 * r, CH) for r in range(2)]
            pick = [piece(2048 + 512 * j, TILES, E) for j in range(TOPK)]
            prod = [piece(3072 + 512 * j, TILES, E) for j in range(TOPK)]
            run = [piece(4096 + 512 * j, TILES, E) for j in range(2)]
            base = piece(5120, TILES, E)
            over = piece(5632, SLOT_BLOCKS, E)
            iota_blk = piece(6912, SLOT_BLOCKS)
            before_blk = piece(6992, SLOT_BLOCKS)
            cnt = [piece(7080 + 16 * j, E) for j in range(8)]
            cnt_i = [piece(7300 + 16 * j, E).bitcast(I32) for j in range(2)]
            row_f = piece(7400, TOPK, TILES)
            top_s = piece(7464, TOPK, TILES)
            sum_s = piece(7528, TILES)
            pick_b = c4.enter_context(nc.sbuf_tensor("pick_b", [P, TILES, E], BF16))
            iota_ready = sem("iota_ready")
            picked = sem("picked")
            counted = sem("counted")
            chain = sem("chain")
            rows_ready = sem("rows_ready")
            scattered = sem("scattered")
            gate_ready = sem("gate_ready")
            up_ready = sem("up_ready")
            gact_ready = sem("gact_ready")
            hid_ready = sem("hid_ready")
            down_ready = sem("down_ready")
            shared_done = sem("shared_done")
            blk = c4.enter_context(nc.Block())

            @blk.gpsimd
            def _(pool):
                pool.iota(iota_blk, [[1, SLOT_BLOCKS]], base=0, channel_multiplier=0,
                          allow_small_or_imprecise_dtypes=True).then_inc(iota_ready, 1)
                pool.wait_ge(rows_ready, 1)
                for t in range(TILES):
                    for j in range(TOPK):
                        pool.indirect_dma_start(
                            out=y_sorted, out_offset=bass.IndirectOffsetOnAxis(ap=row_of[:, j, t:t + 1], axis=0),
                            in_=y_all[:, t, :], in_offset=None).then_inc(scattered, 16)
                pool.wait_ge(scattered, 16 * TOPK * TILES)

            @blk.scalar
            def _(act):
                with act.Fori(0, B) as b:
                    for r in range(2):
                        act.wait_ge(gate_ready, 2 * b + r + 1)
                        act.wait_ge(hid_ready, 2 * b + r)
                        act.activation(gact[r], ps[:, 2 + 2 * r, :], ACT.Silu).then_inc(gact_ready, 1)

            @blk.vector
            def _(dve):
                n = [0]

                def link(ins):
                    n[0] += 1
                    ins.then_inc(chain, 1)
                    dve.wait_ge(chain, n[0])

                ie = iota_e[:, :].unsqueeze(1).broadcast_to((P, TILES, E))
                for j in range(TOPK):
                    link(dve.tensor_tensor(pick[j], ie, chosen[:, j, :].unsqueeze(2).broadcast_to((P, TILES, E)),
                                           ALU.is_equal))
                dve.tensor_tensor(pick_b[:, :, :], pick[0], pick[1], ALU.add).then_inc(picked, 1)
                for j in range(TOPK):
                    link(dve.tensor_tensor(prod[j], pick[j], scores_all[:, :, :], ALU.mult))
                    link(dve.tensor_reduce(top_s[:, j, :], prod[j], AX.X, ALU.add))
                link(dve.tensor_tensor(sum_s, top_s[:, 0, :], top_s[:, 1, :], ALU.add))
                link(dve.tensor_scalar(sum_s, sum_s, 1e-20, None, ALU.add))
                link(dve.reciprocal(sum_s, sum_s))
                link(dve.tensor_tensor(weight[:, :, :], top_s, sum_s.unsqueeze(1).broadcast_to((P, TOPK, TILES)),
                                       ALU.mult))
                dve.wait_ge(counted, 1)
                link(dve.tensor_copy(run[0], ps[:, 1, :].rearrange("p (t e) -> p t e", e=E)))
                at, s = 0, 1
                while s < TILES:
                    dve.tensor_copy(run[1 - at][:, 0:s, :], run[at][:, 0:s, :]).then_inc(chain, 1)
                    n[0] += 1
                    link(dve.tensor_tensor(run[1 - at][:, s:TILES, :], run[at][:, s:TILES, :],
                                           run[at][:, 0:TILES - s, :], ALU.add))
                    at, s = 1 - at, 2 * s
                total = run[at][:, TILES - 1, :]
                link(dve.tensor_scalar(cnt_i[0], total, float(P - 1), None, ALU.add))
                link(dve.tensor_scalar(cnt_i[1], cnt_i[0], P.bit_length() - 1, None, ALU.arith_shift_right))
                link(dve.tensor_copy(cnt[0], cnt_i[1]))
                link(dve.tensor_copy(cnt[1], cnt[0]))
                a, s = 1, 1
                while s < E:
                    dve.tensor_copy(cnt[a + 1][:, 0:s], cnt[a][:, 0:s]).then_inc(chain, 1)
                    n[0] += 1
                    link(dve.tensor_tensor(cnt[a + 1][:, s:E], cnt[a][:, s:E], cnt[a][:, 0:E - s], ALU.add))
                    a, s = a + 1, 2 * s
                ends, first = cnt[a], cnt[a + 1]
                link(dve.tensor_tensor(first, ends, cnt[0], ALU.subtract))
                link(dve.tensor_scalar(first, first, float(P), None, ALU.mult))
                link(dve.tensor_tensor(base, run[at], ps[:, 1, :].rearrange("p (t e) -> p t e", e=E), ALU.subtract))
                link(dve.tensor_tensor(base, base, ps[:, 0, :].rearrange("p (t e) -> p t e", e=E), ALU.add))
                link(dve.tensor_tensor(base, base, first.unsqueeze(1).broadcast_to((P, TILES, E)), ALU.add))
                for j in range(TOPK):
                    link(dve.tensor_tensor(prod[j], pick[j], base, ALU.mult))
                    link(dve.tensor_reduce(row_f[:, j, :], prod[j], AX.X, ALU.add))
                dve.tensor_copy(row_of[:, :, :], row_f).then_inc(rows_ready, 1)
                dve.wait_ge(iota_ready, 1)
                link(dve.tensor_tensor(over, iota_blk.unsqueeze(2).broadcast_to((P, SLOT_BLOCKS, E)),
                                       ends.unsqueeze(1).broadcast_to((P, SLOT_BLOCKS, E)), ALU.is_ge))
                link(dve.tensor_reduce(before_blk, over, AX.X, ALU.add))
                link(dve.tensor_scalar(before_blk, before_blk, float(E - 1), None, ALU.min))
                link(dve.tensor_copy(block_expert[:, :], before_blk))

                with dve.Fori(0, B) as b:
                    for r in range(2):
                        c = 2 * b + r
                        dve.wait_ge(gact_ready, c + 1)
                        dve.wait_ge(up_ready, c + 1)
                        dve.wait_ge(down_ready, 2 * b * 2)
                        dve.tensor_tensor(hid[r], gact[r], ps[:, 3 + 2 * r, :], ALU.mult).then_inc(hid_ready, 1)
                        for i in range(2):
                            dve.wait_ge(down_ready, 2 * c + i + 1)
                            tiles = bass.ds(c * CT + 2 * i, 2)
                            dve.tensor_tensor(sh_all[:, tiles, :], y_all[:, tiles, :],
                                              ps[:, 6 + i, :].rearrange("p (t d) -> p t d", d=D),
                                              ALU.add).then_inc(shared_done, 1)

            @blk.tensor
            def _(pe):
                pe.wait_ge(picked, 1)
                pb = pick_b[:, :, :].rearrange("p t e -> p (t e)")
                pe.matmul(ps[:, 0, :], before_b[:, :], pb, start=True, stop=True)
                pe.matmul(ps[:, 1, :], ones_b[:, :], pb, start=True, stop=True).then_inc(counted, 1)
                with pe.Fori(0, B) as b:
                    for r in range(2):
                        c = 2 * b + r
                        pe.wait_ge(hid_ready, 2 * b)
                        for w, bank, s in ((wsg, 2 + 2 * r, gate_ready), (wsu, 3 + 2 * r, up_ready)):
                            for h in range(DC):
                                mm = pe.matmul(ps[:, bank, :], w[:, h, :], yT_all[:, h, bass.ds(c * CH, CH)],
                                               start=(h == 0), stop=(h == DC - 1))
                            mm.then_inc(s, 1)
                        pe.wait_ge(hid_ready, c + 1)
                        for i in range(2):
                            pe.wait_ge(shared_done, 2 * c)
                            for t in (2 * i, 2 * i + 1):
                                mm = pe.matmul(ps[:, 6 + i, (t % 2) * D:(t % 2 + 1) * D],
                                               hid[r][:, t * P:(t + 1) * P], wsd[:, :], start=True, stop=True)
                            mm.then_inc(down_ready, 1)

        with ExitStack() as c5:
            ys = [piece(512 * r, 2, D) for r in range(2)]
            ysT = [work[:, 1024 + 512 * r:1536 + 512 * r].rearrange("p (h k t) -> p h k t", h=DC, k=2)
                   for r in range(2)]
            gx = [piece(2048 + 256 * r, 2, F) for r in range(2)]
            hx = [piece(2560 + 256 * r, 2, F) for r in range(2)]
            hxT = [piece(3072 + 256 * r, 2, P) for r in range(2)]
            zs = [piece(3584 + 512 * r, 2, D) for r in range(2)]
            ys_loaded = [sem(f"ys_loaded{r}") for r in range(2)]
            z_stored = [sem(f"z_stored{r}") for r in range(2)]
            ysT_ready = sem("ysT_ready")
            ysT_copied = sem("ysT_copied")
            gu_ready = sem("gu_ready")
            gx_ready = sem("gx_ready")
            hx_ready = sem("hx_ready")
            hxT_ready = sem("hxT_ready")
            hxT_copied = sem("hxT_copied")
            z_ready = sem("z_ready")
            z_copied = sem("z_copied")
            y_rows = y_sorted.rearrange("(n p) d -> p n d", p=P)
            z_rows = z_sorted.rearrange("(n p) d -> p n d", p=P)
            blk = c5.enter_context(nc.Block())

            def staggered(eng, stages):
                def turn(n, k2, r):
                    for ahead, stage in stages:
                        if isinstance(n, int) and not 0 <= n + ahead < PAIRS:
                            continue
                        stage(n + ahead, k2 + (r + ahead) // 2, (r + ahead) % 2)

                lead = max(a for a, _ in stages)
                lead += lead % 2
                for n in range(-lead, 2):
                    turn(n, n // 2, n % 2)
                with eng.Fori(1, (PAIRS - lead) // 2) as j:
                    turn(2 * j, j, 0)
                    turn(2 * j + 1, j, 1)
                for n in range(PAIRS - lead, PAIRS):
                    turn(n, n // 2, n % 2)

            @blk.sync
            def _(sp):
                def load(n, k2, r):
                    wait_count(sp, ysT_ready, n - 1)
                    sp.dma_start(ys[r], y_rows[:, bass.ds(2 * n, 2), :]).then_inc(ys_loaded[r], 16)

                load(0, 0, 0)
                load(1, 0, 1)
                with sp.Fori(0, PAIRS // 2 - 1) as j:
                    load(2 * j + 2, j + 1, 0)
                    load(2 * j + 3, j + 1, 1)

            @blk.gpsimd
            def _(pool):
                with pool.Fori(0, PAIRS // 2) as j:
                    for r in range(2):
                        pool.wait_ge(z_copied, 2 * j + r + 1)
                        pool.dma_start(z_rows[:, bass.ds(4 * j + 2 * r, 2), :], zs[r]).then_inc(z_stored[r], 16)
                for r in range(2):
                    pool.wait_ge(z_stored[r], 16 * (PAIRS // 2))

            @blk.scalar
            def _(act):
                def turned(n, k2, r):
                    act.wait_ge(ysT_ready, n + 1)
                    wait_count(act, gu_ready, n - 1)
                    act.activation(ysT[r].rearrange("p h k t -> p (h k t)"), ps[:, r, :], ACT.Copy)\
                        .then_inc(ysT_copied, 1)

                def silu(n, k2, r):
                    act.wait_ge(gu_ready, n + 1)
                    wait_count(act, hx_ready, n - 1)
                    act.activation(gx[r], ps[:, 2 + r, :].rearrange("p (k c) -> p k c", k=2)[:, :, 0:F], ACT.Silu)\
                        .then_inc(gx_ready, 1)

                staggered(act, [(3, turned), (2, silu)])

            @blk.vector
            def _(dve):
                def hidden(n, k2, r):
                    dve.wait_ge(gx_ready, n + 1)
                    wait_count(dve, hxT_ready, n - 1)
                    dve.tensor_tensor(hx[r], gx[r], ps[:, 2 + r, :].rearrange("p (k c) -> p k c", k=2)[:, :, F:2 * F],
                                      ALU.mult).then_inc(hx_ready, 1)

                def turned(n, k2, r):
                    dve.wait_ge(hxT_ready, n + 1)
                    wait_count(dve, z_ready, n - 1)
                    dve.tensor_copy(hxT[r], ps[:, 4 + r, 0:2 * P].rearrange("p (k t) -> p k t", k=2))\
                        .then_inc(hxT_copied, 1)

                def result(n, k2, r):
                    dve.wait_ge(z_ready, n + 1)
                    wait_count(dve, z_stored[r], 16 * k2)
                    dve.tensor_copy(zs[r], ps[:, 6 + r, :].rearrange("p (k d) -> p k d", k=2)).then_inc(z_copied, 1)

                staggered(dve, [(2, hidden), (1, turned), (0, result)])

            @blk.tensor
            def _(pe):
                def expert(n, k):
                    return pe.value_load(block_expert[0:1, bass.ds(2 * n + k, 1)], min_val=0, max_val=E - 1)

                def turn_rows(n, k2, r):
                    pe.wait_ge(ys_loaded[r], 16 * k2 + 16)
                    wait_count(pe, ysT_copied, n - 1)
                    for h in range(DC):
                        for k in range(2):
                            mm = pe.transpose(ps[:, r, (2 * h + k) * P:(2 * h + k + 1) * P],
                                              ys[r][:, k, h * P:(h + 1) * P], ident[:, :])
                    mm.then_inc(ysT_ready, 1)

                def gate_up(n, k2, r):
                    pe.wait_ge(ysT_copied, n + 1)
                    wait_count(pe, hx_ready, n - 1)
                    for k in range(2):
                        e = expert(n, k)
                        for h in range(DC):
                            mm = pe.matmul(ps[:, 2 + r, 2 * F * k:2 * F * (k + 1)], ysT[r][:, h, k, :],
                                           wgu[:, bass.ds(e, 1), h, :].squeeze(1), start=(h == 0), stop=(h == DC - 1))
                    mm.then_inc(gu_ready, 1)

                def turn_hidden(n, k2, r):
                    pe.wait_ge(hx_ready, n + 1)
                    wait_count(pe, hxT_copied, n - 1)
                    for k in range(2):
                        mm = pe.transpose(ps[:, 4 + r, k * P:(k + 1) * P], hx[r][:, k, :], ident[:, :])
                    mm.then_inc(hxT_ready, 1)

                def down(n, k2, r):
                    pe.wait_ge(hxT_copied, n + 1)
                    wait_count(pe, z_copied, n - 1)
                    for k in range(2):
                        e = expert(n, k)
                        mm = pe.matmul(ps[:, 6 + r, D * k:D * (k + 1)], hxT[r][:, k, :],
                                       wdn[:, bass.ds(e, 1), :].squeeze(1), start=True, stop=True)
                    mm.then_inc(z_ready, 1)

                staggered(pe, [(3, turn_rows), (2, gate_up), (1, turn_hidden), (0, down)])

        with ExitStack() as c6:
            zg = [work[:, 2048 * r:2048 * (r + 1)].rearrange("p (t j d) -> p t j d", t=CT, j=TOPK) for r in range(2)]
            acc = [piece(4096 + 1024 * r, CT, D) for r in range(2)]
            stats = c6.enter_context(nc.sbuf_tensor("stats2", [P, CT, 6], F32))
            moments = c6.enter_context(nc.sbuf_tensor("moments2", [P, CT, 2], F32))
            rstd = c6.enter_context(nc.sbuf_tensor("rstd2", [P, CT], F32))
            gathered = [sem(f"gathered{r}") for r in range(2)]
            first_added = sem("first_added")
            both_added = sem("both_added")
            stats_ready = sem("stats_ready2")
            moments_ready = sem("moments_ready2")
            rstd_step = sem("rstd_step2")
            rstd_ready = sem("rstd_ready2")
            out_ready = sem("out_ready")
            out_stored = [sem(f"out_stored{r}") for r in range(2)]
            o_v = out.rearrange("b (t p) d -> p (b t) d", p=P)
            blk = c6.enter_context(nc.Block())

            @blk.gpsimd
            def _(pool):
                def gather(c):
                    wait_count(pool, both_added, CT * (c - 1))
                    for t in range(CT):
                        for j in range(TOPK):
                            pool.indirect_dma_start(
                                out=zg[c % 2][:, t, j, :], out_offset=None, in_=z_sorted,
                                in_offset=bass.IndirectOffsetOnAxis(ap=row_of[:, j, c * CT + t:c * CT + t + 1], axis=0))\
                                .then_inc(gathered[c % 2], 16)

                gather(0)
                for c in range(2 * B):
                    if c + 1 < 2 * B:
                        gather(c + 1)
                    wait_apart(pool, moments_ready, CT * c + CT, pool_waited)
                    pool.tensor_scalar(rstd[:, :], moments[:, :, 1], EPS, None, ALU.add).then_inc(rstd_step, 1)
                    pool.wait_ge(rstd_step, c + 1)
                    pool.tensor_tensor(rstd[:, :], rstd[:, :], minus_half[:, :], ALU.pow).then_inc(rstd_ready, 1)

            @blk.vector
            def _(dve):
                with dve.Fori(0, B) as b:
                    for r in range(2):
                        c = 2 * b + r
                        dve.wait_ge(gathered[r], 16 * TOPK * CT * b + 16 * TOPK * CT)
                        dve.wait_ge(out_stored[r], 16 * b)
                        for t in range(CT):
                            dve.scalar_tensor_tensor(acc[r][:, t, :], zg[r][:, t, 0, :],
                                                     weight[:, 0, bass.ds(c * CT + t, 1)],
                                                     sh_all[:, bass.ds(c * CT + t, 1), :].squeeze(1), ALU.mult, ALU.add)\
                                .then_inc(first_added, 1)
                        for t in range(CT):
                            dve.wait_ge(first_added, CT * c + t + 1)
                            dve.scalar_tensor_tensor(acc[r][:, t, :], zg[r][:, t, 1, :],
                                                     weight[:, 1, bass.ds(c * CT + t, 1)],
                                                     acc[r][:, t, :], ALU.mult, ALU.add).then_inc(both_added, 1)
                        for t in range(CT):
                            dve.wait_ge(both_added, CT * c + t + 1)
                            dve.bn_stats(stats[:, t, :], acc[r][:, t, :]).then_inc(stats_ready, 1)
                        for t in range(CT):
                            wait_apart(dve, stats_ready, CT * c + t + 1, dve_waited)
                            dve.bn_aggr(moments[:, t, :], stats[:, t, :]).then_inc(moments_ready, 1)
                        dve.wait_ge(rstd_ready, c + 1)
                        for t in range(CT):
                            ins = dve.tensor_scalar(acc[r][:, t, :], acc[r][:, t, :], moments[:, t, 0:1],
                                                    rstd[:, t:t + 1], ALU.subtract, ALU.mult)
                        ins.then_inc(out_ready, 1)

            @blk.sync
            def _(sp):
                with sp.Fori(0, B) as b:
                    for r in range(2):
                        sp.wait_ge(out_ready, 2 * b + r + 1)
                        sp.dma_start(o_v[:, bass.ds(b * NT + r * CT, CT), :], acc[r]).then_inc(out_stored[r], 16)
                for r in range(2):
                    sp.wait_ge(out_stored[r], 16 * B)


_INS = ["x", "xT", "Wq", "bq", "Wk", "bk", "Wv", "bv", "Wo", "bo", "gate_w", "expert_bias", "sg_w", "su_w", "sd_w",
        "gu_w", "down_w"]


def kernel(**inputs):
    import numpy as _np
    import concourse.bacc as _bacc
    from concourse import mybir as _mybir
    from concourse.bass_utils import run_bass_kernel_spmd as _run

    given = {n: _np.asarray(inputs["L0_attn_" + n]) for n in ("x", "Wq", "bq", "Wk", "bk", "Wv", "bv", "Wo", "bo")}
    for name in ("bq", "bk"):
        given[name] = given[name].reshape(DC, P).T
    given["xT"] = given["x"].reshape(B * N, D).T
    for name, key in (("gate_w", "gate_w"), ("expert_bias", "expert_bias"), ("sg_w", "shared_gate_w"),
                      ("su_w", "shared_up_w"), ("sd_w", "shared_down_w"), ("gu_w", "experts_gate_up"),
                      ("down_w", "experts_down")):
        given[name] = _np.asarray(inputs["L0_ffn_" + key])
    nc = _bacc.Bacc("TRN2", target_bir_lowering=False, num_devices=1)
    arrays, args = {}, []
    for name in _INS:
        a = _np.ascontiguousarray(given[name])
        arrays[f"in_{name}"] = a
        args.append(nc.dram_tensor(f"in_{name}", a.shape, _mybir.dt.from_np(a.dtype), kind="ExternalInput").ap())
    args.append(nc.dram_tensor("out_0", (B, N, D), _mybir.dt.float32, kind="ExternalOutput").ap())
    build(nc, *args)
    r = _run(nc, [arrays], core_ids=[0])
    return r.results[0]["out_0"]
```

```python
from contextlib import ExitStack

import numpy as np
import concourse.bass as bass
from concourse import mybir

F32 = mybir.dt.float32
BF16 = mybir.dt.bfloat16
I32 = mybir.dt.int32
U32 = mybir.dt.uint32
ALU = mybir.AluOpType
ACT = mybir.ActivationFunctionType
AX = mybir.AxisListType

P = 128
B, N, D = 4, 1024, 256
H, DK = 16, 16
DC = D // P
GH = 4
GROUPS = H // GH
GW = GH * DK
STEPS = B * GROUPS
CH = 512
HALVES = N // CH
CT = CH // P
NT = N // P
TILES = B * NT
E, F, TOPK = 16, 128, 2
EPS = 1e-5
NEG = -1e30

PRODUCTS = [(0, 0), (0, 1), (1, 0), (0, 2), (2, 0), (1, 1)]
KS = len(PRODUCTS) * DK
KM = KS + 3

UNITS = [(qc, kt) for qc in range(HALVES) for kt in range(CT * (qc + 1))]
NU = len(UNITS)
DIAG = [u for u, (qc, kt) in enumerate(UNITS) if kt >= CT * qc]
PSLOTS = 3
MAXES = []
for qt in range(NT):
    for half in range(qt // CT + 1):
        w = min(CH, (qt + 1) * P - half * CH)
        heads = 4 if w == P else 2 if w == 2 * P else 1
        MAXES += [(qt, h, heads, half, w) for h in range(0, GH, heads)]
NM = len(MAXES)
NM0 = sum(m[0] < CT for m in MAXES)
STACKS = 3
RING = [4, 5, 7]


def unit_width(u):
    qc, kt = UNITS[u]
    return CH - max(0, P * (kt - CT * qc))


def attention_order():
    main = [("scores", 0, 0), ("scores", 0, 1), ("weigh", -1, 0)]
    for u in range(NU - 1):
        main += [("scores", u + 1, 0), ("scores", u + 1, 1), ("weigh", u, 0)]
    cost = [unit_width(u) * (2 if what == "weigh" else 1) for what, u, _ in main]
    pieces = [m[2] * m[4] + 60 for m in MAXES]
    order, n, done, spent = [], 0, 0, 0
    for item, c in zip(main, cost):
        order.append(item)
        if item == ("scores", 1, 1):
            order.append(("turn_max", 1, 0))
        if item == ("weigh", 1, 0):
            order.append(("turn_out", 1, 0))
        if item == ("weigh", 5, 0):
            order.append(("turn_out", 0, 0))
        done += c
        while n < NM and (spent + pieces[n] / 2) / sum(pieces) <= done / sum(cost):
            order.append(("max", n, 0))
            spent += pieces[n]
            n += 1
            if n == NM0 + TURN_AFTER:
                order.append(("turn_max", 0, 0))
    assert n == NM
    return order


TURN_AFTER = 3
ORDER = attention_order()
RING_USERS = [item for item in ORDER if item[0] in ("max", "turn_max", "turn_out")]
assert len(RING_USERS) % len(RING) == 0


def ring_bank(item):
    return RING[RING_USERS.index(item) % len(RING)]


def present(item, first, last):
    if first is None:
        return item[0] == "max"
    if last:
        return item in (("turn_max", 1, 0), ("turn_out", 1, 0), ("turn_out", 0, 0))
    return not (first and item == ("turn_out", 1, 0))


def ring_before(item, first, last, second=False):
    at = RING_USERS.index(item) - len(RING)
    while at >= 0:
        if present(RING_USERS[at], first, last):
            return RING_USERS[at], 0
        at -= len(RING)
    if first is None:
        return None, 0
    at += len(RING_USERS)
    while not present(RING_USERS[at], None if first else second, False):
        at -= len(RING)
    return RING_USERS[at], 1


SLOT_BLOCKS = TILES * TOPK + E
PAIRS = SLOT_BLOCKS // 2
ROWS = SLOT_BLOCKS * P


def wait_count(eng, sem, value):
    if isinstance(value, int) and value <= 0:
        return
    eng.wait_ge(sem, value)


def wait_apart(eng, sem, value, waited):
    eng.wait_ge(sem, value)
    eng.sem_inc(waited, 1)


def staggered(eng, stages, count):
    lag = max(b for b, _ in stages)

    def turn(t, k2, r):
        for behind, stage in stages:
            if isinstance(t, int) and not 0 <= t - behind < count:
                continue
            stage(t - behind, k2 + (r - behind) // 2, (r - behind) % 2)

    start = lag + 2 + lag % 2
    for t in range(start):
        turn(t, t // 2, t % 2)
    with eng.Fori(start // 2, count // 2) as j:
        turn(2 * j, j, 0)
        turn(2 * j + 1, j, 1)
    for t in range(count, count + lag):
        turn(t, t // 2, t % 2)


CHUNKS = B * HALVES


def build(nc, x, xT, Wq, bq, Wk, bk, Wv, bv, Wo, bo, gate_w, expert_bias, sg_w, su_w, sd_w, gu_w, down_w, out):
    with ExitStack() as ctx:
        def sb(name, shape, dt):
            return ctx.enter_context(nc.sbuf_tensor(name, shape, dt))

        def sem(name):
            return ctx.enter_context(nc.semaphore(name))

        def dram(name, shape, dt):
            return nc.dram_tensor(name, shape, dt, kind="Internal").ap()

        qk_parts = dram("qk_parts", (2, 3, B * D, N), BF16)
        y_sorted = dram("y_sorted", (ROWS, D), F32)
        z_sorted = dram("z_sorted", (ROWS, D), F32)

        ps = ctx.enter_context(nc.psum_tensor("ps", [P, 8, CH], F32))

        wqk = sb("wqk", [P, 2, DC, D], F32)
        wv = sb("wv", [P, DC, D], F32)
        wo = sb("wo", [P, DC, D], F32)
        bqk = sb("bqk", [P, 2, DC], F32)
        bv_all = sb("bv_all", [P, D], F32)
        bo_all = sb("bo_all", [P, D], F32)
        gate = sb("gate", [P, DC, E], F32)
        ebias = sb("ebias", [P, E], F32)
        wsg = sb("wsg", [P, DC, F], F32)
        wsu = sb("wsu", [P, DC, F], F32)
        wsd = sb("wsd", [P, D], F32)
        wgu = sb("wgu", [P, E, DC, 2 * F], F32)
        wdn = sb("wdn", [P, E, D], F32)
        ident = sb("ident", [P, P], F32)
        ident_b = sb("ident_b", [P, P], BF16)
        mask_b = sb("mask_b", [P, P], BF16)
        before_b = sb("before_b", [P, P], BF16)
        ones_b = sb("ones_b", [P, P], BF16)
        iota_e = sb("iota_e", [P, E], F32)
        minus_half = sb("minus_half", [P, CT], F32)
        v_all = sb("v_all", [P, STEPS, NT, GW], F32)
        y_all = v_all[:, :, :, :].rearrange("p a b c -> p (a b c)").rearrange("p (t d) -> p t d", d=D)
        a_all = sb("a_all", [P, STEPS, NT, GW], F32)
        sh_all = a_all[:, :, :, :].rearrange("p a b c -> p (a b c)").rearrange("p (t d) -> p t d", d=D)
        stacks = sb("stacks", [P, 2, 2, GH, N], BF16)
        yT_all = stacks[:, :, :, :, :].rearrange("p a b c d -> p (a b c d)").bitcast(F32) \
            .rearrange("p (c t) -> p c t", c=DC)
        work = sb("work", [P, 8192], F32)

        def piece(at, *dims):
            n = int(np.prod(dims))
            v = work[:, at:at + n]
            if len(dims) == 2:
                v = v.rearrange("p (a b) -> p a b", b=dims[1])
            if len(dims) == 3:
                v = v.rearrange("p (a b c) -> p a b c", b=dims[1], c=dims[2])
            return v

        w_loaded = sem("w_loaded")
        const_ready = sem("const_ready")
        const_zeroed = sem("const_zeroed")
        dve_waited = sem("dve_waited")
        pool_waited = sem("pool_waited")

        with ExitStack() as c1:
            xt = [piece(1024 * i, DC, CH) for i in range(2)]
            rest = [piece(2048 + 512 * t, CH) for t in range(4)]
            parts = [piece(4096 + 768 * t, 768).bitcast(BF16).rearrange("p (r t) -> p r t", r=3) for t in range(4)]
            xt_loaded = [sem(f"xt_loaded{i}") for i in range(2)]
            proj_ready = [sem(f"proj_ready{t}") for t in range(4)]
            hi_ready = sem("hi_ready")
            rest_ready = [sem(f"rest_ready{t}") for t in range(4)]
            mid_ready = sem("mid_ready")
            lo_ready = sem("lo_ready")
            stored = [sem(f"stored{t}") for t in range(4)]
            v_ready = [sem(f"v_ready{i}") for i in range(2)]
            v_copied = [sem(f"v_copied{i}") for i in range(2)]
            big_loaded = sem("big_loaded")
            xT_v = xT.rearrange("(c p) t -> p c t", p=P)
            blk = c1.enter_context(nc.Block())

            @blk.sync
            def _(sp):
                def load(b, half):
                    sp.dma_start(xt[half], xT_v[:, :, bass.ds(b * N + half * CH, CH)]).then_inc(xt_loaded[half], 16)

                def store(b, half):
                    for t in range(4):
                        sp.wait_ge(lo_ready, (2 * b + half) * 4 + t + 1)
                        sp.dma_start(
                            qk_parts[t // 2, :, bass.ds(b * D + (t % 2) * P, P), half * CH:(half + 1) * CH]
                            .rearrange("r p t -> p r t"), parts[t]).then_inc(stored[t], 16)

                load(0, 0)
                with sp.Fori(0, B - 1) as b:
                    sp.wait_ge(v_ready[1], 2 * b)
                    load(b, 1)
                    store(b, 0)
                    sp.wait_ge(v_ready[1], 2 * b + 1)
                    load(b + 1, 0)
                    store(b, 1)
                sp.wait_ge(v_ready[1], 2 * (B - 1))
                load(B - 1, 1)
                store(B - 1, 0)
                store(B - 1, 1)
                for t in range(4):
                    sp.wait_ge(stored[t], 16 * 2 * B)

            @blk.gpsimd
            def _(pool):
                pool.memset(ident[:, :], 0.0).then_inc(const_zeroed, 1)
                pool.memset(ident_b[:, :], 0.0).then_inc(const_zeroed, 1)
                pool.memset(mask_b[:, :], 0.0).then_inc(const_zeroed, 1)
                pool.memset(before_b[:, :], 0.0).then_inc(const_zeroed, 1)
                pool.memset(ones_b[:, :], 1.0).then_inc(const_zeroed, 1)
                pool.memset(minus_half[:, :], -0.5).then_inc(const_zeroed, 1)
                pool.wait_ge(const_zeroed, 6)
                pool.affine_select(out=ident[:, :], in_=ident[:, :], compare_op=ALU.not_equal, fill=1.0, base=0,
                                   pattern=[[-1, P]], channel_multiplier=1).then_inc(const_ready, 1)
                pool.affine_select(out=ident_b[:, :], in_=ident_b[:, :], compare_op=ALU.not_equal, fill=1.0, base=0,
                                   pattern=[[-1, P]], channel_multiplier=1).then_inc(const_ready, 1)
                pool.affine_select(out=mask_b[:, :], in_=mask_b[:, :], compare_op=ALU.is_ge, fill=NEG, base=0,
                                   pattern=[[-1, P]], channel_multiplier=1).then_inc(const_ready, 1)
                pool.affine_select(out=before_b[:, :], in_=before_b[:, :], compare_op=ALU.is_ge, fill=1.0, base=0,
                                   pattern=[[-1, P]], channel_multiplier=1).then_inc(const_ready, 1)
                pool.iota(iota_e[:, :], [[1, E]], base=0, channel_multiplier=0,
                          allow_small_or_imprecise_dtypes=True).then_inc(const_ready, 1)
                with pool.Fori(0, B) as b:
                    for half in range(2):
                        for t in range(4):
                            pool.wait_ge(mid_ready, (2 * b + half) * 4 + t + 1)
                            pool.tensor_tensor(parts[t][:, 2, :], rest[t], parts[t][:, 1, :],
                                               ALU.subtract).then_inc(lo_ready, 1)

            @blk.scalar
            def _(act):
                for i, w in enumerate((Wq, Wk)):
                    act.dma_start(wqk[:, i], w.rearrange("(c p) n -> p c n", p=P)).then_inc(w_loaded, 16)
                act.dma_start(wv[:, :, :], Wv.rearrange("(c p) n -> p c n", p=P)).then_inc(w_loaded, 16)
                for i, w in enumerate((bq, bk)):
                    act.dma_start(bqk[:, i], w).then_inc(w_loaded, 16)
                act.dma_start(bv_all[:, :], bv.partition_broadcast(P)).then_inc(w_loaded, 16)
                act.dma_start(bo_all[:, :], bo.partition_broadcast(P)).then_inc(big_loaded, 16)
                act.dma_start(ebias[:, :], expert_bias.partition_broadcast(P)).then_inc(big_loaded, 16)
                act.dma_start(wo[:, :, :], Wo.rearrange("(c p) n -> p c n", p=P)).then_inc(big_loaded, 16)
                act.dma_start(gate[:, :, :], gate_w.rearrange("(c p) n -> p c n", p=P)).then_inc(big_loaded, 16)
                act.dma_start(wsg[:, :, :], sg_w.rearrange("(c p) n -> p c n", p=P)).then_inc(big_loaded, 16)
                act.dma_start(wsu[:, :, :], su_w.rearrange("(c p) n -> p c n", p=P)).then_inc(big_loaded, 16)
                act.dma_start(wsd[:, :], sd_w).then_inc(big_loaded, 16)
                act.dma_start(wdn[:, :, :], down_w.rearrange("e p n -> p e n")).then_inc(big_loaded, 16)
                act.wait_ge(w_loaded, 16 * 6)

                def high(b, half, t):
                    act.wait_ge(proj_ready[t], 2 * b + half + 1)
                    act.wait_ge(stored[t], 16 * (2 * b + half))
                    act.activation(parts[t][:, 0, :], ps[:, t, :], ACT.Identity,
                                   bias=bqk[:, t // 2, t % 2:t % 2 + 1]).then_inc(hi_ready, 1)

                def middle(b, half, t):
                    act.wait_ge(rest_ready[t], 2 * b + half + 1)
                    act.activation(parts[t][:, 1, :], rest[t], ACT.Copy).then_inc(mid_ready, 1)

                with act.Fori(0, B) as b:
                    for half in range(2):
                        high(b, half, 0)
                        for t in range(1, 4):
                            high(b, half, t)
                            middle(b, half, t - 1)
                        middle(b, half, 3)
                act.wait_ge(big_loaded, 16 * 8)

            @blk.vector
            def _(dve):
                dve.wait_ge(w_loaded, 16 * 6)
                with dve.Fori(0, B) as b:
                    for half in range(2):
                        for t in range(4):
                            dve.wait_ge(hi_ready, (2 * b + half) * 4 + t + 1)
                            dve.scalar_tensor_tensor(rest[t], ps[:, t, :], bqk[:, t // 2, t % 2:t % 2 + 1],
                                                     parts[t][:, 0, :], ALU.add,
                                                     ALU.subtract).then_inc(rest_ready[t], 1)
                        for i in range(2):
                            dve.wait_ge(v_ready[i], 2 * b + half + 1)
                            for j in range(2):
                                tile = half * CT + 2 * i + j
                                ins = dve.tensor_tensor(
                                    v_all[:, bass.ds(b * GROUPS, GROUPS), tile, :],
                                    ps[:, 4 + i, j * D:(j + 1) * D].rearrange("p (g e) -> p g e", g=GROUPS),
                                    bv_all[:, :].rearrange("p (g e) -> p g e", g=GROUPS), ALU.add)
                            ins.then_inc(v_copied[i], 1)

            @blk.tensor
            def _(pe):
                pe.wait_ge(w_loaded, 16 * 6)
                with pe.Fori(0, B) as b:
                    for half in range(2):
                        pe.wait_ge(xt_loaded[half], 16 * b + 16)
                        for t in range(4):
                            pe.wait_ge(rest_ready[t], 2 * b + half)
                            for c in range(DC):
                                mm = pe.matmul(ps[:, t, :], wqk[:, t // 2, c, (t % 2) * P:(t % 2 + 1) * P],
                                               xt[half][:, c, :], start=(c == 0), stop=(c == DC - 1))
                            mm.then_inc(proj_ready[t], 1)
                        for i in range(2):
                            pe.wait_ge(v_copied[i], 2 * b + half)
                            for j in range(2):
                                tt = 2 * i + j
                                for c in range(DC):
                                    mm = pe.matmul(ps[:, 4 + i, j * D:(j + 1) * D],
                                                   xt[half][:, c, tt * P:(tt + 1) * P], wv[:, c, :],
                                                   start=(c == 0), stop=(c == DC - 1))
                            mm.then_inc(v_ready[i], 1)

        with ExitStack() as c2:
            probs = piece(0, PSLOTS * GH, CH)
            vg = [c2.enter_context(nc.sbuf_tensor(f"vg{r}", [P, NT, GH, 32], F32)) for r in range(2)]
            vg.append(work[:, 6144:7168].rearrange("p (t h e) -> p t h e", t=NT, h=GH))
            oT = [c2.enter_context(nc.sbuf_tensor(f"oT{r}", [P, CH], F32)) for r in range(2)]
            mT = [c2.enter_context(nc.sbuf_tensor(f"mT{r}", [3 * GH, CH], BF16)) for r in range(2)]
            recip = c2.enter_context(nc.sbuf_tensor("recip", [P, CT, GH], F32))
            m_neg = c2.enter_context(nc.sbuf_tensor("m_neg", [P, NT, GH], F32))
            m_neg_late = c2.enter_context(nc.sbuf_tensor("m_neg_late", [P, CT, GH], F32))
            m_rest = c2.enter_context(nc.sbuf_tensor("m_rest", [P, NT, GH], F32))
            m_parts = c2.enter_context(nc.sbuf_tensor("m_parts", [P, NT, 3, GH], BF16))
            zero = piece(7168, 1024)
            third = wgu[:, :, :, :].rearrange("p e c n -> p (e c n)")[:, 0:2 * GH * N // 2].bitcast(BF16) \
                .rearrange("p (s h t) -> p s h t", s=2, h=GH)
            qs = [stacks[:, 0, 0], stacks[:, 1, 0], third[:, 0]]
            ks = [stacks[:, 0, 1], stacks[:, 1, 1], third[:, 1]]
            SCORE_BANK, OUT_BANK = 0, 6

            ones_ready = sem("ones_ready")
            zero_ready = sem("zero_ready")
            zero_stored = sem("zero_stored")
            stack_loaded = [sem(f"stack_loaded{r}") for r in range(STACKS)]
            m_loaded = [sem(f"m_loaded{r}") for r in range(2)]
            score_max_ready = sem("score_max_ready")
            reduced = sem("reduced")
            m_step = sem("m_step")
            m_ready = [sem(f"m_ready{r}") for r in range(2)]
            mT_ready = [sem(f"mT_ready{r}") for r in range(2)]
            mT_copied = [sem(f"mT_copied{r}") for r in range(2)]
            score_ready = sem("score_ready")
            exp_done = sem("exp_done")
            masked = sem("masked")
            pv_done = sem("pv_done")
            o_copied = sem("o_copied")
            oT_ready = sem("oT_ready")
            recip_ready = sem("recip_ready")
            a_written = sem("a_written")
            vg_ready = sem("vg_ready")
            blk = c2.enter_context(nc.Block())

            @blk.sync
            def _(sp):
                def load_stacks(i, r):
                    for n, (qp, kp) in enumerate(PRODUCTS):
                        for s, (dst, part) in enumerate(((qs, qp), (ks, kp))):
                            sp.dma_start(dst[r][n * DK:(n + 1) * DK],
                                         qk_parts[s, part, bass.ds(i * GW, GW), :]
                                         .rearrange("(h d) t -> d h t", d=DK)).then_inc(stack_loaded[r], 16)

                def load_max(i, r, qc):
                    sp.wait_ge(mT_copied[qc], i + 1)
                    for part in range(3):
                        sp.dma_start(qs[r][KS + part:KS + part + 1, :, qc * CH:(qc + 1) * CH],
                                     mT[qc][part * GH:(part + 1) * GH, :]).then_inc(m_loaded[qc], 16)

                def step(i, r, more=True, load=True):
                    load_max(i, r, 1)
                    if more:
                        if load:
                            wait_count(sp, pv_done, NU * i)
                            load_stacks(i + 2, (r + 2) % STACKS)
                        load_max(i + 1, (r + 1) % STACKS, 0)

                load_stacks(0, 0)
                load_stacks(1, 1)
                sp.wait_ge(zero_ready, 1)
                for n in range(ROWS * D // (P * 4096)):
                    sp.dma_start(y_sorted[n * 16 * P:(n + 1) * 16 * P, :].rearrange("(p a) d -> p (a d)", p=P)
                                 .rearrange("p (a d) -> p a d", a=4),
                                 zero.unsqueeze(1).broadcast_to((P, 4, 1024))).then_inc(zero_stored, 16)
                load_max(0, 0, 0)
                step(0, 0)
                with sp.Fori(0, 4) as j:
                    for q in range(STACKS):
                        step(STACKS * j + q + 1, (q + 1) % STACKS)
                step(13, 13 % STACKS)
                step(14, 14 % STACKS, load=False)
                step(15, 15 % STACKS, more=False)
                sp.wait_ge(zero_stored, 16 * (ROWS * D // (P * 4096)))

            @blk.gpsimd
            def _(pool):
                for r in range(STACKS):
                    pool.memset(vg[r][:, :, :, DK:32], 1.0).then_inc(ones_ready, 1)
                pool.memset(zero, 0.0).then_inc(zero_ready, 1)
                pool.wait_ge(ones_ready, 2 * STACKS)

                def values(i, r):
                    pool.tensor_copy(vg[r][:, :, :, 0:DK],
                                     v_all[:, bass.ds(i, 1)].rearrange("p a t (h e) -> p (a t) h e", e=DK))\
                        .then_inc(vg_ready, 1)

                def mask(i, u):
                    off = P * (UNITS[u][1] - CT * UNITS[u][0])
                    s = (u % PSLOTS) * GH
                    wait_apart(pool, exp_done, 2 * (NU * i + u) + 2, pool_waited)
                    blk_ = probs[:, s:s + GH, off:off + P]
                    pool.affine_select(out=blk_, in_=blk_, compare_op=ALU.is_ge, fill=0.0, base=0,
                                       pattern=[[0, GH], [1, P]], channel_multiplier=-1).then_inc(masked, 1)

                def step(i, r, more=True):
                    for u in DIAG[:CT]:
                        mask(i, u)
                    if more:
                        wait_count(pool, pv_done, NU * (i - 1))
                        values(i + 1, (r + 1) % STACKS)
                    for u in DIAG[CT:]:
                        mask(i, u)

                values(0, 0)
                step(0, 0)
                with pool.Fori(0, 4) as j:
                    for q in range(STACKS):
                        step(STACKS * j + q + 1, (q + 1) % STACKS)
                step(13, 13 % STACKS)
                step(14, 14 % STACKS)
                step(15, 15 % STACKS, more=False)

            @blk.scalar
            def _(act):
                def exp(i, u):
                    off = CH - unit_width(u)
                    s = (u % PSLOTS) * GH
                    wait_count(act, pv_done, NU * i + u - PSLOTS + 1)
                    for pair in range(2):
                        act.wait_ge(score_ready, 2 * (NU * i + u) + pair + 1)
                        act.activation(probs[:, s + 2 * pair:s + 2 * pair + 2, off:CH],
                                       ps[:, SCORE_BANK + 2 * pair:SCORE_BANK + 2 * pair + 2, off:CH],
                                       ACT.Exp, scale=float(DK) ** -0.5).then_inc(exp_done, 1)

                def copy_out(i, qc):
                    act.wait_ge(pv_done, NU * i + (CT if qc == 0 else NU))
                    wait_count(act, oT_ready, 2 * i + qc - 1)
                    act.activation(oT[qc][:, :], ps[:, OUT_BANK, :], ACT.Copy).then_inc(o_copied, 1)

                def step(i, prev=True):
                    for u in range(NU):
                        exp(i, u)
                        if u == 0 and prev:
                            copy_out(i - 1, 1)
                        if u == CT:
                            copy_out(i, 0)

                step(0, prev=False)
                with act.Fori(1, STEPS) as i:
                    step(i)
                copy_out(STEPS - 1, 1)

            @blk.vector
            def _(dve):
                def maximum(i, n):
                    qt, h, heads, half, w = MAXES[n]
                    dst = m_neg[:, qt, h:h + heads] if half == 0 else m_neg_late[:, qt - CT, h:h + heads]
                    dve.wait_ge(score_max_ready, NM * i + n + 1)
                    dve.tensor_reduce(dst, ps[:, ring_bank(("max", n, 0)), 0:heads * w]
                                      .rearrange("p (h k) -> p h k", h=heads), AX.X, ALU.max,
                                      negate=True).then_inc(reduced, 1)

                def copy_max(i, qc):
                    dve.wait_ge(mT_ready[qc], i + 1)
                    wait_count(dve, m_loaded[qc], 48 * i)
                    dve.tensor_copy(mT[qc][:, :], ps[0:3 * GH, ring_bank(("turn_max", qc, 0)), :].bitcast(BF16)[:, 0:CH])\
                        .then_inc(mT_copied[qc], 1)

                def max_parts(i, qc):
                    tiles = slice(qc * CT, (qc + 1) * CT)
                    done = 7 * i + 3 * qc
                    dve.wait_ge(reduced, NM * i + (NM if qc else NM0))
                    if qc:
                        dve.tensor_tensor(m_neg[:, tiles, :], m_neg[:, tiles, :], m_neg_late[:, :, :], ALU.min)\
                            .then_inc(m_step, 1)
                        done += 1
                        dve.wait_ge(m_step, done)
                    wait_count(dve, mT_ready[qc], i)
                    dve.tensor_copy(m_parts[:, tiles, 0, :], m_neg[:, tiles, :]).then_inc(m_step, 1)
                    dve.wait_ge(m_step, done + 1)
                    dve.tensor_tensor(m_rest[:, tiles, :], m_neg[:, tiles, :], m_parts[:, tiles, 0, :],
                                      ALU.subtract).then_inc(m_step, 1)
                    dve.wait_ge(m_step, done + 2)
                    dve.tensor_copy(m_parts[:, tiles, 1, :], m_rest[:, tiles, :]).then_inc(m_step, 1)
                    dve.wait_ge(m_step, done + 3)
                    dve.tensor_tensor(m_parts[:, tiles, 2, :], m_rest[:, tiles, :], m_parts[:, tiles, 1, :],
                                      ALU.subtract).then_inc(m_ready[qc], 1)

                def normalise(i, qc):
                    o = ps[:, ring_bank(("turn_out", qc, 0)), :].rearrange("p (t h e) -> p t h e", t=CT, e=32)
                    dve.wait_ge(oT_ready, 2 * i + qc + 1)
                    wait_count(dve, a_written, 2 * i + qc)
                    dve.reciprocal(recip[:, :, :], o[:, :, :, DK]).then_inc(recip_ready, 1)
                    dve.wait_ge(recip_ready, 2 * i + qc + 1)
                    dve.tensor_tensor(a_all[:, bass.ds(i, 1), qc * CT:(qc + 1) * CT, :]
                                      .rearrange("p a t (h e) -> p (a t) h e", e=DK), o[:, :, :, 0:DK],
                                      recip[:, :, :].unsqueeze(3).broadcast_to((P, CT, GH, DK)), ALU.mult)\
                        .then_inc(a_written, 1)

                def step(i, first=False, last=False):
                    max_parts(i, 1)
                    for item in ORDER:
                        what, n, _ = item
                        if item not in RING_USERS or not present(item, first, last):
                            continue
                        if what == "max":
                            maximum(i + 1, n)
                            if n == NM0 - 1:
                                max_parts(i + 1, 0)
                        elif what == "turn_max":
                            copy_max(i + 1 - n, n)
                        else:
                            normalise(i - n, n)

                for r in range(STACKS):
                    dve.memset(ks[r][KS:KM], 1.0).then_inc(ones_ready, 1)
                for n in range(NM):
                    maximum(0, n)
                    if n == NM0 - 1:
                        max_parts(0, 0)
                copy_max(0, 0)
                step(0, first=True)
                with dve.Fori(1, STEPS - 1) as i:
                    step(i)
                step(STEPS - 1, last=True)
                normalise(STEPS - 1, 1)

            @blk.tensor
            def _(pe):
                pe.wait_ge(ones_ready, 2 * STACKS)

                def scores(i, r, u, pair):
                    qc, kt = UNITS[u]
                    off = CH - unit_width(u)
                    if pair == 0 and kt == 0:
                        pe.wait_ge(m_loaded[qc], 48 * i + 48)
                    wait_count(pe, exp_done, 2 * (NU * i + u) + pair - 1)
                    for h in (2 * pair, 2 * pair + 1):
                        mm = pe.matmul(ps[:, SCORE_BANK + h, off:CH], ks[r][0:KM, h, kt * P:(kt + 1) * P],
                                       qs[r][0:KM, h, qc * CH + off:(qc + 1) * CH], start=True, stop=True)
                    mm.then_inc(score_ready, 1)

                def weigh(i, r, u):
                    qc, kt = UNITS[u]
                    off = CH - unit_width(u)
                    s = (u % PSLOTS) * GH
                    if u in DIAG:
                        pe.wait_ge(masked, len(DIAG) * i + DIAG.index(u) + 1)
                    else:
                        pe.wait_ge(exp_done, 2 * (NU * i + u) + 2)
                    if kt == 0:
                        wait_count(pe, o_copied, 2 * i + qc)
                    for h in range(GH):
                        mm = pe.matmul(ps[32 * h:32 * h + 32, OUT_BANK, off:CH], vg[r][:, kt, h, :],
                                       probs[:, s + h, off:CH], start=(kt == 0), stop=(kt == CT * (qc + 1) - 1))
                    mm.then_inc(pv_done, 1)

                def ring_free(i, item, first, last, second=False):
                    before, ago = ring_before(item, first, last, second)
                    if before is None:
                        return
                    what, n, _ = before
                    if what == "max":
                        wait_count(pe, reduced, NM * (i + 1 - ago) + n + 1)
                    elif what == "turn_max":
                        wait_count(pe, mT_copied[n], i + 2 - n - ago)
                    else:
                        wait_count(pe, a_written, 2 * (i - ago) + (1 if n == 0 else 0))

                def maximum(i, r, n):
                    qt, h0, heads, half, w = MAXES[n]
                    bank = ring_bank(("max", n, 0))
                    for m in range(heads):
                        dst = ps[:, bank, m * w:(m + 1) * w]
                        diag = half == qt // CT
                        mm = pe.matmul(dst, qs[r][0:KS, h0 + m, qt * P:(qt + 1) * P],
                                       ks[r][0:KS, h0 + m, half * CH:half * CH + w], start=True, stop=not diag)
                        if diag:
                            mm = pe.matmul(dst[:, w - P:w], ident_b[:, :], mask_b[:, :], start=False, stop=True)
                    mm.then_inc(score_max_ready, 1)

                def turn_max(i, qc):
                    pe.wait_ge(m_ready[qc], i + 1)
                    dst = ps[0:3 * GH, ring_bank(("turn_max", qc, 0)), :].bitcast(BF16)
                    for t in range(CT):
                        mm = pe.transpose(dst[:, t * P:(t + 1) * P],
                                          m_parts[:, qc * CT + t].rearrange("p r h -> p (r h)"), ident_b[:, :])
                    mm.then_inc(mT_ready[qc], 1)

                def turn_out(i, qc):
                    pe.wait_ge(o_copied, 2 * i + qc + 1)
                    for t in range(CT):
                        mm = pe.transpose(ps[:, ring_bank(("turn_out", qc, 0)), t * P:(t + 1) * P],
                                          oT[qc][:, t * P:(t + 1) * P], ident[:, :])
                    mm.then_inc(oT_ready, 1)

                def step(i, k3, r, first=False, last=False, second=False):
                    pe.wait_ge(vg_ready, i + 1)
                    if not last:
                        pe.wait_ge(stack_loaded[(r + 1) % STACKS], 192 * (k3 + (r + 1) // STACKS) + 192)
                    for item in ORDER:
                        what, n, pair = item
                        if what == "scores":
                            scores(i, r, n, pair)
                        elif what == "weigh":
                            if n >= 0:
                                weigh(i, r, n)
                            elif not first:
                                weigh(i - 1, (r - 1) % STACKS, NU - 1)
                        elif present(item, first, last):
                            ring_free(i, item, first, last, second)
                            if what == "max":
                                maximum(i + 1, (r + 1) % STACKS, n)
                            elif what == "turn_max":
                                turn_max(i + 1 - n, n)
                            else:
                                turn_out(i - n, n)

                pe.wait_ge(stack_loaded[0], 192)
                for n in range(NM):
                    ring_free(-1, ("max", n, 0), None, False)
                    maximum(0, 0, n)
                pe.wait_ge(reduced, NM)
                turn_max(0, 0)
                pe.wait_ge(mT_copied[0], 1)
                step(0, 0, 0, first=True)
                step(1, 0, 1, second=True)
                with pe.Fori(0, 4) as j:
                    for q in range(STACKS):
                        step(STACKS * j + q + 2, j + (q + 2) // STACKS, (q + 2) % STACKS)
                step(14, 4, 14 % STACKS)
                step(15, 5, 15 % STACKS, last=True)
                weigh(STEPS - 1, 15 % STACKS, NU - 1)
                pe.wait_ge(a_written, 2 * STEPS - 1)
                turn_out(STEPS - 1, 1)

        scores_all = sb("scores_all", [P, TILES, E], F32)
        chosen = sb("chosen", [P, TOPK, TILES], F32)
        weight = sb("weight", [P, TOPK, TILES], F32)
        row_of = sb("row_of", [P, TOPK, TILES], U32)
        block_expert = sb("block_expert", [P, SLOT_BLOCKS], U32)

        with ExitStack() as c3:
            attn = [piece(1024 * r, CT, D) for r in range(2)]
            attnT = [piece(2048 + 1024 * r, DC, CH) for r in range(2)]
            xr = [piece(4096 + 1024 * r, CT, D) for r in range(2)]
            res = [piece(6144 + 1024 * r, CT, D) for r in range(2)]
            yT = [c3.enter_context(nc.sbuf_tensor(f"yT{r}", [P, DC, CH], F32)) for r in range(2)]
            stats = c3.enter_context(nc.sbuf_tensor("stats", [P, CT, 6], F32))
            moments = [c3.enter_context(nc.sbuf_tensor(f"moments{r}", [P, CT, 2], F32)) for r in range(2)]
            rstd = [c3.enter_context(nc.sbuf_tensor(f"rstd{r}", [P, CT], F32)) for r in range(2)]
            enl = c3.enter_context(nc.sbuf_tensor("enl", [P, CT, E], F32))
            biased = c3.enter_context(nc.sbuf_tensor("biased", [P, CT, E], F32))
            top = c3.enter_context(nc.sbuf_tensor("top", [P, CT, 8], F32))
            top_at = c3.enter_context(nc.sbuf_tensor("top_at", [P, CT, 8], U32))
            wgu_loaded = sem("wgu_loaded")
            x_loaded = [sem(f"x_loaded{r}") for r in range(2)]
            xb_ready = sem("xb_ready")
            attn_ready = sem("attn_ready")
            aT_ready = sem("aT_ready")
            aT_copied = sem("aT_copied")
            wo_ready = sem("wo_ready")
            res_ready = sem("res_ready")
            stats_ready = sem("stats_ready")
            moments_ready = sem("moments_ready")
            rstd_step = sem("rstd_step")
            rstd_ready = sem("rstd_ready")
            y_ready = sem("y_ready")
            y_saved = sem("y_saved")
            yT_saved = sem("yT_saved")
            yT_ready = sem("yT_ready")
            yT_copied = sem("yT_copied")
            logit_ready = sem("logit_ready")
            enl_ready = sem("enl_ready")
            route_step = sem("route_step")
            x_v = x.rearrange("b (t p) d -> p (b t) d", p=P)
            RS = 4 + 2 * CT
            blk = c3.enter_context(nc.Block())

            @blk.sync
            def _(sp):
                def load(c, b, r):
                    wait_count(sp, res_ready, c - 1)
                    sp.dma_start(xr[r], x_v[:, bass.ds(c * CT, CT), :]).then_inc(x_loaded[r], 16)

                staggered(sp, [(0, load)], CHUNKS)

            @blk.gpsimd
            def _(pool):
                def add_bias(c, b, r):
                    pool.wait_ge(x_loaded[r], 16 * b + 16)
                    pool.tensor_tensor(xr[r], xr[r], bo_all[:, :].unsqueeze(1).broadcast_to((P, CT, D)),
                                       ALU.add).then_inc(xb_ready, 1)

                def deviation(c, b, r):
                    wait_apart(pool, moments_ready, CT * c + CT, pool_waited)
                    pool.tensor_scalar(rstd[r][:, :], moments[r][:, :, 1], EPS, None, ALU.add).then_inc(rstd_step, 1)
                    pool.wait_ge(rstd_step, c + 1)
                    pool.tensor_tensor(rstd[r][:, :], rstd[r][:, :], minus_half[:, :], ALU.pow)\
                        .then_inc(rstd_ready, 1)

                staggered(pool, [(0, add_bias), (1, deviation)], CHUNKS)

            @blk.scalar
            def _(act):
                act.dma_start(wgu[:, :, :, :].rearrange("p e c n -> p (e c) n"),
                              gu_w.rearrange("e (c p) n -> p (e c) n", p=P)).then_inc(wgu_loaded, 16)

                def gather_heads(c, b, r):
                    wait_count(act, aT_ready, c - 1)
                    act.activation(attn[r].rearrange("p t (g e) -> p t g e", g=GROUPS),
                                   a_all[:, bass.ds(b * GROUPS, GROUPS), r * CT:(r + 1) * CT, :]
                                   .rearrange("p g t e -> p t g e"), ACT.Copy).then_inc(attn_ready, 1)

                def copy_attn(c, b, r):
                    act.wait_ge(aT_ready, c + 1)
                    wait_count(act, wo_ready, 2 * c - 2)
                    act.activation(attnT[r], ps[:, 0:2, :], ACT.Copy).then_inc(aT_copied, 1)

                def save_y(c, b, r):
                    act.wait_ge(y_ready, c + 1)
                    act.activation(y_all[:, bass.ds(c * CT, CT), :], res[r], ACT.Copy).then_inc(y_saved, 1)

                def copy_y(c, b, r):
                    act.wait_ge(yT_ready, c + 1)
                    wait_count(act, logit_ready, c - 1)
                    act.activation(yT[r][:, :, :], ps[:, 4:6, :], ACT.Copy).then_inc(yT_copied, 1)
                    act.wait_ge(yT_copied, c + 1)
                    act.activation(yT_all[:, :, bass.ds(c * CH, CH)], yT[r][:, :, :], ACT.Copy).then_inc(yT_saved, 1)

                def exp(c, b, r):
                    act.wait_ge(logit_ready, c + 1)
                    wait_count(act, route_step, RS * (c - 1) + 1)
                    act.activation(enl[:, :, :], ps[:, 6, 0:CT * E].rearrange("p (t e) -> p t e", e=E), ACT.Exp,
                                   scale=-1.0).then_inc(enl_ready, 1)

                staggered(act, [(0, gather_heads), (0, copy_attn), (2, save_y), (2, copy_y), (3, exp)], CHUNKS)
                act.wait_ge(wgu_loaded, 16)

            @blk.vector
            def _(dve):
                def residual(c, b, r):
                    wait_count(dve, yT_ready, c - 1)
                    wait_count(dve, y_saved, c - 1)
                    dve.wait_ge(xb_ready, c + 1)
                    for i in range(2):
                        dve.wait_ge(wo_ready, 2 * c + i + 1)
                        ins = dve.tensor_tensor(res[r][:, 2 * i:2 * i + 2, :],
                                                ps[:, 2 + i, :].rearrange("p (t d) -> p t d", d=D),
                                                xr[r][:, 2 * i:2 * i + 2, :], ALU.add)
                    ins.then_inc(res_ready, 1)
                    dve.wait_ge(res_ready, c + 1)
                    for t in range(CT):
                        dve.bn_stats(stats[:, t, :], res[r][:, t, :]).then_inc(stats_ready, 1)
                    wait_apart(dve, stats_ready, CT * c + CT, dve_waited)
                    for t in range(CT):
                        dve.bn_aggr(moments[r][:, t, :], stats[:, t, :]).then_inc(moments_ready, 1)

                def norm(c, b, r):
                    dve.wait_ge(rstd_ready, c + 1)
                    for t in range(CT):
                        ins = dve.tensor_scalar(res[r][:, t, :], res[r][:, t, :],
                                                moments[r][:, t, 0:1], rstd[r][:, t:t + 1], ALU.subtract, ALU.mult)
                    ins.then_inc(y_ready, 1)

                def route(c, b, r):
                    tiles = bass.ds(c * CT, CT)
                    dve.wait_ge(enl_ready, c + 1)
                    dve.tensor_scalar(biased[:, :, :], enl[:, :, :], 1.0, None, ALU.add).then_inc(route_step, 1)
                    dve.wait_ge(route_step, RS * c + 1)
                    dve.reciprocal(scores_all[:, tiles, :], biased[:, :, :]).then_inc(route_step, 1)
                    dve.wait_ge(route_step, RS * c + 2)
                    dve.tensor_tensor(biased[:, :, :], scores_all[:, tiles, :],
                                      ebias[:, :].unsqueeze(1).broadcast_to((P, CT, E)), ALU.add)\
                        .then_inc(route_step, 1)
                    wait_apart(dve, route_step, RS * c + 3, dve_waited)
                    for t in range(CT):
                        dve.max(top[:, t, :], biased[:, t, :]).then_inc(route_step, 1)
                    wait_apart(dve, route_step, RS * c + 3 + CT, dve_waited)
                    for t in range(CT):
                        dve.max_index(top_at[:, t, :], top[:, t, :], biased[:, t, :]).then_inc(route_step, 1)
                    dve.wait_ge(route_step, RS * c + 3 + 2 * CT)
                    dve.tensor_copy(chosen[:, :, tiles].rearrange("p j t -> p t j"), top_at[:, :, 0:TOPK])\
                        .then_inc(route_step, 1)

                staggered(dve, [(1, norm), (0, residual), (3, route)], CHUNKS)

            @blk.tensor
            def _(pe):
                def turn_attn(c, b, r):
                    pe.wait_ge(attn_ready, c + 1)
                    wait_count(pe, aT_copied, c)
                    for h in range(DC):
                        for t in range(CT):
                            mm = pe.transpose(ps[:, h, t * P:(t + 1) * P], attn[r][:, t, h * P:(h + 1) * P],
                                              ident[:, :])
                    mm.then_inc(aT_ready, 1)

                def project(c, b, r):
                    pe.wait_ge(aT_copied, c + 1)
                    wait_count(pe, res_ready, c)
                    for i in range(2):
                        for t in (2 * i, 2 * i + 1):
                            for h in range(DC):
                                mm = pe.matmul(ps[:, 2 + i, (t % 2) * D:(t % 2 + 1) * D],
                                               attnT[r][:, h, t * P:(t + 1) * P], wo[:, h, :],
                                               start=(h == 0), stop=(h == DC - 1))
                        mm.then_inc(wo_ready, 1)

                def turn_y(c, b, r):
                    pe.wait_ge(y_ready, c + 1)
                    wait_count(pe, yT_copied, c)
                    for h in range(DC):
                        for t in range(CT):
                            mm = pe.transpose(ps[:, 4 + h, t * P:(t + 1) * P], res[r][:, t, h * P:(h + 1) * P],
                                              ident[:, :])
                    mm.then_inc(yT_ready, 1)

                def logits(c, b, r):
                    pe.wait_ge(yT_copied, c + 1)
                    wait_count(pe, enl_ready, c)
                    for t in range(CT):
                        for h in range(DC):
                            mm = pe.matmul(ps[:, 6, t * E:(t + 1) * E], yT[r][:, h, t * P:(t + 1) * P], gate[:, h, :],
                                           start=(h == 0), stop=(h == DC - 1))
                    mm.then_inc(logit_ready, 1)

                staggered(pe, [(0, turn_attn), (2, turn_y), (0, project), (2, logits)], CHUNKS)

        with ExitStack() as c4:
            gact = [piece(512 * r, CH) for r in range(2)]
            hid = [piece(1024 + 512 * r, CH) for r in range(2)]
            pick = [piece(2048 + 512 * j, TILES, E) for j in range(TOPK)]
            prod = [piece(3072 + 512 * j, TILES, E) for j in range(TOPK)]
            run = [piece(4096 + 512 * j, TILES, E) for j in range(2)]
            base = piece(5120, TILES, E)
            over = piece(5632, SLOT_BLOCKS, E)
            iota_blk = piece(6912, SLOT_BLOCKS)
            before_blk = piece(6992, SLOT_BLOCKS)
            cnt = [piece(7080 + 16 * j, E) for j in range(8)]
            cnt_i = [piece(7300 + 16 * j, E).bitcast(I32) for j in range(2)]
            row_f = piece(7400, TOPK, TILES)
            top_s = piece(7464, TOPK, TILES)
            sum_s = piece(7528, TILES)
            pick_b = c4.enter_context(nc.sbuf_tensor("pick_b", [P, TILES, E], BF16))
            iota_ready = sem("iota_ready")
            picked = sem("picked")
            counted = sem("counted")
            chain = sem("chain")
            rows_ready = sem("rows_ready")
            scattered = sem("scattered")
            gate_ready = sem("gate_ready")
            up_ready = sem("up_ready")
            gact_ready = sem("gact_ready")
            hid_ready = sem("hid_ready")
            down_ready = sem("down_ready")
            shared_done = sem("shared_done")
            blk = c4.enter_context(nc.Block())

            @blk.gpsimd
            def _(pool):
                pool.iota(iota_blk, [[1, SLOT_BLOCKS]], base=0, channel_multiplier=0,
                          allow_small_or_imprecise_dtypes=True).then_inc(iota_ready, 1)
                pool.wait_ge(rows_ready, 1)
                for t in range(TILES):
                    for j in range(TOPK):
                        pool.indirect_dma_start(
                            out=y_sorted, out_offset=bass.IndirectOffsetOnAxis(ap=row_of[:, j, t:t + 1], axis=0),
                            in_=y_all[:, t, :], in_offset=None).then_inc(scattered, 16)
                pool.wait_ge(scattered, 16 * TOPK * TILES)

            @blk.scalar
            def _(act):
                with act.Fori(0, B) as b:
                    for r in range(2):
                        act.wait_ge(gate_ready, 2 * b + r + 1)
                        act.wait_ge(hid_ready, 2 * b + r)
                        act.activation(gact[r], ps[:, 2 + 2 * r, :], ACT.Silu).then_inc(gact_ready, 1)

            @blk.vector
            def _(dve):
                n = [0]

                def link(ins):
                    n[0] += 1
                    ins.then_inc(chain, 1)
                    dve.wait_ge(chain, n[0])

                ie = iota_e[:, :].unsqueeze(1).broadcast_to((P, TILES, E))
                for j in range(TOPK):
                    link(dve.tensor_tensor(pick[j], ie, chosen[:, j, :].unsqueeze(2).broadcast_to((P, TILES, E)),
                                           ALU.is_equal))
                dve.tensor_tensor(pick_b[:, :, :], pick[0], pick[1], ALU.add).then_inc(picked, 1)
                for j in range(TOPK):
                    link(dve.tensor_tensor(prod[j], pick[j], scores_all[:, :, :], ALU.mult))
                    link(dve.tensor_reduce(top_s[:, j, :], prod[j], AX.X, ALU.add))
                link(dve.tensor_tensor(sum_s, top_s[:, 0, :], top_s[:, 1, :], ALU.add))
                link(dve.tensor_scalar(sum_s, sum_s, 1e-20, None, ALU.add))
                link(dve.reciprocal(sum_s, sum_s))
                link(dve.tensor_tensor(weight[:, :, :], top_s, sum_s.unsqueeze(1).broadcast_to((P, TOPK, TILES)),
                                       ALU.mult))
                dve.wait_ge(counted, 1)
                link(dve.tensor_copy(run[0], ps[:, 1, :].rearrange("p (t e) -> p t e", e=E)))
                at, s = 0, 1
                while s < TILES:
                    dve.tensor_copy(run[1 - at][:, 0:s, :], run[at][:, 0:s, :]).then_inc(chain, 1)
                    n[0] += 1
                    link(dve.tensor_tensor(run[1 - at][:, s:TILES, :], run[at][:, s:TILES, :],
                                           run[at][:, 0:TILES - s, :], ALU.add))
                    at, s = 1 - at, 2 * s
                total = run[at][:, TILES - 1, :]
                link(dve.tensor_scalar(cnt_i[0], total, float(P - 1), None, ALU.add))
                link(dve.tensor_scalar(cnt_i[1], cnt_i[0], P.bit_length() - 1, None, ALU.arith_shift_right))
                link(dve.tensor_copy(cnt[0], cnt_i[1]))
                link(dve.tensor_copy(cnt[1], cnt[0]))
                a, s = 1, 1
                while s < E:
                    dve.tensor_copy(cnt[a + 1][:, 0:s], cnt[a][:, 0:s]).then_inc(chain, 1)
                    n[0] += 1
                    link(dve.tensor_tensor(cnt[a + 1][:, s:E], cnt[a][:, s:E], cnt[a][:, 0:E - s], ALU.add))
                    a, s = a + 1, 2 * s
                ends, first = cnt[a], cnt[a + 1]
                link(dve.tensor_tensor(first, ends, cnt[0], ALU.subtract))
                link(dve.tensor_scalar(first, first, float(P), None, ALU.mult))
                link(dve.tensor_tensor(base, run[at], ps[:, 1, :].rearrange("p (t e) -> p t e", e=E), ALU.subtract))
                link(dve.tensor_tensor(base, base, ps[:, 0, :].rearrange("p (t e) -> p t e", e=E), ALU.add))
                link(dve.tensor_tensor(base, base, first.unsqueeze(1).broadcast_to((P, TILES, E)), ALU.add))
                for j in range(TOPK):
                    link(dve.tensor_tensor(prod[j], pick[j], base, ALU.mult))
                    link(dve.tensor_reduce(row_f[:, j, :], prod[j], AX.X, ALU.add))
                dve.tensor_copy(row_of[:, :, :], row_f).then_inc(rows_ready, 1)
                dve.wait_ge(iota_ready, 1)
                link(dve.tensor_tensor(over, iota_blk.unsqueeze(2).broadcast_to((P, SLOT_BLOCKS, E)),
                                       ends.unsqueeze(1).broadcast_to((P, SLOT_BLOCKS, E)), ALU.is_ge))
                link(dve.tensor_reduce(before_blk, over, AX.X, ALU.add))
                link(dve.tensor_scalar(before_blk, before_blk, float(E - 1), None, ALU.min))
                link(dve.tensor_copy(block_expert[:, :], before_blk))

                with dve.Fori(0, B) as b:
                    for r in range(2):
                        c = 2 * b + r
                        dve.wait_ge(gact_ready, c + 1)
                        dve.wait_ge(up_ready, c + 1)
                        dve.wait_ge(down_ready, 2 * b * 2)
                        dve.tensor_tensor(hid[r], gact[r], ps[:, 3 + 2 * r, :], ALU.mult).then_inc(hid_ready, 1)
                        for i in range(2):
                            dve.wait_ge(down_ready, 2 * c + i + 1)
                            tiles = bass.ds(c * CT + 2 * i, 2)
                            dve.tensor_tensor(sh_all[:, tiles, :], y_all[:, tiles, :],
                                              ps[:, 6 + i, :].rearrange("p (t d) -> p t d", d=D),
                                              ALU.add).then_inc(shared_done, 1)

            @blk.tensor
            def _(pe):
                pe.wait_ge(picked, 1)
                pb = pick_b[:, :, :].rearrange("p t e -> p (t e)")
                pe.matmul(ps[:, 0, :], before_b[:, :], pb, start=True, stop=True)
                pe.matmul(ps[:, 1, :], ones_b[:, :], pb, start=True, stop=True).then_inc(counted, 1)
                with pe.Fori(0, B) as b:
                    for r in range(2):
                        c = 2 * b + r
                        pe.wait_ge(hid_ready, 2 * b)
                        for w, bank, s in ((wsg, 2 + 2 * r, gate_ready), (wsu, 3 + 2 * r, up_ready)):
                            for h in range(DC):
                                mm = pe.matmul(ps[:, bank, :], w[:, h, :], yT_all[:, h, bass.ds(c * CH, CH)],
                                               start=(h == 0), stop=(h == DC - 1))
                            mm.then_inc(s, 1)
                        pe.wait_ge(hid_ready, c + 1)
                        for i in range(2):
                            pe.wait_ge(shared_done, 2 * c)
                            for t in (2 * i, 2 * i + 1):
                                mm = pe.matmul(ps[:, 6 + i, (t % 2) * D:(t % 2 + 1) * D],
                                               hid[r][:, t * P:(t + 1) * P], wsd[:, :], start=True, stop=True)
                            mm.then_inc(down_ready, 1)

        with ExitStack() as c5:
            ys = [piece(512 * r, 2, D) for r in range(2)]
            ysT = [work[:, 1024 + 512 * r:1536 + 512 * r].rearrange("p (h k t) -> p h k t", h=DC, k=2)
                   for r in range(2)]
            gx = [piece(2048 + 256 * r, 2, F) for r in range(2)]
            hx = [piece(2560 + 256 * r, 2, F) for r in range(2)]
            hxT = [piece(3072 + 256 * r, 2, P) for r in range(2)]
            zs = [piece(3584 + 512 * r, 2, D) for r in range(2)]
            ys_loaded = [sem(f"ys_loaded{r}") for r in range(2)]
            z_stored = [sem(f"z_stored{r}") for r in range(2)]
            ysT_ready = sem("ysT_ready")
            ysT_copied = sem("ysT_copied")
            gu_ready = sem("gu_ready")
            gx_ready = sem("gx_ready")
            hx_ready = sem("hx_ready")
            hxT_ready = sem("hxT_ready")
            hxT_copied = sem("hxT_copied")
            z_ready = sem("z_ready")
            z_copied = sem("z_copied")
            y_rows = y_sorted.rearrange("(n p) d -> p n d", p=P)
            z_rows = z_sorted.rearrange("(n p) d -> p n d", p=P)
            blk = c5.enter_context(nc.Block())

            @blk.sync
            def _(sp):
                def load(n, k2, r):
                    wait_count(sp, ysT_ready, n - 1)
                    sp.dma_start(ys[r], y_rows[:, bass.ds(2 * n, 2), :]).then_inc(ys_loaded[r], 16)

                staggered(sp, [(0, load)], PAIRS)

            @blk.gpsimd
            def _(pool):
                with pool.Fori(0, PAIRS // 2) as j:
                    for r in range(2):
                        pool.wait_ge(z_copied, 2 * j + r + 1)
                        pool.dma_start(z_rows[:, bass.ds(4 * j + 2 * r, 2), :], zs[r]).then_inc(z_stored[r], 16)
                for r in range(2):
                    pool.wait_ge(z_stored[r], 16 * (PAIRS // 2))

            @blk.scalar
            def _(act):
                def turned(n, k2, r):
                    act.wait_ge(ysT_ready, n + 1)
                    wait_count(act, gu_ready, n - 1)
                    act.activation(ysT[r].rearrange("p h k t -> p (h k t)"), ps[:, r, :], ACT.Copy)\
                        .then_inc(ysT_copied, 1)

                def silu(n, k2, r):
                    act.wait_ge(gu_ready, n + 1)
                    wait_count(act, hx_ready, n - 1)
                    act.activation(gx[r], ps[:, 2 + r, :].rearrange("p (k c) -> p k c", k=2)[:, :, 0:F], ACT.Silu)\
                        .then_inc(gx_ready, 1)

                staggered(act, [(0, turned), (1, silu)], PAIRS)

            @blk.vector
            def _(dve):
                def hidden(n, k2, r):
                    dve.wait_ge(gx_ready, n + 1)
                    wait_count(dve, hxT_ready, n - 1)
                    dve.tensor_tensor(hx[r], gx[r], ps[:, 2 + r, :].rearrange("p (k c) -> p k c", k=2)[:, :, F:2 * F],
                                      ALU.mult).then_inc(hx_ready, 1)

                def turned(n, k2, r):
                    dve.wait_ge(hxT_ready, n + 1)
                    wait_count(dve, z_ready, n - 1)
                    dve.tensor_copy(hxT[r], ps[:, 4 + r, 0:2 * P].rearrange("p (k t) -> p k t", k=2))\
                        .then_inc(hxT_copied, 1)

                def result(n, k2, r):
                    dve.wait_ge(z_ready, n + 1)
                    wait_count(dve, z_stored[r], 16 * k2)
                    dve.tensor_copy(zs[r], ps[:, 6 + r, :].rearrange("p (k d) -> p k d", k=2)).then_inc(z_copied, 1)

                staggered(dve, [(0, hidden), (1, turned), (2, result)], PAIRS)

            @blk.tensor
            def _(pe):
                picks = {}

                def experts(n, what):
                    _, picks[what] = nc.values_load_multi_w_load_instructions(
                        block_expert[0:1, bass.ds(2 * n, 2)], engines=[mybir.EngineType.PE], min_val=0, max_val=E - 1,
                        skip_runtime_bounds_check_because="the experts are clamped to the last one")

                def turn_rows(n, k2, r):
                    pe.wait_ge(ys_loaded[r], 16 * k2 + 16)
                    wait_count(pe, ysT_copied, n - 1)
                    for h in range(DC):
                        for k in range(2):
                            mm = pe.transpose(ps[:, r, (2 * h + k) * P:(2 * h + k + 1) * P],
                                              ys[r][:, k, h * P:(h + 1) * P], ident[:, :])
                    mm.then_inc(ysT_ready, 1)

                def gate_up(n, k2, r):
                    pe.wait_ge(ysT_copied, n + 1)
                    wait_count(pe, hx_ready, n - 1)
                    for k in range(2):
                        e = picks["gate_up"][k]
                        for h in range(DC):
                            mm = pe.matmul(ps[:, 2 + r, 2 * F * k:2 * F * (k + 1)], ysT[r][:, h, k, :],
                                           wgu[:, bass.ds(e, 1), h, :].squeeze(1), start=(h == 0), stop=(h == DC - 1))
                    mm.then_inc(gu_ready, 1)

                def turn_hidden(n, k2, r):
                    pe.wait_ge(hx_ready, n + 1)
                    wait_count(pe, hxT_copied, n - 1)
                    for k in range(2):
                        mm = pe.transpose(ps[:, 4 + r, k * P:(k + 1) * P], hx[r][:, k, :], ident[:, :])
                    mm.then_inc(hxT_ready, 1)

                def down(n, k2, r):
                    pe.wait_ge(hxT_copied, n + 1)
                    wait_count(pe, z_copied, n - 1)
                    for k in range(2):
                        e = picks["down"][k]
                        mm = pe.matmul(ps[:, 6 + r, D * k:D * (k + 1)], hxT[r][:, k, :],
                                       wdn[:, bass.ds(e, 1), :].squeeze(1), start=True, stop=True)
                    mm.then_inc(z_ready, 1)

                staggered(pe, [(1, lambda n, k2, r: experts(n, "gate_up")), (3, lambda n, k2, r: experts(n, "down")),
                               (0, turn_rows), (1, gate_up), (2, turn_hidden), (3, down)], PAIRS)

        with ExitStack() as c6:
            zg = [work[:, 2048 * r:2048 * (r + 1)].rearrange("p (t j d) -> p t j d", t=CT, j=TOPK) for r in range(2)]
            acc = [piece(4096 + 1024 * r, CT, D) for r in range(2)]
            stats = c6.enter_context(nc.sbuf_tensor("stats2", [P, CT, 6], F32))
            moments = c6.enter_context(nc.sbuf_tensor("moments2", [P, CT, 2], F32))
            rstd = c6.enter_context(nc.sbuf_tensor("rstd2", [P, CT], F32))
            gathered = [sem(f"gathered{r}") for r in range(2)]
            first_added = sem("first_added")
            both_added = sem("both_added")
            stats_ready = sem("stats_ready2")
            moments_ready = sem("moments_ready2")
            rstd_step = sem("rstd_step2")
            rstd_ready = sem("rstd_ready2")
            out_ready = sem("out_ready")
            out_stored = [sem(f"out_stored{r}") for r in range(2)]
            o_v = out.rearrange("b (t p) d -> p (b t) d", p=P)
            blk = c6.enter_context(nc.Block())

            @blk.gpsimd
            def _(pool):
                def gather(c):
                    wait_count(pool, both_added, CT * (c - 1))
                    for t in range(CT):
                        for j in range(TOPK):
                            pool.indirect_dma_start(
                                out=zg[c % 2][:, t, j, :], out_offset=None, in_=z_sorted,
                                in_offset=bass.IndirectOffsetOnAxis(ap=row_of[:, j, c * CT + t:c * CT + t + 1], axis=0))\
                                .then_inc(gathered[c % 2], 16)

                gather(0)
                for c in range(2 * B):
                    if c + 1 < 2 * B:
                        gather(c + 1)
                    wait_apart(pool, moments_ready, CT * c + CT, pool_waited)
                    pool.tensor_scalar(rstd[:, :], moments[:, :, 1], EPS, None, ALU.add).then_inc(rstd_step, 1)
                    pool.wait_ge(rstd_step, c + 1)
                    pool.tensor_tensor(rstd[:, :], rstd[:, :], minus_half[:, :], ALU.pow).then_inc(rstd_ready, 1)

            @blk.vector
            def _(dve):
                with dve.Fori(0, B) as b:
                    for r in range(2):
                        c = 2 * b + r
                        dve.wait_ge(gathered[r], 16 * TOPK * CT * b + 16 * TOPK * CT)
                        dve.wait_ge(out_stored[r], 16 * b)
                        for t in range(CT):
                            dve.scalar_tensor_tensor(acc[r][:, t, :], zg[r][:, t, 0, :],
                                                     weight[:, 0, bass.ds(c * CT + t, 1)],
                                                     sh_all[:, bass.ds(c * CT + t, 1), :].squeeze(1), ALU.mult, ALU.add)\
                                .then_inc(first_added, 1)
                        for t in range(CT):
                            dve.wait_ge(first_added, CT * c + t + 1)
                            dve.scalar_tensor_tensor(acc[r][:, t, :], zg[r][:, t, 1, :],
                                                     weight[:, 1, bass.ds(c * CT + t, 1)],
                                                     acc[r][:, t, :], ALU.mult, ALU.add).then_inc(both_added, 1)
                        for t in range(CT):
                            dve.wait_ge(both_added, CT * c + t + 1)
                            dve.bn_stats(stats[:, t, :], acc[r][:, t, :]).then_inc(stats_ready, 1)
                        for t in range(CT):
                            wait_apart(dve, stats_ready, CT * c + t + 1, dve_waited)
                            dve.bn_aggr(moments[:, t, :], stats[:, t, :]).then_inc(moments_ready, 1)
                        dve.wait_ge(rstd_ready, c + 1)
                        for t in range(CT):
                            ins = dve.tensor_scalar(acc[r][:, t, :], acc[r][:, t, :], moments[:, t, 0:1],
                                                    rstd[:, t:t + 1], ALU.subtract, ALU.mult)
                        ins.then_inc(out_ready, 1)

            @blk.sync
            def _(sp):
                with sp.Fori(0, B) as b:
                    for r in range(2):
                        sp.wait_ge(out_ready, 2 * b + r + 1)
                        sp.dma_start(o_v[:, bass.ds(b * NT + r * CT, CT), :], acc[r]).then_inc(out_stored[r], 16)
                for r in range(2):
                    sp.wait_ge(out_stored[r], 16 * B)


_INS = ["x", "xT", "Wq", "bq", "Wk", "bk", "Wv", "bv", "Wo", "bo", "gate_w", "expert_bias", "sg_w", "su_w", "sd_w",
        "gu_w", "down_w"]


def kernel(**inputs):
    import numpy as _np
    import concourse.bacc as _bacc
    from concourse import mybir as _mybir
    from concourse.bass_utils import run_bass_kernel_spmd as _run

    given = {n: _np.asarray(inputs["L0_attn_" + n]) for n in ("x", "Wq", "bq", "Wk", "bk", "Wv", "bv", "Wo", "bo")}
    for name in ("bq", "bk"):
        given[name] = given[name].reshape(DC, P).T
    given["xT"] = given["x"].reshape(B * N, D).T
    for name, key in (("gate_w", "gate_w"), ("expert_bias", "expert_bias"), ("sg_w", "shared_gate_w"),
                      ("su_w", "shared_up_w"), ("sd_w", "shared_down_w"), ("gu_w", "experts_gate_up"),
                      ("down_w", "experts_down")):
        given[name] = _np.asarray(inputs["L0_ffn_" + key])
    nc = _bacc.Bacc("TRN2", target_bir_lowering=False, num_devices=1)
    arrays, args = {}, []
    for name in _INS:
        a = _np.ascontiguousarray(given[name])
        arrays[f"in_{name}"] = a
        args.append(nc.dram_tensor(f"in_{name}", a.shape, _mybir.dt.from_np(a.dtype), kind="ExternalInput").ap())
    args.append(nc.dram_tensor("out_0", (B, N, D), _mybir.dt.float32, kind="ExternalOutput").ap())
    build(nc, *args)
    r = _run(nc, [arrays], core_ids=[0])
    return r.results[0]["out_0"]
```

```python
from contextlib import ExitStack

import numpy as np
import concourse.bass as bass
from concourse import mybir

F32 = mybir.dt.float32
BF16 = mybir.dt.bfloat16
I32 = mybir.dt.int32
U32 = mybir.dt.uint32
ALU = mybir.AluOpType
ACT = mybir.ActivationFunctionType
AX = mybir.AxisListType

CONSTANTS = 6
P = 128
B, N, D = 4, 1024, 256
H, DK = 16, 16
DC = D // P
GH = 4
GROUPS = H // GH
GW = GH * DK
STEPS = B * GROUPS
CH = 512
HALVES = N // CH
CT = CH // P
NT = N // P
TILES = B * NT
E, F, TOPK = 16, 128, 2
EPS = 1e-5
NEG = -1e30

PRODUCTS = [(0, 0), (0, 1), (1, 0), (0, 2), (2, 0), (1, 1)]
KS = len(PRODUCTS) * DK
KM = KS + 3

UNITS = [(qc, kt) for qc in range(HALVES) for kt in range(CT * (qc + 1))]
NU = len(UNITS)
DIAG = [u for u, (qc, kt) in enumerate(UNITS) if kt >= CT * qc]
PSLOTS = 3
MAXES = []
for qt in range(NT):
    for half in range(qt // CT + 1):
        w = min(CH, (qt + 1) * P - half * CH)
        heads = 4 if w == P else 2 if w == 2 * P else 1
        MAXES += [(qt, h, heads, half, w) for h in range(0, GH, heads)]
NM = len(MAXES)
NM0 = sum(m[0] < CT for m in MAXES)
STACKS = 3
RING = [4, 5, 7]


def unit_width(u):
    qc, kt = UNITS[u]
    return CH - max(0, P * (kt - CT * qc))


def attention_order():
    main = [("scores", 0, 0), ("scores", 0, 1), ("weigh", -1, 0)]
    for u in range(NU - 1):
        main += [("scores", u + 1, 0), ("scores", u + 1, 1), ("weigh", u, 0)]
    cost = [unit_width(u) * (2 if what == "weigh" else 1) for what, u, _ in main]
    pieces = [m[2] * m[4] + 60 for m in MAXES]
    order, n, done, spent = [], 0, 0, 0
    for item, c in zip(main, cost):
        order.append(item)
        if item == ("scores", 1, 1):
            order.append(("turn_max", 1, 0))
        if item == ("weigh", 1, 0):
            order.append(("turn_out", 1, 0))
        if item == ("weigh", 5, 0):
            order.append(("turn_out", 0, 0))
        done += c
        while n < NM and (spent + pieces[n] / 2) / sum(pieces) <= done / sum(cost):
            order.append(("max", n, 0))
            spent += pieces[n]
            n += 1
            if n == NM0 + TURN_AFTER:
                order.append(("turn_max", 0, 0))
    assert n == NM
    return order


TURN_AFTER = 3
ORDER = attention_order()
RING_USERS = [item for item in ORDER if item[0] in ("max", "turn_max", "turn_out")]
assert len(RING_USERS) % len(RING) == 0


def ring_bank(item):
    return RING[RING_USERS.index(item) % len(RING)]


def present(item, first, last):
    if last:
        return item in (("turn_max", 1, 0), ("turn_out", 1, 0), ("turn_out", 0, 0))
    return not (first and item == ("turn_out", 1, 0))


def ring_before(item, first, last, second=False):
    at = RING_USERS.index(item) - len(RING)
    while at >= 0:
        if present(RING_USERS[at], first, last):
            return RING_USERS[at], 0
        at -= len(RING)
    if first:
        return None, 0
    at += len(RING_USERS)
    while not present(RING_USERS[at], second, False):
        at -= len(RING)
    return RING_USERS[at], 1


EARLY = [("max", n) for n in range(NM)]
EARLY.insert(NM0 + TURN_AFTER, ("turn_max", 0))
EARLY_BANKS = [6, 7]
EARLY_CHUNKS = 3


def early_share(c, g):
    slot = (c - (2 * B - EARLY_CHUNKS)) * 6 + g
    if slot < 0:
        return []
    per = len(EARLY) / (6 * EARLY_CHUNKS)
    return list(range(round(slot * per), round((slot + 1) * per)))


SECTIONS = 2
CHUNKS = B * HALVES
SEC_CHUNKS = CHUNKS // SECTIONS
SEC_TILES = TILES // SECTIONS
SEC_BLOCKS = SEC_TILES * TOPK + E
SEC_PAIRS = SEC_BLOCKS // 2
SEC_ROWS = SEC_BLOCKS * P
PAIRS = SECTIONS * SEC_PAIRS
FILLS = 4
ZEROS = 1024
ZSLOTS = 5


def wait_count(eng, sem, value):
    if isinstance(value, int) and value <= 0:
        return
    eng.wait_ge(sem, value)


def wait_apart(eng, sem, value, waited):
    eng.wait_ge(sem, value)
    eng.sem_inc(waited, 1)


def staggered(eng, stages, count, base=0, turns=None, until=None, beside=None):
    lag = max(b for b, _ in stages)

    def turn(t, k2, r):
        for behind, stage in stages:
            if isinstance(t, int) and not base <= t - behind < base + count:
                continue
            stage(t - behind, k2 + (r - behind) // 2, (r - behind) % 2)

    low, high = turns or (base, base + count + lag)
    start = max(base + lag + 2, low)
    start += start % 2
    end = min(base + count, high, until or high) // 2 * 2
    if start >= end:
        start = end = high
    for t in range(low, start):
        turn(t, t // 2, t % 2)
    if start < end:
        with eng.Fori(start // 2, end // 2) as j:
            turn(2 * j, j, 0)
            turn(2 * j + 1, j, 1)
    for t in range(end, high):
        turn(t, t // 2, t % 2)
        if beside is not None:
            beside(t)


def build(nc, x, xT, Wq, bq, Wk, bk, Wv, bv, Wo, bo, gate_w, expert_bias, sg_w, su_w, sd_w, gu_w, down_w, out):
    with ExitStack() as ctx:
        def sb(name, shape, dt):
            return ctx.enter_context(nc.sbuf_tensor(name, shape, dt))

        def sem(name):
            return ctx.enter_context(nc.semaphore(name))

        def dram(name, shape, dt):
            return nc.dram_tensor(name, shape, dt, kind="Internal").ap()

        qk_parts = dram("qk_parts", (2, 3, B * D, N), BF16)
        y_sorted = [dram(f"y_sorted{g}", (SEC_ROWS, D), F32) for g in range(SECTIONS)]
        z_sorted = [dram(f"z_sorted{g}", (SEC_ROWS, D), F32) for g in range(SECTIONS)]

        ps = ctx.enter_context(nc.psum_tensor("ps", [P, 8, CH], F32))

        wqk = sb("wqk", [P, 2, DC, D], F32)
        wv = sb("wv", [P, DC, D], F32)
        wo = sb("wo", [P, DC, D], F32)
        bqk = sb("bqk", [P, 2, DC], F32)
        bv_all = sb("bv_all", [P, D], F32)
        bo_all = sb("bo_all", [P, D], F32)
        gate = sb("gate", [P, DC, E], F32)
        ebias = sb("ebias", [P, E], F32)
        wsg = sb("wsg", [P, DC, F], F32)
        wsu = sb("wsu", [P, DC, F], F32)
        wsd = sb("wsd", [P, D], F32)
        wgu = sb("wgu", [P, E, DC, 2 * F], F32)
        wdn = sb("wdn", [P, E, D], F32)
        ident = sb("ident", [P, P], F32)
        ident_b = sb("ident_b", [P, P], BF16)
        mask_b = sb("mask_b", [P, P], BF16)
        before_b = sb("before_b", [P, P], BF16)
        ones_b = sb("ones_b", [P, P], BF16)
        iota_e = sb("iota_e", [P, E], F32)
        iota_blk = sb("iota_blk", [P, SEC_BLOCKS], F32)
        minus_half = sb("minus_half", [P, CT], F32)
        v_all = sb("v_all", [P, STEPS, NT, GW], F32)
        y_all = v_all[:, :, :, :].rearrange("p a b c -> p (a b c)").rearrange("p (t d) -> p t d", d=D)
        a_all = sb("a_all", [P, STEPS, NT, GW], F32)
        sh_all = a_all[:, :, :, :].rearrange("p a b c -> p (a b c)").rearrange("p (t d) -> p t d", d=D)
        stacks = sb("stacks", [P, 2, 2, GH, N], BF16)
        yT_all = stacks[:, :, :, :, :].rearrange("p a b c d -> p (a b c d)").bitcast(F32) \
            .rearrange("p (c t) -> p c t", c=DC)
        work = sb("work", [P, 8192], F32)

        def piece(at, *dims):
            n = int(np.prod(dims))
            v = work[:, at:at + n]
            if len(dims) == 2:
                v = v.rearrange("p (a b) -> p a b", b=dims[1])
            if len(dims) == 3:
                v = v.rearrange("p (a b c) -> p a b c", b=dims[1], c=dims[2])
            return v

        wqk_loaded = [sem("wq_loaded"), sem("wk_loaded")]
        bqk_loaded = sem("bqk_loaded")
        wv_loaded = sem("wv_loaded")
        bv_loaded = sem("bv_loaded")
        const_ready = sem("const_ready")
        const_zeroed = sem("const_zeroed")
        dve_waited = sem("dve_waited")
        pool_waited = sem("pool_waited")

        third = wgu[:, :, :, :].rearrange("p e c n -> p (e c n)")[:, 0:2 * GH * N // 2].bitcast(BF16) \
            .rearrange("p (s h t) -> p s h t", s=2, h=GH)
        qs = [stacks[:, 0, 0], stacks[:, 1, 0], third[:, 0]]
        ks = [stacks[:, 0, 1], stacks[:, 1, 1], third[:, 1]]
        ones_ready = sem("ones_ready")
        vg_ready = sem("vg_ready")
        stack_loaded = [sem(f"stack_loaded{r}") for r in range(STACKS)]

        def load_stacks(sp, i, r):
            for n, (qp, kp) in enumerate(PRODUCTS):
                for s, (dst, part) in enumerate(((qs, qp), (ks, kp))):
                    sp.dma_start(dst[r][n * DK:(n + 1) * DK],
                                 qk_parts[s, part, bass.ds(i * GW, GW), :]
                                 .rearrange("(h d) t -> d h t", d=DK)).then_inc(stack_loaded[r], 16)

        held = ctx.enter_context(ExitStack())
        vg = [held.enter_context(nc.sbuf_tensor(f"vg{r}", [P, NT, GH, 32], F32)) for r in range(2)]
        vg.append(work[:, 6144:7168].rearrange("p (t h e) -> p t h e", t=NT, h=GH))
        oT = [held.enter_context(nc.sbuf_tensor(f"oT{r}", [P, CH], F32)) for r in range(2)]
        mT = [held.enter_context(nc.sbuf_tensor(f"mT{r}", [3 * GH, CH], BF16)) for r in range(2)]
        recip = held.enter_context(nc.sbuf_tensor("recip", [P, CT, GH], F32))
        m_neg = held.enter_context(nc.sbuf_tensor("m_neg", [P, NT, GH], F32))
        m_neg_late = held.enter_context(nc.sbuf_tensor("m_neg_late", [P, CT, GH], F32))
        m_rest = held.enter_context(nc.sbuf_tensor("m_rest", [P, NT, GH], F32))
        m_parts = held.enter_context(nc.sbuf_tensor("m_parts", [P, NT, 3, GH], BF16))
        m_loaded = [sem(f"m_loaded{r}") for r in range(2)]
        score_max_ready = sem("score_max_ready")
        reduced = sem("reduced")
        m_step = sem("m_step")
        m_ready = [sem(f"m_ready{r}") for r in range(2)]
        mT_ready = [sem(f"mT_ready{r}") for r in range(2)]
        mT_copied = [sem(f"mT_copied{r}") for r in range(2)]

        def values(pool, i, r):
            pool.tensor_copy(vg[r][:, :, :, 0:DK],
                             v_all[:, bass.ds(i, 1)].rearrange("p a t (h e) -> p (a t) h e", e=DK))\
                .then_inc(vg_ready, 1)

        def piece_scores(pe, i, r, n, bank):
            qt, h0, heads, half, w = MAXES[n]
            for m in range(heads):
                dst = ps[:, bank, m * w:(m + 1) * w]
                diag = half == qt // CT
                mm = pe.matmul(dst, qs[r][0:KS, h0 + m, qt * P:(qt + 1) * P],
                               ks[r][0:KS, h0 + m, half * CH:half * CH + w], start=True, stop=not diag)
                if diag:
                    mm = pe.matmul(dst[:, w - P:w], ident_b[:, :], mask_b[:, :], start=False, stop=True)
            mm.then_inc(score_max_ready, 1)

        def turn_maxima(pe, i, qc, bank):
            pe.wait_ge(m_ready[qc], i + 1)
            dst = ps[0:3 * GH, bank, :].bitcast(BF16)
            for t in range(CT):
                mm = pe.transpose(dst[:, t * P:(t + 1) * P],
                                  m_parts[:, qc * CT + t].rearrange("p r h -> p (r h)"), ident_b[:, :])
            mm.then_inc(mT_ready[qc], 1)

        def piece_maximum(dve, i, n, bank):
            qt, h, heads, half, w = MAXES[n]
            dst = m_neg[:, qt, h:h + heads] if half == 0 else m_neg_late[:, qt - CT, h:h + heads]
            dve.wait_ge(score_max_ready, NM * i + n + 1)
            dve.tensor_reduce(dst, ps[:, bank, 0:heads * w].rearrange("p (h k) -> p h k", h=heads), AX.X, ALU.max,
                              negate=True).then_inc(reduced, 1)

        def copy_maxima(dve, i, qc, bank):
            dve.wait_ge(mT_ready[qc], i + 1)
            wait_count(dve, m_loaded[qc], 48 * i)
            dve.tensor_copy(mT[qc][:, :], ps[0:3 * GH, bank, :].bitcast(BF16)[:, 0:CH]).then_inc(mT_copied[qc], 1)

        def max_parts(dve, i, qc):
            tiles = slice(qc * CT, (qc + 1) * CT)
            done = 7 * i + 3 * qc
            dve.wait_ge(reduced, NM * i + (NM if qc else NM0))
            if qc:
                dve.tensor_tensor(m_neg[:, tiles, :], m_neg[:, tiles, :], m_neg_late[:, :, :], ALU.min)\
                    .then_inc(m_step, 1)
                done += 1
                dve.wait_ge(m_step, done)
            wait_count(dve, mT_ready[qc], i)
            dve.tensor_copy(m_parts[:, tiles, 0, :], m_neg[:, tiles, :]).then_inc(m_step, 1)
            dve.wait_ge(m_step, done + 1)
            dve.tensor_tensor(m_rest[:, tiles, :], m_neg[:, tiles, :], m_parts[:, tiles, 0, :],
                              ALU.subtract).then_inc(m_step, 1)
            dve.wait_ge(m_step, done + 2)
            dve.tensor_copy(m_parts[:, tiles, 1, :], m_rest[:, tiles, :]).then_inc(m_step, 1)
            dve.wait_ge(m_step, done + 3)
            dve.tensor_tensor(m_parts[:, tiles, 2, :], m_rest[:, tiles, :], m_parts[:, tiles, 1, :],
                              ALU.subtract).then_inc(m_ready[qc], 1)

        def load_max(sp, i, r, qc):
            sp.wait_ge(mT_copied[qc], i + 1)
            for part in range(3):
                sp.dma_start(qs[r][KS + part:KS + part + 1, :, qc * CH:(qc + 1) * CH],
                             mT[qc][part * GH:(part + 1) * GH, :]).then_inc(m_loaded[qc], 16)

        with ExitStack() as c1:
            xt = [piece(1024 * i, DC, CH) for i in range(2)]
            rest = [piece(2048 + 512 * t, CH) for t in range(4)]
            parts = [piece(4096 + 768 * t, 768).bitcast(BF16).rearrange("p (r t) -> p r t", r=3) for t in range(4)]
            xt_loaded = [sem(f"xt_loaded{i}") for i in range(2)]
            proj_ready = [sem(f"proj_ready{t}") for t in range(4)]
            hi_ready = sem("hi_ready")
            rest_ready = [sem(f"rest_ready{t}") for t in range(4)]
            mid_ready = sem("mid_ready")
            lo_ready = sem("lo_ready")
            stored = [sem(f"stored{t}") for t in range(4)]
            v_ready = [sem(f"v_ready{i}") for i in range(2)]
            v_copied = [sem(f"v_copied{i}") for i in range(2)]
            big_loaded = sem("big_loaded")
            xT_v = xT.rearrange("(c p) t -> p c t", p=P)
            blk = c1.enter_context(nc.Block())

            @blk.sync
            def _(sp):
                def load(c, b, half):
                    wait_count(sp, v_ready[1], c - 1)
                    sp.dma_start(xt[half], xT_v[:, :, bass.ds(c * CH, CH)]).then_inc(xt_loaded[half], 16)

                def store(c, b, half):
                    for t in range(4):
                        sp.wait_ge(lo_ready, c * 4 + t + 1)
                        sp.dma_start(
                            qk_parts[t // 2, :, bass.ds(b * D + (t % 2) * P, P), half * CH:(half + 1) * CH]
                            .rearrange("r p t -> p r t"), parts[t]).then_inc(stored[t], 16)

                staggered(sp, [(0, load), (1, store)], CHUNKS, turns=(0, 4))
                for t in range(4):
                    sp.wait_ge(stored[t], 16 * HALVES)
                load_stacks(sp, 0, 0)
                staggered(sp, [(0, load), (1, store)], CHUNKS, turns=(4, 8))
                load_stacks(sp, 1, 1)
                load_max(sp, 0, 0, 0)
                store(CHUNKS - 1, B - 1, 1)
                for t in range(4):
                    sp.wait_ge(stored[t], 16 * CHUNKS)

            @blk.gpsimd
            def _(pool):
                pool.memset(ident[:, :], 0.0).then_inc(const_zeroed, 1)
                pool.memset(ident_b[:, :], 0.0).then_inc(const_zeroed, 1)
                pool.memset(mask_b[:, :], 0.0).then_inc(const_zeroed, 1)
                pool.memset(before_b[:, :], 0.0).then_inc(const_zeroed, 1)
                pool.memset(ones_b[:, :], 1.0).then_inc(const_zeroed, 1)
                pool.memset(minus_half[:, :], -0.5).then_inc(const_zeroed, 1)
                pool.wait_ge(const_zeroed, 6)
                pool.affine_select(out=ident[:, :], in_=ident[:, :], compare_op=ALU.not_equal, fill=1.0, base=0,
                                   pattern=[[-1, P]], channel_multiplier=1).then_inc(const_ready, 1)
                pool.affine_select(out=ident_b[:, :], in_=ident_b[:, :], compare_op=ALU.not_equal, fill=1.0, base=0,
                                   pattern=[[-1, P]], channel_multiplier=1).then_inc(const_ready, 1)
                pool.affine_select(out=mask_b[:, :], in_=mask_b[:, :], compare_op=ALU.is_ge, fill=NEG, base=0,
                                   pattern=[[-1, P]], channel_multiplier=1).then_inc(const_ready, 1)
                pool.affine_select(out=before_b[:, :], in_=before_b[:, :], compare_op=ALU.is_ge, fill=1.0, base=0,
                                   pattern=[[-1, P]], channel_multiplier=1).then_inc(const_ready, 1)
                for r in range(2):
                    pool.memset(vg[r][:, :, :, DK:32], 1.0).then_inc(ones_ready, 1)
                pool.iota(iota_e[:, :], [[1, E]], base=0, channel_multiplier=0,
                          allow_small_or_imprecise_dtypes=True).then_inc(const_ready, 1)
                pool.iota(iota_blk[:, :], [[1, SEC_BLOCKS]], base=0, channel_multiplier=0,
                          allow_small_or_imprecise_dtypes=True).then_inc(const_ready, 1)

                def low(c, b, half):
                    for t in range(4):
                        pool.wait_ge(mid_ready, c * 4 + t + 1)
                        pool.tensor_tensor(parts[t][:, 2, :], rest[t], parts[t][:, 1, :],
                                           ALU.subtract).then_inc(lo_ready, 1)

                staggered(pool, [(0, low)], CHUNKS)
                for i in range(2):
                    pool.wait_ge(v_copied[i], HALVES)
                values(pool, 0, 0)

            @blk.scalar
            def _(act):
                for i, (w, bias) in enumerate(((Wq, bq), (Wk, bk))):
                    act.dma_start(wqk[:, i], w.rearrange("(c p) n -> p c n", p=P)).then_inc(wqk_loaded[i], 16)
                    act.dma_start(bqk[:, i], bias).then_inc(bqk_loaded, 16)
                act.dma_start(wv[:, :, :], Wv.rearrange("(c p) n -> p c n", p=P)).then_inc(wv_loaded, 16)
                act.dma_start(bv_all[:, :], bv.partition_broadcast(P)).then_inc(bv_loaded, 16)
                act.dma_start(bo_all[:, :], bo.partition_broadcast(P)).then_inc(big_loaded, 16)
                act.dma_start(ebias[:, :], expert_bias.partition_broadcast(P)).then_inc(big_loaded, 16)
                act.dma_start(wo[:, :, :], Wo.rearrange("(c p) n -> p c n", p=P)).then_inc(big_loaded, 16)
                act.dma_start(gate[:, :, :], gate_w.rearrange("(c p) n -> p c n", p=P)).then_inc(big_loaded, 16)
                act.dma_start(wsg[:, :, :], sg_w.rearrange("(c p) n -> p c n", p=P)).then_inc(big_loaded, 16)
                act.dma_start(wsu[:, :, :], su_w.rearrange("(c p) n -> p c n", p=P)).then_inc(big_loaded, 16)
                act.dma_start(wsd[:, :], sd_w).then_inc(big_loaded, 16)
                act.dma_start(wdn[:, :, :], down_w.rearrange("e p n -> p e n")).then_inc(big_loaded, 16)
                act.wait_ge(bqk_loaded, 32)

                def high(c, t):
                    act.wait_ge(proj_ready[t], c + 1)
                    wait_count(act, stored[t], 16 * c)
                    act.activation(parts[t][:, 0, :], ps[:, t, :], ACT.Identity,
                                   bias=bqk[:, t // 2, t % 2:t % 2 + 1]).then_inc(hi_ready, 1)

                def middle(c, t):
                    act.wait_ge(rest_ready[t], c + 1)
                    act.activation(parts[t][:, 1, :], rest[t], ACT.Copy).then_inc(mid_ready, 1)

                def split(c, b, half):
                    high(c, 0)
                    for t in range(1, 4):
                        high(c, t)
                        middle(c, t - 1)
                    middle(c, 3)

                staggered(act, [(0, split)], CHUNKS)
                act.wait_ge(big_loaded, 16 * 8)

            @blk.vector
            def _(dve):
                for r in range(STACKS):
                    dve.memset(ks[r][KS:KM], 1.0).then_inc(ones_ready, 1)
                dve.wait_ge(bqk_loaded, 32)
                dve.wait_ge(bv_loaded, 16)

                def early(c, g):
                    for k in early_share(c, g):
                        what, n = EARLY[k]
                        if what == "max":
                            piece_maximum(dve, 0, n, EARLY_BANKS[k % 2])
                            if n == NM0 - 1:
                                max_parts(dve, 0, 0)
                        else:
                            copy_maxima(dve, 0, 0, EARLY_BANKS[k % 2])

                def take(c, b, half):
                    for t in range(4):
                        if isinstance(c, int):
                            early(c, t)
                        dve.wait_ge(hi_ready, c * 4 + t + 1)
                        dve.scalar_tensor_tensor(rest[t], ps[:, t, :], bqk[:, t // 2, t % 2:t % 2 + 1],
                                                 parts[t][:, 0, :], ALU.add, ALU.subtract)\
                            .then_inc(rest_ready[t], 1)
                    for i in range(2):
                        dve.wait_ge(v_ready[i], c + 1)
                        for j in range(2):
                            tile = half * CT + 2 * i + j
                            ins = dve.tensor_tensor(
                                v_all[:, bass.ds(b * GROUPS, GROUPS), tile, :],
                                ps[:, 4 + i, j * D:(j + 1) * D].rearrange("p (g e) -> p g e", g=GROUPS),
                                bv_all[:, :].rearrange("p (g e) -> p g e", g=GROUPS), ALU.add)
                        ins.then_inc(v_copied[i], 1)
                        if isinstance(c, int):
                            early(c, 4 + i)

                staggered(dve, [(0, take)], CHUNKS, until=CHUNKS - 4)

            @blk.tensor
            def _(pe):

                def early(c, g):
                    for k in early_share(c, g):
                        if k == 0:
                            pe.wait_ge(const_ready, CONSTANTS)
                            pe.wait_ge(stack_loaded[0], 192)
                        if k >= 2:
                            what, n = EARLY[k - 2]
                            pe.wait_ge(*((reduced, n + 1) if what == "max" else (mT_copied[0], 1)))
                        what, n = EARLY[k]
                        if what == "max":
                            piece_scores(pe, 0, 0, n, EARLY_BANKS[k % 2])
                        else:
                            turn_maxima(pe, 0, 0, EARLY_BANKS[k % 2])

                def project(c, b, half):
                    pe.wait_ge(xt_loaded[half], 16 * b + 16)
                    for t in range(4):
                        if isinstance(c, int) and c == 0 and t % 2 == 0:
                            pe.wait_ge(wqk_loaded[t // 2], 16)
                        wait_count(pe, rest_ready[t], c)
                        for h in range(DC):
                            mm = pe.matmul(ps[:, t, :], wqk[:, t // 2, h, (t % 2) * P:(t % 2 + 1) * P],
                                           xt[half][:, h, :], start=(h == 0), stop=(h == DC - 1))
                        mm.then_inc(proj_ready[t], 1)
                        if isinstance(c, int):
                            early(c, t)
                    for i in range(2):
                        if isinstance(c, int) and c == 0 and i == 0:
                            pe.wait_ge(wv_loaded, 16)
                        wait_count(pe, v_copied[i], c)
                        for j in range(2):
                            tt = 2 * i + j
                            for h in range(DC):
                                mm = pe.matmul(ps[:, 4 + i, j * D:(j + 1) * D],
                                               xt[half][:, h, tt * P:(tt + 1) * P], wv[:, h, :],
                                               start=(h == 0), stop=(h == DC - 1))
                        mm.then_inc(v_ready[i], 1)
                        if isinstance(c, int):
                            early(c, 4 + i)

                staggered(pe, [(0, project)], CHUNKS, until=CHUNKS - 4)

        with ExitStack() as c2:
            probs = piece(0, PSLOTS * GH, CH)
            zero = piece(7168, ZEROS)
            SCORE_BANK, OUT_BANK = 0, 6

            zero_ready = sem("zero_ready")
            zero_stored = sem("zero_stored")
            score_ready = sem("score_ready")
            exp_done = sem("exp_done")
            masked = sem("masked")
            pv_done = sem("pv_done")
            o_copied = sem("o_copied")
            oT_ready = sem("oT_ready")
            recip_ready = sem("recip_ready")
            a_written = sem("a_written")
            blk = c2.enter_context(nc.Block())

            @blk.sync
            def _(sp):
                def step(i, r, more=True, load=True):
                    load_max(sp, i, r, 1)
                    if more:
                        if load:
                            wait_count(sp, pv_done, NU * i)
                            load_stacks(sp, i + 2, (r + 2) % STACKS)
                        load_max(sp, i + 1, (r + 1) % STACKS, 0)

                step(0, 0)
                sp.wait_ge(zero_ready, 1)
                with sp.Fori(0, FILLS) as j:
                    for q in range(STACKS):
                        step(STACKS * j + q + 1, (q + 1) % STACKS)
                        if q < SECTIONS:
                            part = SEC_ROWS // FILLS
                            sp.dma_start(y_sorted[q][bass.ds(j * part, part), :]
                                         .rearrange("(p a) d -> p (a d)", p=P)
                                         .rearrange("p (a d) -> p a d", a=part * D // (P * ZEROS)),
                                         zero.unsqueeze(1).broadcast_to((P, part * D // (P * ZEROS), ZEROS)))\
                                .then_inc(zero_stored, 16)
                step(13, 13 % STACKS)
                step(14, 14 % STACKS, load=False)
                step(15, 15 % STACKS, more=False)
                sp.wait_ge(zero_stored, 16 * SECTIONS * FILLS)

            @blk.gpsimd
            def _(pool):
                pool.memset(vg[2][:, :, :, DK:32], 1.0).then_inc(ones_ready, 1)
                pool.memset(zero, 0.0).then_inc(zero_ready, 1)

                def mask(i, u):
                    off = P * (UNITS[u][1] - CT * UNITS[u][0])
                    s = (u % PSLOTS) * GH
                    wait_apart(pool, exp_done, 2 * (NU * i + u) + 2, pool_waited)
                    blk_ = probs[:, s:s + GH, off:off + P]
                    pool.affine_select(out=blk_, in_=blk_, compare_op=ALU.is_ge, fill=0.0, base=0,
                                       pattern=[[0, GH], [1, P]], channel_multiplier=-1).then_inc(masked, 1)

                def step(i, r, more=True):
                    for u in DIAG[:CT]:
                        mask(i, u)
                    if more:
                        wait_count(pool, pv_done, NU * (i - 1))
                        values(pool, i + 1, (r + 1) % STACKS)
                    for u in DIAG[CT:]:
                        mask(i, u)

                for i in range(STACKS + 1):
                    step(i, i % STACKS)
                with pool.Fori(1, 4) as j:
                    for q in range(STACKS):
                        step(STACKS * j + q + 1, (q + 1) % STACKS)
                step(13, 13 % STACKS)
                step(14, 14 % STACKS)
                step(15, 15 % STACKS, more=False)

            @blk.scalar
            def _(act):
                def exp(i, u):
                    off = CH - unit_width(u)
                    s = (u % PSLOTS) * GH
                    wait_count(act, pv_done, NU * i + u - PSLOTS + 1)
                    for pair in range(2):
                        act.wait_ge(score_ready, 2 * (NU * i + u) + pair + 1)
                        act.activation(probs[:, s + 2 * pair:s + 2 * pair + 2, off:CH],
                                       ps[:, SCORE_BANK + 2 * pair:SCORE_BANK + 2 * pair + 2, off:CH],
                                       ACT.Exp, scale=float(DK) ** -0.5).then_inc(exp_done, 1)

                def copy_out(i, qc):
                    act.wait_ge(pv_done, NU * i + (CT if qc == 0 else NU))
                    wait_count(act, oT_ready, 2 * i + qc - 1)
                    act.activation(oT[qc][:, :], ps[:, OUT_BANK, :], ACT.Copy).then_inc(o_copied, 1)

                def step(i, prev=True):
                    for u in range(NU):
                        exp(i, u)
                        if u == 0 and prev:
                            copy_out(i - 1, 1)
                        if u == CT:
                            copy_out(i, 0)

                step(0, prev=False)
                step(1)
                with act.Fori(2, STEPS) as i:
                    step(i)
                copy_out(STEPS - 1, 1)

            @blk.vector
            def _(dve):
                def normalise(i, qc):
                    o = ps[:, ring_bank(("turn_out", qc, 0)), :].rearrange("p (t h e) -> p t h e", t=CT, e=32)
                    dve.wait_ge(oT_ready, 2 * i + qc + 1)
                    wait_count(dve, a_written, 2 * i + qc)
                    dve.reciprocal(recip[:, :, :], o[:, :, :, DK]).then_inc(recip_ready, 1)
                    dve.wait_ge(recip_ready, 2 * i + qc + 1)
                    dve.tensor_tensor(a_all[:, bass.ds(i, 1), qc * CT:(qc + 1) * CT, :]
                                      .rearrange("p a t (h e) -> p (a t) h e", e=DK), o[:, :, :, 0:DK],
                                      recip[:, :, :].unsqueeze(3).broadcast_to((P, CT, GH, DK)), ALU.mult)\
                        .then_inc(a_written, 1)

                def step(i, first=False, last=False):
                    max_parts(dve, i, 1)
                    for item in ORDER:
                        what, n, _ = item
                        if item not in RING_USERS or not present(item, first, last):
                            continue
                        if what == "max":
                            piece_maximum(dve, i + 1, n, ring_bank(item))
                            if n == NM0 - 1:
                                max_parts(dve, i + 1, 0)
                        elif what == "turn_max":
                            copy_maxima(dve, i + 1 - n, n, ring_bank(item))
                        else:
                            normalise(i - n, n)

                step(0, first=True)
                with dve.Fori(1, STEPS - 1) as i:
                    step(i)
                step(STEPS - 1, last=True)
                normalise(STEPS - 1, 1)

            @blk.tensor
            def _(pe):

                def scores(i, r, u, pair):
                    qc, kt = UNITS[u]
                    off = CH - unit_width(u)
                    if pair == 0 and kt == 0:
                        pe.wait_ge(m_loaded[qc], 48 * i + 48)
                    wait_count(pe, exp_done, 2 * (NU * i + u) + pair - 1)
                    for h in (2 * pair, 2 * pair + 1):
                        mm = pe.matmul(ps[:, SCORE_BANK + h, off:CH], ks[r][0:KM, h, kt * P:(kt + 1) * P],
                                       qs[r][0:KM, h, qc * CH + off:(qc + 1) * CH], start=True, stop=True)
                    mm.then_inc(score_ready, 1)

                def weigh(i, r, u):
                    qc, kt = UNITS[u]
                    off = CH - unit_width(u)
                    s = (u % PSLOTS) * GH
                    if u in DIAG:
                        pe.wait_ge(masked, len(DIAG) * i + DIAG.index(u) + 1)
                    else:
                        pe.wait_ge(exp_done, 2 * (NU * i + u) + 2)
                    if kt == 0:
                        wait_count(pe, o_copied, 2 * i + qc)
                    for h in range(GH):
                        mm = pe.matmul(ps[32 * h:32 * h + 32, OUT_BANK, off:CH], vg[r][:, kt, h, :],
                                       probs[:, s + h, off:CH], start=(kt == 0), stop=(kt == CT * (qc + 1) - 1))
                    mm.then_inc(pv_done, 1)

                def ring_free(i, item, first, last, second=False):
                    before, ago = ring_before(item, first, last, second)
                    if before is None:
                        return
                    what, n, _ = before
                    if what == "max":
                        wait_count(pe, reduced, NM * (i + 1 - ago) + n + 1)
                    elif what == "turn_max":
                        wait_count(pe, mT_copied[n], i + 2 - n - ago)
                    else:
                        wait_count(pe, a_written, 2 * (i - ago) + (1 if n == 0 else 0))

                def turn_out(i, qc):
                    pe.wait_ge(o_copied, 2 * i + qc + 1)
                    for t in range(CT):
                        mm = pe.transpose(ps[:, ring_bank(("turn_out", qc, 0)), t * P:(t + 1) * P],
                                          oT[qc][:, t * P:(t + 1) * P], ident[:, :])
                    mm.then_inc(oT_ready, 1)

                def step(i, k3, r, first=False, last=False, second=False):
                    pe.wait_ge(vg_ready, i + 1)
                    for item in ORDER:
                        what, n, pair = item
                        if item == ("max", 0, 0) and not last:
                            pe.wait_ge(stack_loaded[(r + 1) % STACKS], 192 * (k3 + (r + 1) // STACKS) + 192)
                        if what == "scores":
                            scores(i, r, n, pair)
                        elif what == "weigh":
                            if n >= 0:
                                weigh(i, r, n)
                            elif not first:
                                weigh(i - 1, (r - 1) % STACKS, NU - 1)
                        elif present(item, first, last):
                            ring_free(i, item, first, last, second)
                            if what == "max":
                                piece_scores(pe, i + 1, (r + 1) % STACKS, n, ring_bank(item))
                            elif what == "turn_max":
                                turn_maxima(pe, i + 1 - n, n, ring_bank(item))
                            else:
                                turn_out(i - n, n)

                step(0, 0, 0, first=True)
                step(1, 0, 1, second=True)
                pe.wait_ge(ones_ready, 2 * STACKS)
                with pe.Fori(0, 4) as j:
                    for q in range(STACKS):
                        step(STACKS * j + q + 2, j + (q + 2) // STACKS, (q + 2) % STACKS)
                step(14, 4, 14 % STACKS)
                step(15, 5, 15 % STACKS, last=True)
                weigh(STEPS - 1, 15 % STACKS, NU - 1)
                pe.wait_ge(a_written, 2 * STEPS - 1)
                turn_out(STEPS - 1, 1)

        held.close()
        scores_all = sb("scores_all", [P, TILES, E], F32)
        chosen = sb("chosen", [P, TOPK, TILES], F32)
        weight = sb("weight", [P, TOPK, TILES], F32)
        row_of = sb("row_of", [P, TOPK, TILES], U32)
        block_expert = sb("block_expert", [P, SECTIONS * SEC_BLOCKS], U32)

        with ExitStack() as c3:
            def small(name, shape, dt=F32):
                return c3.enter_context(nc.sbuf_tensor(name, shape, dt))

            attn = [piece(1024 * r, CT, D) for r in range(2)]
            attnT = [piece(2048 + 1024 * r, DC, CH) for r in range(2)]
            xr = [piece(4096 + 1024 * r, CT, D) for r in range(2)]
            res = [piece(6144 + 1024 * r, CT, D) for r in range(2)]
            yT = [small(f"yT{r}", [P, DC, CH]) for r in range(2)]
            stats = small("stats", [P, CT, 6])
            moments = [small(f"moments{r}", [P, CT, 2]) for r in range(2)]
            rstd = [small(f"rstd{r}", [P, CT]) for r in range(2)]
            enl = small("enl", [P, CT, E])
            biased = small("biased", [P, CT, E])
            top = small("top", [P, CT, 8])
            top_at = small("top_at", [P, CT, 8], U32)
            gact = [wqk[:, r, :, :].rearrange("p c n -> p (c n)") for r in range(2)]
            TE = SEC_TILES * E

            def by_tile(words):
                return words.rearrange("p (t e) -> p t e", e=E)

            picks_at = wv[:, :, :].rearrange("p c n -> p (c n)")
            pick = [by_tile(picks_at[:, TE * j:TE * (j + 1)]) for j in range(TOPK)]
            at = SEC_BLOCKS * E
            sorting = small("sorting", [P, at + SEC_BLOCKS + (2 * TOPK + 1) * SEC_TILES])
            run = [by_tile(sorting[:, TE * j:TE * (j + 1)]) for j in range(2)]
            over = sorting[:, 0:at].rearrange("p (n e) -> p n e", e=E)
            before_blk = sorting[:, at:at + SEC_BLOCKS]
            at += SEC_BLOCKS
            row_f, top_s = [sorting[:, at + k * TOPK * SEC_TILES:at + (k + 1) * TOPK * SEC_TILES]
                            .rearrange("p (j t) -> p j t", j=TOPK) for k in range(2)]
            at += 2 * TOPK * SEC_TILES
            sum_s = sorting[:, at:at + SEC_TILES]
            cnt = [bv_all[:, E * j:E * (j + 1)] for j in range(8)]
            cnt_i = [bv_all[:, E * (8 + j):E * (9 + j)].bitcast(I32) for j in range(2)]
            pick_b = small("pick_b", [P, SEC_TILES, E], BF16)
            ys = [piece(512 * r, 2, D) for r in range(2)]
            ysT = [work[:, 1024 + 512 * r:1536 + 512 * r].rearrange("p (h k t) -> p h k t", h=DC, k=2)
                   for r in range(2)]
            gx = [piece(2048 + 256 * r, 2, F) for r in range(2)]
            hx = [piece(2560 + 256 * r, 2, F) for r in range(2)]
            hxT = [piece(3072 + 256 * r, 2, P) for r in range(2)]
            zs = [piece(3584 + 512 * r, 2, D) for r in range(2)]
            zg = [piece(4608 + 512 * r, TOPK, D) for r in range(ZSLOTS)]
            acc = [yT[r][:, :, :].rearrange("p c t -> p (c t)").rearrange("p (t d) -> p t d", d=D) for r in range(2)]
            acc.append(piece(7168, CT, D))
            moments2 = [small(f"second_moments{r}", [P, CT, 2]) for r in range(2)]
            stats2 = small("second_stats", [P, CT, 6])
            rstd2 = [small(f"second_rstd{r}", [P, CT]) for r in range(2)]

            wgu_loaded = sem("wgu_loaded")
            x_loaded = [sem(f"x_loaded{r}") for r in range(2)]
            xb_ready = sem("xb_ready")
            attn_ready = sem("attn_ready")
            aT_ready = sem("aT_ready")
            aT_copied = sem("aT_copied")
            wo_ready = sem("wo_ready")
            res_ready = sem("res_ready")
            stats_ready = sem("stats_ready")
            moments_ready = sem("moments_ready")
            rstd_step = sem("rstd_step")
            rstd_ready = sem("rstd_ready")
            y_ready = sem("y_ready")
            y_saved = sem("y_saved")
            yT_saved = sem("yT_saved")
            yT_ready = sem("yT_ready")
            yT_copied = sem("yT_copied")
            logit_ready = sem("logit_ready")
            enl_ready = sem("enl_ready")
            route_step = sem("route_step")
            picked = sem("picked")
            counted = sem("counted")
            counts_used = sem("counts_used")
            chain = sem("chain")
            rows_ready = sem("rows_ready")
            blocks_ready = sem("blocks_ready")
            scattered = [sem(f"scattered{g}") for g in range(SECTIONS)]
            gate_ready = sem("gate_ready")
            up_ready = sem("up_ready")
            gact_ready = sem("gact_ready")
            hid_ready = sem("hid_ready")
            down_ready = sem("down_ready")
            shared_done = sem("shared_done")
            ys_loaded = [sem(f"ys_loaded{r}") for r in range(2)]
            z_stored = [sem(f"z_stored{r}") for r in range(2)]
            ysT_ready = sem("ysT_ready")
            ysT_copied = sem("ysT_copied")
            gu_ready = sem("gu_ready")
            gx_ready = sem("gx_ready")
            hx_ready = sem("hx_ready")
            hxT_ready = sem("hxT_ready")
            hxT_copied = sem("hxT_copied")
            z_ready = sem("z_ready")
            z_copied = sem("z_copied")
            gathered = [sem(f"gathered{r}") for r in range(ZSLOTS)]
            first_added = sem("first_added")
            both_added = sem("both_added")
            stats2_ready = sem("stats2_ready")
            moments2_ready = sem("moments2_ready")
            rstd2_step = sem("rstd2_step")
            rstd2_ready = sem("rstd2_ready")
            out_ready = sem("out_ready")
            out_stored = [sem(f"out_stored{c}") for c in range(CHUNKS)]
            x_v = x.rearrange("b (t p) d -> p (b t) d", p=P)
            o_v = out.rearrange("b (t p) d -> p (b t) d", p=P)
            RS = 4 + 2 * CT
            y_rows = [y_sorted[g].rearrange("(n p) d -> p n d", p=P) for g in range(SECTIONS)]
            z_rows = [z_sorted[g].rearrange("(n p) d -> p n d", p=P) for g in range(SECTIONS)]
            LAST_FROM = SEC_PAIRS + 5
            COUNT_BANK = 7
            NORM_BEHIND = CT + 2
            blk = c3.enter_context(nc.Block())

            @blk.sync
            def _(sp):
                def load_x(c, b, r):
                    wait_count(sp, res_ready, c - 1)
                    sp.dma_start(xr[r], x_v[:, bass.ds(c * CT, CT), :]).then_inc(x_loaded[r], 16)

                staggered(sp, [(0, load_x)], CHUNKS, turns=(0, 2))
                sp.dma_start(wgu[:, :, :, :].rearrange("p e c n -> p (e c) n"),
                             gu_w.rearrange("e (c p) n -> p (e c) n", p=P)).then_inc(wgu_loaded, 16)
                staggered(sp, [(0, load_x)], CHUNKS, turns=(2, CHUNKS))
                for g in range(SECTIONS):
                    def load_rows(n, k2, r):
                        wait_count(sp, ysT_ready, n - 1)
                        sp.dma_start(ys[r], y_rows[g][:, bass.ds(2 * n - g * SEC_BLOCKS, 2), :])\
                            .then_inc(ys_loaded[r], 16)

                    sp.wait_ge(scattered[g], 16 * TOPK * SEC_TILES)
                    staggered(sp, [(0, load_rows)], SEC_PAIRS, base=g * SEC_PAIRS)
                for c in range(SEC_CHUNKS, CHUNKS):
                    sp.wait_ge(out_ready, c + 1)
                    sp.dma_start(o_v[:, c * CT:(c + 1) * CT, :], acc[c % len(acc)]).then_inc(out_stored[c], 16)
                for c in range(CHUNKS):
                    sp.wait_ge(out_stored[c], 16)

            @blk.gpsimd
            def _(pool):
                def add_bias(c, b, r):
                    pool.wait_ge(x_loaded[r], 16 * b + 16)
                    pool.tensor_tensor(xr[r], xr[r], bo_all[:, :].unsqueeze(1).broadcast_to((P, CT, D)),
                                       ALU.add).then_inc(xb_ready, 1)

                def deviation(c, b, r):
                    wait_apart(pool, moments_ready, CT * c + CT, pool_waited)
                    pool.tensor_scalar(rstd[r][:, :], moments[r][:, :, 1], EPS, None, ALU.add).then_inc(rstd_step, 1)
                    pool.wait_ge(rstd_step, c + 1)
                    pool.tensor_tensor(rstd[r][:, :], rstd[r][:, :], minus_half[:, :], ALU.pow)\
                        .then_inc(rstd_ready, 1)

                def scatter(t):
                    g = t // SEC_TILES
                    for j in range(TOPK):
                        pool.indirect_dma_start(
                            out=y_sorted[g], out_offset=bass.IndirectOffsetOnAxis(ap=row_of[:, j, t:t + 1], axis=0),
                            in_=y_all[:, t, :], in_offset=None).then_inc(scattered[g], 16)

                def gather(u):
                    wait_count(pool, both_added, u - ZSLOTS + 1)
                    for j in range(TOPK):
                        pool.indirect_dma_start(
                            out=zg[u % ZSLOTS][:, j, :], out_offset=None, in_=z_sorted[u // SEC_TILES],
                            in_offset=bass.IndirectOffsetOnAxis(ap=row_of[:, j, u:u + 1], axis=0))\
                            .then_inc(gathered[u % ZSLOTS], 16)

                def second_deviation(c):
                    r = c % 2
                    pool.wait_ge(moments2_ready, CT * c + CT)
                    pool.tensor_scalar(rstd2[r][:, :], moments2[r][:, :, 1], EPS, None, ALU.add)\
                        .then_inc(rstd2_step, 1)
                    pool.wait_ge(rstd2_step, c + 1)
                    pool.tensor_tensor(rstd2[r][:, :], rstd2[r][:, :], minus_half[:, :], ALU.pow)\
                        .then_inc(rstd2_ready, 1)

                def store(c):
                    pool.wait_ge(out_ready, c + 1)
                    pool.dma_start(o_v[:, c * CT:(c + 1) * CT, :], acc[c % len(acc)]).then_inc(out_stored[c], 16)

                staggered(pool, [(0, add_bias), (1, deviation)], CHUNKS)
                for g in range(SECTIONS):
                    pool.wait_ge(rows_ready, g + 1)
                    for t in range(g * SEC_TILES, (g + 1) * SEC_TILES):
                        scatter(t)
                for g in range(SECTIONS):
                    for r in range(2):
                        pool.wait_ge(z_stored[r], 16 * (g + 1) * SEC_PAIRS // 2)
                    first = g * SEC_CHUNKS
                    for u in range(g * SEC_TILES, (g + 1) * SEC_TILES):
                        gather(u)
                        c = u // CT - 1
                        if c >= first and u % CT == 1:
                            second_deviation(c)
                            if g == 0 and c - 2 >= first:
                                store(c - 2)
                    last = first + SEC_CHUNKS - 1
                    second_deviation(last)
                    if g == 0:
                        for c in range(last - 2, last + 1):
                            store(c)

            @blk.scalar
            def _(act):
                def gather_heads(c, b, r):
                    wait_count(act, aT_ready, c - 1)
                    act.activation(attn[r].rearrange("p t (g e) -> p t g e", g=GROUPS),
                                   a_all[:, bass.ds(b * GROUPS, GROUPS), r * CT:(r + 1) * CT, :]
                                   .rearrange("p g t e -> p t g e"), ACT.Copy).then_inc(attn_ready, 1)

                def copy_attn(c, b, r):
                    act.wait_ge(aT_ready, c + 1)
                    wait_count(act, wo_ready, 2 * c - 2)
                    act.activation(attnT[r], ps[:, 0:2, :], ACT.Copy).then_inc(aT_copied, 1)

                def save_y(c, b, r):
                    act.wait_ge(y_ready, c + 1)
                    act.activation(y_all[:, bass.ds(c * CT, CT), :], res[r], ACT.Copy).then_inc(y_saved, 1)

                def copy_y(c, b, r):
                    act.wait_ge(yT_ready, c + 1)
                    wait_count(act, logit_ready, c - 1)
                    act.activation(yT[r][:, :, :], ps[:, 4:6, :], ACT.Copy).then_inc(yT_copied, 1)
                    act.wait_ge(yT_copied, c + 1)
                    act.activation(yT_all[:, :, bass.ds(c * CH, CH)], yT[r][:, :, :], ACT.Copy).then_inc(yT_saved, 1)

                def exp(c, b, r):
                    act.wait_ge(logit_ready, c + 1)
                    wait_count(act, route_step, RS * (c - 1) + 1)
                    act.activation(enl[:, :, :], ps[:, 6, 0:CT * E].rearrange("p (t e) -> p t e", e=E), ACT.Exp,
                                   scale=-1.0).then_inc(enl_ready, 1)

                def gate(c, b, r):
                    act.wait_ge(gate_ready, c + 1)
                    wait_count(act, down_ready, 2 * (c - 1))
                    act.activation(gact[r], ps[:, 4 * r, :], ACT.Silu).then_inc(gact_ready, 1)

                def turned(n, k2, r):
                    act.wait_ge(ysT_ready, n + 1)
                    wait_count(act, gu_ready, n - 1)
                    act.activation(ysT[r].rearrange("p h k t -> p (h k t)"), ps[:, r, :], ACT.Copy)\
                        .then_inc(ysT_copied, 1)

                def silu(n, k2, r):
                    act.wait_ge(gu_ready, n + 1)
                    wait_count(act, hx_ready, n - 1)
                    act.activation(gx[r], ps[:, 2 + r, :].rearrange("p (k c) -> p k c", k=2)[:, :, 0:F], ACT.Silu)\
                        .then_inc(gx_ready, 1)

                def result(g):
                    def stage(n, k2, r):
                        act.wait_ge(z_ready, n + 1)
                        wait_count(act, z_stored[r], 16 * k2)
                        act.activation(zs[r], ps[:, 6 + r, :].rearrange("p (k d) -> p k d", k=2), ACT.Copy)\
                            .then_inc(z_copied, 1)
                        act.wait_ge(z_copied, n + 1)
                        act.dma_start(z_rows[g][:, bass.ds(2 * n - g * SEC_BLOCKS, 2), :], zs[r])\
                            .then_inc(z_stored[r], 16)
                    return stage

                def chunk_turns(low, high):
                    staggered(act, [(0, gather_heads), (0, copy_attn), (2, save_y), (2, copy_y), (3, exp)], CHUNKS,
                              turns=(low, high))

                chunk_turns(0, CHUNKS + 1)
                gate(0, 0, 0)
                save_y(CHUNKS - 1, B - 1, 1)
                copy_y(CHUNKS - 1, B - 1, 1)
                gate(1, 0, 1)
                exp(CHUNKS - 2, B - 1, 0)
                exp(CHUNKS - 1, B - 1, 1)
                staggered(act, [(0, gate)], CHUNKS, turns=(2, CHUNKS))
                act.wait_ge(wgu_loaded, 16)
                for g in range(SECTIONS):
                    staggered(act, [(0, turned), (1, silu), (3, result(g))], PAIRS,
                              turns=(g * (SEC_PAIRS + 3), (g + 1) * SEC_PAIRS + 3))
                for r in range(2):
                    act.wait_ge(z_stored[r], 16 * PAIRS // 2)

            @blk.vector
            def _(dve):
                def residual(c, b, r):
                    wait_count(dve, yT_ready, c - 1)
                    wait_count(dve, y_saved, c - 1)
                    dve.wait_ge(xb_ready, c + 1)
                    for i in range(2):
                        dve.wait_ge(wo_ready, 2 * c + i + 1)
                        ins = dve.tensor_tensor(res[r][:, 2 * i:2 * i + 2, :],
                                                ps[:, 2 + i, :].rearrange("p (t d) -> p t d", d=D),
                                                xr[r][:, 2 * i:2 * i + 2, :], ALU.add)
                    ins.then_inc(res_ready, 1)
                    dve.wait_ge(res_ready, c + 1)
                    for t in range(CT):
                        dve.bn_stats(stats[:, t, :], res[r][:, t, :]).then_inc(stats_ready, 1)
                    wait_apart(dve, stats_ready, CT * c + CT, dve_waited)
                    for t in range(CT):
                        dve.bn_aggr(moments[r][:, t, :], stats[:, t, :]).then_inc(moments_ready, 1)

                def norm(c, b, r):
                    dve.wait_ge(rstd_ready, c + 1)
                    for t in range(CT):
                        ins = dve.tensor_scalar(res[r][:, t, :], res[r][:, t, :],
                                                moments[r][:, t, 0:1], rstd[r][:, t:t + 1], ALU.subtract, ALU.mult)
                    ins.then_inc(y_ready, 1)

                def route(c, b, r):
                    tiles = bass.ds(c * CT, CT)
                    dve.wait_ge(enl_ready, c + 1)
                    dve.tensor_scalar(biased[:, :, :], enl[:, :, :], 1.0, None, ALU.add).then_inc(route_step, 1)
                    dve.wait_ge(route_step, RS * c + 1)
                    dve.reciprocal(scores_all[:, tiles, :], biased[:, :, :]).then_inc(route_step, 1)
                    dve.wait_ge(route_step, RS * c + 2)
                    dve.tensor_tensor(biased[:, :, :], scores_all[:, tiles, :],
                                      ebias[:, :].unsqueeze(1).broadcast_to((P, CT, E)), ALU.add)\
                        .then_inc(route_step, 1)
                    wait_apart(dve, route_step, RS * c + 3, dve_waited)
                    for t in range(CT):
                        dve.max(top[:, t, :], biased[:, t, :]).then_inc(route_step, 1)
                    wait_apart(dve, route_step, RS * c + 3 + CT, dve_waited)
                    for t in range(CT):
                        dve.max_index(top_at[:, t, :], top[:, t, :], biased[:, t, :]).then_inc(route_step, 1)
                    dve.wait_ge(route_step, RS * c + 3 + 2 * CT)
                    dve.tensor_copy(chosen[:, :, tiles].rearrange("p j t -> p t j"), top_at[:, :, 0:TOPK])\
                        .then_inc(route_step, 1)

                links = [0]

                def link(ins):
                    links[0] += 1
                    ins.then_inc(chain, 1)
                    dve.wait_ge(chain, links[0])

                def tiles_of(g):
                    return slice(g * SEC_TILES, (g + 1) * SEC_TILES)

                def pick_experts(g):
                    dve.wait_ge(route_step, RS * SEC_CHUNKS * (g + 1))
                    for j in range(TOPK):
                        link(dve.tensor_tensor(pick[j], iota_e[:, :].unsqueeze(1).broadcast_to((P, SEC_TILES, E)),
                                               chosen[:, j, tiles_of(g)].unsqueeze(2).broadcast_to((P, SEC_TILES, E)),
                                               ALU.is_equal))
                    dve.tensor_tensor(pick_b[:, :, :], pick[0], pick[1], ALU.add).then_inc(picked, 1)

                def weights(g):
                    prod = run[0]
                    for j in range(TOPK):
                        link(dve.tensor_tensor(prod, pick[j], scores_all[:, tiles_of(g), :], ALU.mult))
                        link(dve.tensor_reduce(top_s[:, j, :], prod, AX.X, ALU.add))
                    link(dve.tensor_tensor(sum_s, top_s[:, 0, :], top_s[:, 1, :], ALU.add))
                    link(dve.tensor_scalar(sum_s, sum_s, 1e-20, None, ALU.add))
                    link(dve.reciprocal(sum_s, sum_s))
                    link(dve.tensor_tensor(weight[:, :, tiles_of(g)], top_s,
                                           sum_s.unsqueeze(1).broadcast_to((P, TOPK, SEC_TILES)), ALU.mult))

                def expert_ends(g):
                    dve.wait_ge(counted, g + 1)
                    link(dve.tensor_copy(run[0], ps[:, COUNT_BANK, SEC_TILES * E:].rearrange("p (t e) -> p t e", e=E)))
                    at, s = 0, 1
                    while s < SEC_TILES:
                        dve.tensor_copy(run[1 - at][:, 0:s, :], run[at][:, 0:s, :]).then_inc(chain, 1)
                        links[0] += 1
                        link(dve.tensor_tensor(run[1 - at][:, s:SEC_TILES, :], run[at][:, s:SEC_TILES, :],
                                               run[at][:, 0:SEC_TILES - s, :], ALU.add))
                        at, s = 1 - at, 2 * s
                    assert at == 0
                    total = run[at][:, SEC_TILES - 1, :]
                    link(dve.tensor_scalar(cnt_i[0], total, float(P - 1), None, ALU.add))
                    link(dve.tensor_scalar(cnt_i[1], cnt_i[0], P.bit_length() - 1, None, ALU.arith_shift_right))
                    link(dve.tensor_copy(cnt[0], cnt_i[1]))
                    link(dve.tensor_copy(cnt[1], cnt[0]))
                    a, s = 1, 1
                    while s < E:
                        dve.tensor_copy(cnt[a + 1][:, 0:s], cnt[a][:, 0:s]).then_inc(chain, 1)
                        links[0] += 1
                        link(dve.tensor_tensor(cnt[a + 1][:, s:E], cnt[a][:, s:E], cnt[a][:, 0:E - s], ALU.add))
                        a, s = a + 1, 2 * s
                    link(dve.tensor_tensor(cnt[a + 1], cnt[a], cnt[0], ALU.subtract))
                    link(dve.tensor_scalar(cnt[a + 1], cnt[a + 1], float(P), None, ALU.mult))
                    return run[at], cnt[a], cnt[a + 1]

                def rows(g, up_to, first):
                    count = ps[:, COUNT_BANK, :].rearrange("p (j t e) -> p j t e", j=2, e=E)
                    base, prod = up_to, run[1]
                    link(dve.tensor_tensor(base, base, count[:, 1], ALU.subtract))
                    dve.tensor_tensor(base, base, count[:, 0], ALU.add).then_inc(counts_used, 1)
                    dve.wait_ge(counts_used, g + 1)
                    link(dve.tensor_tensor(base, base, first.unsqueeze(1).broadcast_to((P, SEC_TILES, E)), ALU.add))
                    for j in range(TOPK):
                        link(dve.tensor_tensor(prod, pick[j], base, ALU.mult))
                        link(dve.tensor_reduce(row_f[:, j, :], prod, AX.X, ALU.add))
                    dve.tensor_copy(row_of[:, :, tiles_of(g)], row_f).then_inc(rows_ready, 1)

                def block_experts(g, ends):
                    link(dve.tensor_tensor(over, iota_blk[:, :].unsqueeze(2).broadcast_to((P, SEC_BLOCKS, E)),
                                           ends.unsqueeze(1).broadcast_to((P, SEC_BLOCKS, E)), ALU.is_ge))
                    link(dve.tensor_reduce(before_blk, over, AX.X, ALU.add))
                    link(dve.tensor_scalar(before_blk, before_blk, float(E - 1), None, ALU.min))
                    dve.tensor_copy(block_expert[:, g * SEC_BLOCKS:(g + 1) * SEC_BLOCKS], before_blk)\
                        .then_inc(blocks_ready, 1)

                def shared_hidden(c):
                    dve.wait_ge(gact_ready, c + 1)
                    dve.wait_ge(up_ready, c + 1)
                    dve.tensor_tensor(gact[c % 2], gact[c % 2], ps[:, 4 * (c % 2) + 1, :], ALU.mult)\
                        .then_inc(hid_ready, 1)

                def shared_add(c):
                    for i in range(2):
                        dve.wait_ge(down_ready, 2 * c + i + 1)
                        dve.wait_ge(y_saved, c + 1)
                        tiles = slice(c * CT + 2 * i, c * CT + 2 * i + 2)
                        dve.tensor_tensor(sh_all[:, tiles, :], y_all[:, tiles, :],
                                          ps[:, 2 + i, :].rearrange("p (t d) -> p t d", d=D),
                                          ALU.add).then_inc(shared_done, 1)

                def hidden(n, k2, r):
                    dve.wait_ge(gx_ready, n + 1)
                    wait_count(dve, hxT_ready, n - 1)
                    dve.tensor_tensor(hx[r], gx[r], ps[:, 2 + r, :].rearrange("p (k c) -> p k c", k=2)[:, :, F:2 * F],
                                      ALU.mult).then_inc(hx_ready, 1)

                def hidden_turned(n, k2, r):
                    dve.wait_ge(hxT_ready, n + 1)
                    wait_count(dve, z_ready, n - 1)
                    dve.tensor_copy(hxT[r], ps[:, 4 + r, 0:2 * P].rearrange("p (k t) -> p k t", k=2))\
                        .then_inc(hxT_copied, 1)

                def combine(u):
                    c, t = u // CT, u % CT
                    z, a = zg[u % ZSLOTS], acc[c % len(acc)]
                    dve.wait_ge(gathered[u % ZSLOTS], 16 * TOPK * (u // ZSLOTS + 1))
                    if t == 0 and c >= len(acc):
                        dve.wait_ge(out_stored[c - len(acc)], 16)
                    dve.scalar_tensor_tensor(a[:, t, :], z[:, 0, :], weight[:, 0, u:u + 1], sh_all[:, u, :],
                                             ALU.mult, ALU.add).then_inc(first_added, 1)
                    dve.wait_ge(first_added, u + 1)
                    dve.scalar_tensor_tensor(a[:, t, :], z[:, 1, :], weight[:, 1, u:u + 1], a[:, t, :],
                                             ALU.mult, ALU.add).then_inc(both_added, 1)
                    dve.wait_ge(both_added, u + 1)
                    dve.bn_stats(stats2[:, t, :], a[:, t, :]).then_inc(stats2_ready, 1)
                    dve.wait_ge(stats2_ready, u + 1)
                    dve.bn_aggr(moments2[c % 2][:, t, :], stats2[:, t, :]).then_inc(moments2_ready, 1)

                def second_norm(u):
                    c, t = u // CT, u % CT
                    if t == 0:
                        dve.wait_ge(rstd2_ready, c + 1)
                    a = acc[c % len(acc)][:, t, :]
                    ins = dve.tensor_scalar(a, a, moments2[c % 2][:, t, 0:1],
                                            rstd2[c % 2][:, t:t + 1], ALU.subtract, ALU.mult)
                    if t == CT - 1:
                        ins.then_inc(out_ready, 1)

                def last_stage(t):
                    if 0 <= t - LAST_FROM < SEC_TILES:
                        combine(t - LAST_FROM)
                    if 0 <= t - LAST_FROM - NORM_BEHIND < SEC_TILES:
                        second_norm(t - LAST_FROM - NORM_BEHIND)

                def chunk_turns(low, high):
                    staggered(dve, [(1, norm), (0, residual), (3, route)], CHUNKS, turns=(low, high))

                chunk_turns(0, CHUNKS)
                pick_experts(0)
                norm(CHUNKS - 1, B - 1, 1)
                up_to, ends, first_row = expert_ends(0)
                rows(0, up_to, first_row)
                shared_hidden(0)
                route(CHUNKS - 3, B - 2, 1)
                shared_hidden(1)
                shared_add(0)
                route(CHUNKS - 2, B - 1, 0)
                block_experts(0, ends)
                shared_hidden(2)
                shared_add(1)
                route(CHUNKS - 1, B - 1, 1)
                weights(0)
                pick_experts(1)
                shared_hidden(3)
                shared_add(2)
                shared_hidden(4)
                shared_add(3)
                up_to, ends, first_row = expert_ends(1)
                shared_hidden(5)
                shared_add(4)
                rows(1, up_to, first_row)
                shared_hidden(6)
                shared_add(5)
                weights(1)
                shared_hidden(7)
                shared_add(6)
                block_experts(1, ends)
                shared_add(7)
                staggered(dve, [(0, hidden), (1, hidden_turned)], PAIRS, until=LAST_FROM // 2 * 2, beside=last_stage)
                for t in range(PAIRS + 1, LAST_FROM + NORM_BEHIND + SEC_TILES):
                    last_stage(t)
                for u in range(SEC_TILES, TILES):
                    combine(u)
                    if u % CT == 1 and u > SEC_TILES + CT:
                        for v in range(u - 1 - CT, u - 1):
                            second_norm(v)
                for v in range(TILES - CT, TILES):
                    second_norm(v)

            @blk.tensor
            def _(pe):
                def turn_attn(c, b, r):
                    pe.wait_ge(attn_ready, c + 1)
                    wait_count(pe, aT_copied, c)
                    for h in range(DC):
                        for t in range(CT):
                            mm = pe.transpose(ps[:, h, t * P:(t + 1) * P], attn[r][:, t, h * P:(h + 1) * P],
                                              ident[:, :])
                    mm.then_inc(aT_ready, 1)

                def project(c, b, r):
                    pe.wait_ge(aT_copied, c + 1)
                    wait_count(pe, res_ready, c)
                    for i in range(2):
                        for t in (2 * i, 2 * i + 1):
                            for h in range(DC):
                                mm = pe.matmul(ps[:, 2 + i, (t % 2) * D:(t % 2 + 1) * D],
                                               attnT[r][:, h, t * P:(t + 1) * P], wo[:, h, :],
                                               start=(h == 0), stop=(h == DC - 1))
                        mm.then_inc(wo_ready, 1)

                def turn_y(c, b, r):
                    pe.wait_ge(y_ready, c + 1)
                    wait_count(pe, yT_copied, c)
                    for h in range(DC):
                        for t in range(CT):
                            mm = pe.transpose(ps[:, 4 + h, t * P:(t + 1) * P], res[r][:, t, h * P:(h + 1) * P],
                                              ident[:, :])
                    mm.then_inc(yT_ready, 1)

                def logits(c, b, r):
                    pe.wait_ge(yT_copied, c + 1)
                    wait_count(pe, enl_ready, c)
                    for t in range(CT):
                        for h in range(DC):
                            mm = pe.matmul(ps[:, 6, t * E:(t + 1) * E], yT[r][:, h, t * P:(t + 1) * P], gate[:, h, :],
                                           start=(h == 0), stop=(h == DC - 1))
                    mm.then_inc(logit_ready, 1)

                def count_picks(g):
                    pe.wait_ge(picked, g + 1)
                    pb = pick_b[:, :, :].rearrange("p t e -> p (t e)")
                    pe.matmul(ps[:, COUNT_BANK, 0:SEC_TILES * E], before_b[:, :], pb, start=True, stop=True)
                    pe.matmul(ps[:, COUNT_BANK, SEC_TILES * E:], ones_b[:, :], pb, start=True, stop=True)\
                        .then_inc(counted, 1)

                def shared_gate_up(c, b, r):
                    pe.wait_ge(yT_saved, c + 1)
                    for w, bank, s, used in ((wsg, 4 * r, gate_ready, gact_ready),
                                             (wsu, 4 * r + 1, up_ready, hid_ready)):
                        wait_count(pe, used, c - 1)
                        for h in range(DC):
                            mm = pe.matmul(ps[:, bank, :], w[:, h, :], yT_all[:, h, bass.ds(c * CH, CH)],
                                           start=(h == 0), stop=(h == DC - 1))
                        mm.then_inc(s, 1)

                def shared_down(c, b, r):
                    pe.wait_ge(hid_ready, c + 1)
                    for i in range(2):
                        wait_count(pe, shared_done, 2 * c + i - 1)
                        for t in (2 * i, 2 * i + 1):
                            mm = pe.matmul(ps[:, 2 + i, (t % 2) * D:(t % 2 + 1) * D],
                                           gact[r][:, t * P:(t + 1) * P], wsd[:, :], start=True, stop=True)
                        mm.then_inc(down_ready, 1)

                picks = {}

                def experts(n, what):
                    _, picks[what] = nc.values_load_multi_w_load_instructions(
                        block_expert[0:1, bass.ds(2 * n, 2)], engines=[mybir.EngineType.PE], min_val=0, max_val=E - 1,
                        skip_runtime_bounds_check_because="the experts are clamped to the last one")

                def turn_rows(n, k2, r):
                    pe.wait_ge(ys_loaded[r], 16 * k2 + 16)
                    wait_count(pe, ysT_copied, n - 1)
                    for h in range(DC):
                        for k in range(2):
                            mm = pe.transpose(ps[:, r, (2 * h + k) * P:(2 * h + k + 1) * P],
                                              ys[r][:, k, h * P:(h + 1) * P], ident[:, :])
                    mm.then_inc(ysT_ready, 1)

                def gate_up(n, k2, r):
                    pe.wait_ge(ysT_copied, n + 1)
                    wait_count(pe, hx_ready, n - 1)
                    for k in range(2):
                        e = picks["gate_up"][k]
                        for h in range(DC):
                            mm = pe.matmul(ps[:, 2 + r, 2 * F * k:2 * F * (k + 1)], ysT[r][:, h, k, :],
                                           wgu[:, bass.ds(e, 1), h, :].squeeze(1), start=(h == 0), stop=(h == DC - 1))
                    mm.then_inc(gu_ready, 1)

                def turn_hidden(n, k2, r):
                    pe.wait_ge(hx_ready, n + 1)
                    wait_count(pe, hxT_copied, n - 1)
                    for k in range(2):
                        mm = pe.transpose(ps[:, 4 + r, k * P:(k + 1) * P], hx[r][:, k, :], ident[:, :])
                    mm.then_inc(hxT_ready, 1)

                def down(n, k2, r):
                    pe.wait_ge(hxT_copied, n + 1)
                    wait_count(pe, z_copied, n - 1)
                    for k in range(2):
                        e = picks["down"][k]
                        mm = pe.matmul(ps[:, 6 + r, D * k:D * (k + 1)], hxT[r][:, k, :],
                                       wdn[:, bass.ds(e, 1), :].squeeze(1), start=True, stop=True)
                    mm.then_inc(z_ready, 1)

                def chunk_turns(low, high):
                    staggered(pe, [(0, turn_attn), (3, logits), (2, turn_y), (0, project)], CHUNKS, turns=(low, high))

                def shared_turns(low, high):
                    staggered(pe, [(0, shared_gate_up), (1, shared_down)], CHUNKS, turns=(low, high))

                chunk_turns(0, CHUNKS)
                logits(CHUNKS - 3, B - 2, 1)
                turn_y(CHUNKS - 2, B - 1, 0)
                shared_gate_up(0, 0, 0)
                logits(CHUNKS - 2, B - 1, 0)
                count_picks(0)
                turn_y(CHUNKS - 1, B - 1, 1)
                pe.wait_ge(yT_copied, CHUNKS)
                shared_gate_up(1, 0, 1)
                shared_down(0, 0, 0)
                logits(CHUNKS - 1, B - 1, 1)
                shared_gate_up(2, 1, 0)
                shared_down(1, 0, 1)
                shared_gate_up(3, 1, 1)
                shared_down(2, 1, 0)
                shared_gate_up(4, 2, 0)
                pe.wait_ge(counts_used, 1)
                count_picks(1)
                shared_down(3, 1, 1)
                shared_turns(5, CHUNKS + 1)
                pe.wait_ge(counts_used, 2)
                pe.wait_ge(shared_done, 2 * CHUNKS)
                pe.wait_ge(wgu_loaded, 16)
                pe.wait_ge(blocks_ready, SECTIONS)
                staggered(pe, [(1, lambda n, k2, r: experts(n, "gate_up")), (3, lambda n, k2, r: experts(n, "down")),
                               (0, turn_rows), (1, gate_up), (2, turn_hidden), (3, down)], PAIRS)


_INS = ["x", "xT", "Wq", "bq", "Wk", "bk", "Wv", "bv", "Wo", "bo", "gate_w", "expert_bias", "sg_w", "su_w", "sd_w",
        "gu_w", "down_w"]


def kernel(**inputs):
    import numpy as _np
    import concourse.bacc as _bacc
    from concourse import mybir as _mybir
    from concourse.bass_utils import run_bass_kernel_spmd as _run

    given = {n: _np.asarray(inputs["L0_attn_" + n]) for n in ("x", "Wq", "bq", "Wk", "bk", "Wv", "bv", "Wo", "bo")}
    for name in ("bq", "bk"):
        given[name] = given[name].reshape(DC, P).T
    given["xT"] = given["x"].reshape(B * N, D).T
    for name, key in (("gate_w", "gate_w"), ("expert_bias", "expert_bias"), ("sg_w", "shared_gate_w"),
                      ("su_w", "shared_up_w"), ("sd_w", "shared_down_w"), ("gu_w", "experts_gate_up"),
                      ("down_w", "experts_down")):
        given[name] = _np.asarray(inputs["L0_ffn_" + key])
    nc = _bacc.Bacc("TRN2", target_bir_lowering=False, num_devices=1)
    arrays, args = {}, []
    for name in _INS:
        a = _np.ascontiguousarray(given[name])
        arrays[f"in_{name}"] = a
        args.append(nc.dram_tensor(f"in_{name}", a.shape, _mybir.dt.from_np(a.dtype), kind="ExternalInput").ap())
    args.append(nc.dram_tensor("out_0", (B, N, D), _mybir.dt.float32, kind="ExternalOutput").ap())
    build(nc, *args)
    r = _run(nc, [arrays], core_ids=[0])
    return r.results[0]["out_0"]
```
